# Optimizing a Trainium2 kernel written in Bass

```python
import numpy as np
import jax
import jax.numpy as jnp

def _softmax(x, axis=-1):
    return jax.nn.softmax(x, axis=axis)

def _gelu(x):
    return jax.nn.gelu(x, approximate=True)

def _silu(x):
    return jax.nn.silu(x)

def _sigmoid(x):
    return jax.nn.sigmoid(x)

def _layernorm(x, axis=-1, eps=1e-05):
    m = jnp.mean(x, axis=axis, keepdims=True)
    v = jnp.var(x, axis=axis, keepdims=True)
    return (x - m) / jnp.sqrt(v + eps)

def _scatter_add(tgt, idx, src, axis=0):
    return tgt.at[idx].add(src)

def _segment_sum(src, seg, n):
    return jax.ops.segment_sum(src, seg, n)
kernel_name = 'mk_gnn_resnorm_d2_gnn_r8_0d7f06'

def setup_inputs(seed: int=0):
    np.random.seed(seed)
    _w = jnp.asarray

    def _rec_inputs():
        import jax
        import jax.numpy as jnp
        _gk = jax.random.key(seed)
        x = -0.000202 + 1 * jax.random.normal(jax.random.fold_in(_gk, 1), (12500, 128), jnp.float32)
        _s = jax.random.randint(jax.random.fold_in(_gk, 2), (100000,), 0, 12500, jnp.int32)
        _d = jax.random.randint(jax.random.fold_in(_gk, 3), (100000,), 0, 12500, jnp.int32)
        _loop = jnp.arange(12500, dtype=jnp.int32)
        src = jnp.concatenate([_s, _d, _loop])
        dst = jnp.concatenate([_d, _s, _loop])
        _o = jnp.argsort(dst, stable=True)
        src = src[_o]
        dst = dst[_o]
        edge_attr_128 = -4.21973e-05 + 0.999841 * jax.random.normal(jax.random.fold_in(_gk, 11), (212500, 128), jnp.float32)
        return (x, src, dst, edge_attr_128)
    x, src, dst, edge_attr_128 = _rec_inputs()

    def _L0_gnn_setup():
        import jax, jax.numpy as jnp
        import numpy as np
        NUM_HEADS = 8
        BN_EPS = 1e-05
        ATTN_EPS = 1e-06
        key = jax.random.key(seed)
        N, E, D = (6250, 75000, 128)
        ks = jax.random.split(key, 7)
        s = 1.0 / np.sqrt(D).astype(np.float32)
        return {'x': jax.random.normal(ks[0], (N, D), jnp.float32), 'edge_attr': jax.random.normal(ks[1], (E, D), jnp.float32), 'WQ': jax.random.normal(ks[2], (D, D), jnp.float32) * s, 'WK': jax.random.normal(ks[3], (D, D), jnp.float32) * s, 'WV': jax.random.normal(ks[4], (D, D), jnp.float32) * s, 'WE': jax.random.normal(ks[5], (D, D), jnp.float32) * s, 'bn_gamma': jnp.ones((D,), jnp.float32), 'bn_beta': jnp.zeros((D,), jnp.float32), 'edge_index': jax.random.randint(ks[6], (2, E), 0, N, dtype=jnp.int32)}
    _L0_gnn_all = _L0_gnn_setup()
    _L0_gnn_in = {k: v for k, v in _L0_gnn_all.items() if k in ('WQ', 'WK', 'WV', 'WE', 'bn_gamma', 'bn_beta')}
    del _L0_gnn_all

    def _L1_gnn_setup():
        import jax, jax.numpy as jnp
        import numpy as np
        NEG_SLOPE = 0.2
        BN_EPS = 1e-05
        SM_EPS = 1e-16

        def _bn_relu(h, gamma, beta):
            mu = h.mean(axis=0)
            var = ((h - mu) ** 2).mean(axis=0)
            return jax.nn.relu((h - mu) * jax.lax.rsqrt(var + BN_EPS) * gamma + beta)
        N, E, C = (6250, 100000, 128)
        key = jax.random.key(seed)
        ks = jax.random.split(key, 12)
        s = 1.0 / np.sqrt(C)
        return {'x': jax.random.normal(ks[0], (N, C), jnp.float32), 'edge_index': jax.random.randint(ks[1], (2, E), 0, N, jnp.int64), 'W': jax.random.uniform(ks[2], (C, C), jnp.float32, -s, s), 'att_src': jax.random.uniform(ks[3], (C,), jnp.float32, -s, s), 'att_dst': jax.random.uniform(ks[4], (C,), jnp.float32, -s, s), 'bias_gat': jnp.zeros((C,), jnp.float32), 'W1': jax.random.uniform(ks[5], (C, C), jnp.float32, -s, s), 'b1': jax.random.uniform(ks[6], (C,), jnp.float32, -s, s), 'g1': jnp.ones((C,), jnp.float32), 'be1': jnp.zeros((C,), jnp.float32), 'W2': jax.random.uniform(ks[7], (C, C), jnp.float32, -s, s), 'b2': jax.random.uniform(ks[8], (C,), jnp.float32, -s, s), 'g2': jnp.ones((C,), jnp.float32), 'be2': jnp.zeros((C,), jnp.float32)}
    _L1_gnn_all = _L1_gnn_setup()
    _L1_gnn_in = {k: v for k, v in _L1_gnn_all.items() if k in ('W', 'att_src', 'att_dst', 'bias_gat', 'W1', 'b1', 'g1', 'be1', 'W2', 'b2', 'g2', 'be2')}
    del _L1_gnn_all
    return {'x': x, 'src': src, 'dst': dst, 'edge_attr_128': edge_attr_128, 'L0_gnn_WQ': _L0_gnn_in['WQ'], 'L0_gnn_WK': _L0_gnn_in['WK'], 'L0_gnn_WV': _L0_gnn_in['WV'], 'L0_gnn_WE': _L0_gnn_in['WE'], 'L0_gnn_bn_gamma': _L0_gnn_in['bn_gamma'], 'L0_gnn_bn_beta': _L0_gnn_in['bn_beta'], 'L1_gnn_W': _L1_gnn_in['W'], 'L1_gnn_att_src': _L1_gnn_in['att_src'], 'L1_gnn_att_dst': _L1_gnn_in['att_dst'], 'L1_gnn_bias_gat': _L1_gnn_in['bias_gat'], 'L1_gnn_W1': _L1_gnn_in['W1'], 'L1_gnn_b1': _L1_gnn_in['b1'], 'L1_gnn_g1': _L1_gnn_in['g1'], 'L1_gnn_be1': _L1_gnn_in['be1'], 'L1_gnn_W2': _L1_gnn_in['W2'], 'L1_gnn_b2': _L1_gnn_in['b2'], 'L1_gnn_g2': _L1_gnn_in['g2'], 'L1_gnn_be2': _L1_gnn_in['be2']}

def reference(x, src, dst, edge_attr_128, L0_gnn_WQ, L0_gnn_WK, L0_gnn_WV, L0_gnn_WE, L0_gnn_bn_gamma, L0_gnn_bn_beta, L1_gnn_W, L1_gnn_att_src, L1_gnn_att_dst, L1_gnn_bias_gat, L1_gnn_W1, L1_gnn_b1, L1_gnn_g1, L1_gnn_be1, L1_gnn_W2, L1_gnn_b2, L1_gnn_g2, L1_gnn_be2):
    import jax
    import jax.numpy as jnp

    def _L0_gnn_ref(x, edge_attr, WQ, WK, WV, WE, bn_gamma, bn_beta, edge_index):
        import jax, jax.numpy as jnp
        import numpy as np
        NUM_HEADS = 8
        BN_EPS = 1e-05
        ATTN_EPS = 1e-06
        N, D = x.shape
        H = NUM_HEADS
        dh = D // H
        Q = (x @ WQ).reshape(N, H, dh)
        K = (x @ WK).reshape(N, H, dh)
        V = (x @ WV).reshape(N, H, dh)
        Eh = (edge_attr @ WE).reshape(-1, H, dh)
        src, dst = (edge_index[0], edge_index[1])
        score = K[src] * Q[dst] / jnp.sqrt(jnp.float32(dh)) * Eh
        score = jnp.exp(jnp.clip(score.sum(-1, keepdims=True), -5.0, 5.0))
        msg = V[src] * score
        wV = jax.ops.segment_sum(msg, dst, num_segments=N)
        Z = jax.ops.segment_sum(score, dst, num_segments=N)
        h_attn = (wV / (Z + ATTN_EPS)).reshape(N, D)
        h = x + h_attn
        mean = h.mean(axis=0)
        var = jnp.mean((h - mean) ** 2, axis=0)
        return (h - mean) * jax.lax.rsqrt(var + BN_EPS) * bn_gamma + bn_beta

    def _L1_gnn_ref(x, edge_index, W, att_src, att_dst, bias_gat, W1, b1, g1, be1, W2, b2, g2, be2):
        import jax, jax.numpy as jnp
        import numpy as np
        NEG_SLOPE = 0.2
        BN_EPS = 1e-05
        SM_EPS = 1e-16

        def _bn_relu(h, gamma, beta):
            mu = h.mean(axis=0)
            var = ((h - mu) ** 2).mean(axis=0)
            return jax.nn.relu((h - mu) * jax.lax.rsqrt(var + BN_EPS) * gamma + beta)
        N = x.shape[0]
        loops = jnp.arange(N, dtype=edge_index.dtype)
        src = jnp.concatenate([edge_index[0], loops])
        dst = jnp.concatenate([edge_index[1], loops])
        xl = x @ W
        a_src = xl @ att_src
        a_dst = xl @ att_dst
        e = jax.nn.leaky_relu(a_src[src] + a_dst[dst], NEG_SLOPE)
        m = jax.ops.segment_max(e, dst, num_segments=N)
        e = jnp.exp(e - m[dst])
        denom = jax.ops.segment_sum(e, dst, num_segments=N)
        alpha = e / (denom[dst] + SM_EPS)
        out = jax.ops.segment_sum(alpha[:, None] * xl[src], dst, num_segments=N) + bias_gat
        h = _bn_relu(out @ W1 + b1, g1, be1)
        h = _bn_relu(h @ W2 + b2, g2, be2)
        return h + x
    edge_index = jnp.stack([src, dst])
    x = _layernorm(x + _L0_gnn_ref(x, edge_attr_128, L0_gnn_WQ, L0_gnn_WK, L0_gnn_WV, L0_gnn_WE, L0_gnn_bn_gamma, L0_gnn_bn_beta, edge_index), axis=-1)
    x = _layernorm(x + _L1_gnn_ref(x, edge_index, L1_gnn_W, L1_gnn_att_src, L1_gnn_att_dst, L1_gnn_bias_gat, L1_gnn_W1, L1_gnn_b1, L1_gnn_g1, L1_gnn_be1, L1_gnn_W2, L1_gnn_b2, L1_gnn_g2, L1_gnn_be2), axis=-1)
    return x

_drawn_inputs = setup_inputs


def setup_inputs(seed=0):
    import zlib

    import numpy as np

    out = dict(_drawn_inputs(seed))
    spreads = {'L0_gnn_bn_gamma': (1.0, 0.2),
     'L0_gnn_bn_beta': (0.0, 0.1),
     'L1_gnn_bias_gat': (0.0, 0.8),
     'L1_gnn_g1': (1.0, 0.2),
     'L1_gnn_be1': (0.0, 0.279),
     'L1_gnn_g2': (1.0, 0.2),
     'L1_gnn_be2': (0.0, 0.1)}
    factors = {'L1_gnn_b1': 8.0, 'L1_gnn_b2': 8.0}
    for name, (base, spread) in spreads.items():
        noise = np.random.default_rng([zlib.crc32(name.encode()), seed]).standard_normal(out[name].shape)
        drawn = base * np.exp(spread * noise) if base else spread * noise
        out[name] = jnp.asarray(drawn.astype(out[name].dtype))
    for name, factor in factors.items():
        out[name] = (out[name] * factor).astype(out[name].dtype)
    return out
```

```python
from contextlib import ExitStack

import concourse.bass as bass
from concourse import mybir

F32 = mybir.dt.float32
I32 = mybir.dt.int32
ALU = mybir.AluOpType
ACT = mybir.ActivationFunctionType
AX = mybir.AxisListType.X

P = 128
D = 128
H = 8
DH = D // H
N = 12500
E = 212500
G = 512
NG = -(-N // G)
NP = NG * G
T = G // P
CE = 512
K = CE // P
U = 4
NC = -(-(-(-E // CE)) // U) * U
CR = 104
CJ = NC // CR
W = 64
SG = N // NG
ROW1 = 132
LAST = E - (NC - 1) * CE
FAR = 1.0e6
MASKED = -1.0e30
NORM_EPS = 1e-5
LEAD = 1
DMA_LEAD = 16
ATTN_EPS = 1e-6
SM_EPS = 1e-16
SLOPE = 0.2
CLIP = 5.0
assert NG * SG == N and CR * CJ == NC and LAST % K == 0 and NG % 2 == 1

WQ, WK, WV, WE, W1G, WM1, WM2 = range(7)
(GAMMA0, BETA0, ASRC, ADST, BGAT, B1, G1, BE1, B2, G2, BE2) = range(11)


class Steps:

    def __init__(self, eng, sem, start=0):
        self.eng, self.sem, self.start, self.n = eng, sem, start, 0

    def ordered(self, ins):
        self.n += 1
        ins.then_inc(self.sem, 1)
        self.eng.wait_ge(self.sem, self.start + self.n)


def alone(eng, passed):
    eng.sem_inc(passed, 1)


def lead(eng, sems, by):
    for sem in sems:
        eng.sem_inc(sem, by)


def over_groups(eng, body):
    with eng.Fori(0, NG // 2) as turn:
        body(turn * 2, 0)
        body(turn * 2 + 1, 1)
    body(NG - 1, 0)


def over_chunks(eng, body, last):
    with eng.Fori(0, last // U - 1) as turn:
        for u in range(U):
            body(turn * U + u, u, False)
    for u in range(U):
        body(last - U + u, u, True)


def at(i, n):
    return bass.ds(i * n, n)


def row(ap, i):
    entry = ap[bass.ds(i, 1)]
    return entry.rearrange("a p k d -> p (a k) d") if len(ap.shape) == 4 else entry.rearrange("a p k -> p (a k)")


def before(i, slot, each, slots):
    return (i - slot) * (each // slots)


def landed(i, slot, each, slots):
    return before(i, slot, each, slots) + each


def build(nc, x, src, dst_rows, dst_cols, edges, weights, vectors, out):
    with ExitStack() as ctx:
        def sb(name, shape, dt=F32):
            return ctx.enter_context(nc.sbuf_tensor(name, shape, dt))

        def dram(name, shape, dt=F32):
            return nc.dram_tensor(name, shape, dt, kind="Internal").ap()

        m = {}
        m["q_table"] = dram("q_table", [NP, D])
        m["kv_table"] = dram("kv_table", [NP, 2 * D])
        m["xl_table"] = dram("xl_table", [NP, ROW1])
        m["ad_row"] = dram("ad_row", [NP])
        m["x1t_table"] = dram("x1t_table", [P, NP])
        m["base_table"] = dram("base_table", [NC], I32)
        m["far_table"] = dram("far_table", [NC], I32)
        m["acc"] = sb("acc", [P, 3, NP])
        m["dst_local"] = sb("dst_local", [P, NC, K])
        m["base_row"] = sb("base_row", [P, NC], I32)
        m["w"] = sb("w", [P, 7, D])
        m["vec"] = sb("vec", [P, 11])
        m["ident"] = sb("ident", [P, P])
        m["iota"] = sb("iota", [P, W])
        m["eps"] = sb("eps", [P, 1])
        prologue(nc, m, dst_rows, dst_cols, weights, vectors)
        project(nc, m, x)
        edges0(nc, m, src, edges)
        nodes0(nc, m)
        edges1(nc, m, src)
        nodes1(nc, m, out)


def prologue(nc, m, dst_rows, dst_cols, weights, vectors):
    with ExitStack() as ctx:
        sem = lambda name: ctx.enter_context(nc.semaphore(name))
        sb = lambda name, shape, dt=F32: ctx.enter_context(nc.sbuf_tensor(name, shape, dt))
        weights_in, rows_in, cols_in = sem("weights_in"), sem("rows_in"), sem("cols_in")
        base_ready, base_stored, base_back = sem("base_ready"), sem("base_stored"), sem("base_back")
        ident_zero, made, step = sem("ident_zero"), sem("made"), sem("pro_step")
        rows = m["acc"][0:CR, 0, 0:CJ * CE].rearrange("p (j e) -> p j e", e=CE)
        low = m["acc"][0:CR, 1, 0:CJ * CE].rearrange("p (j e) -> p j e", e=CE)
        rows_i = m["acc"][0:CR, 2, 0:CJ * CE].bitcast(I32).rearrange("p (j e) -> p j e", e=CE)
        cols_i = m["acc"][:, 0, CJ * CE:CJ * CE + NC * K].bitcast(I32).rearrange("p (c k) -> p c k", k=K)
        base_f = sb("base_f", [P, CJ])
        base_i = sb("base_i", [P, CJ], I32)
        far_f = sb("far_f", [P, CJ])
        far_i = sb("far_i", [P, CJ], I32)
        base_all_i = sb("base_all_i", [P, NC], I32)
        base_all = sb("base_all", [P, NC])
        block = ctx.enter_context(nc.Block())

        @block.sync
        def _(sp):
            sp.dma_start(rows_i, dst_rows.rearrange("(p j) e -> p j e", j=CJ)).then_inc(rows_in, 16)
            sp.dma_start(cols_i, dst_cols).then_inc(cols_in, 16)
            sp.wait_ge(base_ready, 1)
            sp.dma_start(m["base_table"].rearrange("(p j) -> p j", j=CJ), base_i[0:CR, :]).then_inc(base_stored, 16)
            sp.dma_start(m["far_table"].rearrange("(p j) -> p j", j=CJ), far_i[0:CR, :]).then_inc(base_stored, 16)
            sp.wait_ge(base_stored, 32)
            sp.dma_start(m["base_row"][0:1, :], m["base_table"].unsqueeze(0)).then_inc(base_back, 16)
            sp.dma_start(base_all_i[:], m["base_table"].partition_broadcast(P)).then_inc(base_back, 16)
            sp.wait_ge(base_back, 32)

        @block.scalar
        def _(act):
            act.dma_start(m["w"][:], weights).then_inc(weights_in, 16)
            act.dma_start(m["vec"][:], vectors).then_inc(weights_in, 16)
            act.wait_ge(weights_in, 32)

        @block.gpsimd
        def _(pool):
            nc.gpsimd.memset(m["ident"][:], 0.0).then_inc(ident_zero, 1)
            pool.wait_ge(ident_zero, 1)
            nc.gpsimd.affine_select(out=m["ident"][:], in_=m["ident"][:], compare_op=ALU.not_equal, fill=1.0,
                                    base=0, pattern=[[-1, P]], channel_multiplier=1).then_inc(made, 1)
            nc.gpsimd.iota(m["iota"][:], pattern=[[1, W]], base=0, channel_multiplier=0,
                           allow_small_or_imprecise_dtypes=True).then_inc(made, 1)
            nc.gpsimd.memset(m["eps"][:], NORM_EPS).then_inc(made, 1)
            pool.wait_ge(made, 3)

        @block.vector
        def _(dve):
            do = Steps(dve, step).ordered
            dve.wait_ge(rows_in, 16)
            do(nc.vector.tensor_copy(rows, rows_i))
            do(nc.vector.tensor_scalar(low, rows, 0.0, FAR, ALU.is_lt, ALU.mult))
            do(nc.vector.tensor_tensor(low, low, rows, ALU.add))
            do(nc.vector.tensor_reduce(base_f[0:CR, :], low, AX, ALU.min))
            do(nc.vector.tensor_reduce(far_f[0:CR, :], rows, AX, ALU.max))
            do(nc.vector.tensor_copy(base_i[0:CR, :], base_f[0:CR, :]))
            do(nc.vector.tensor_tensor(far_f[0:CR, :], far_f[0:CR, :], base_f[0:CR, :], ALU.subtract))
            nc.vector.tensor_copy(far_i[0:CR, :], far_f[0:CR, :]).then_inc(base_ready, 1)
            dve.wait_ge(cols_in, 16)
            do(nc.vector.tensor_copy(m["dst_local"][:], cols_i))
            dve.wait_ge(base_back, 32)
            do(nc.vector.tensor_copy(base_all[:], base_all_i[:]))
            do(nc.vector.tensor_tensor(m["dst_local"][:], m["dst_local"][:],
                                       base_all[:].unsqueeze(2).to_broadcast([P, NC, K]), ALU.subtract))


def project(nc, m, x):
    with ExitStack() as ctx:
        sem = lambda name: ctx.enter_context(nc.semaphore(name))
        sb = lambda name, shape, dt=F32: ctx.enter_context(nc.sbuf_tensor(name, shape, dt))
        ps = lambda name, shape: ctx.enter_context(nc.psum_tensor(name, shape, F32))
        x_in = [sem(f"x_in{s}") for s in range(2)]
        stored = [sem(f"qkv_stored{s}") for s in range(2)]
        turned, copied, kept = sem("x_turned"), sem("xt_copied"), sem("xt_kept")
        projected, q_out, kv_out = sem("projected"), sem("q_out"), sem("kv_out")
        xn = sb("xn", [P, 2, T, D])
        xt = sb("xt", [P, 2, G])
        q = sb("q", [P, 2, T, D])
        kv = sb("kv", [P, 2, T, 2 * D])
        ps_xt = ps("ps_xt", [P, 2, G])
        ps_qkv = ps("ps_qkv", [P, T, G])
        xg = x.rearrange("(g k p) d -> g p k d", k=T, p=P)
        qg = m["q_table"].rearrange("(g k p) d -> g p k d", k=T, p=P)
        kvg = m["kv_table"].rearrange("(g k p) d -> g p k d", k=T, p=P)
        wqkv = m["w"][:, WQ:WV + 1, :].rearrange("p a d -> p (a d)")
        block = ctx.enter_context(nc.Block())

        @block.sync
        def _(sp):
            lead(sp, [*stored], DMA_LEAD)
            for s in range(2):
                sp.dma_start(xn[:, s], xg[s]).then_inc(x_in[s], 16)

            def body(g, s, ahead):
                if ahead:
                    sp.wait_ge(turned, g + 1)
                    sp.dma_start(xn[:, s], row(xg, g + 2)).then_inc(x_in[s], 16)
                sp.wait_ge(q_out, g + 1 + LEAD)
                sp.dma_start(row(qg, g), q[:, s]).then_inc(stored[s], 16)
                sp.wait_ge(kv_out, g + 1 + LEAD)
                sp.dma_start(row(kvg, g), kv[:, s]).then_inc(stored[s], 16)

            with sp.Fori(0, (NG - 3) // 2) as turn:
                body(turn * 2, 0, True)
                body(turn * 2 + 1, 1, True)
            for g in range(NG - 3, NG):
                body(g, g % 2, g + 2 < NG)
            sp.wait_ge(stored[0], 32 * (NG // 2 + 1) + DMA_LEAD)
            sp.wait_ge(stored[1], 32 * (NG // 2) + DMA_LEAD)

        @block.tensor
        def _(pe):
            lead(pe, [projected], LEAD)
            def body(g, s):
                pe.wait_ge(x_in[s], landed(g, s, 16, 2))
                pe.wait_ge(kept, g + LEAD)
                for k in range(T):
                    mm = nc.tensor.transpose(ps_xt[:, s, at(k, P)], xn[:, s, k], m["ident"][:])
                mm.then_inc(turned, 1)
                pe.wait_ge(copied, g + 1)
                pe.wait_ge(kv_out, g + LEAD)
                pe.wait_ge(q_out, g + LEAD)
                for k in range(T):
                    mm = nc.tensor.matmul(ps_qkv[:, k, 0:3 * D], xt[:, s, at(k, P)], wqkv, start=True, stop=True)
                mm.then_inc(projected, 1)
            over_groups(pe, body)

        @block.scalar
        def _(act):
            lead(act, [q_out], LEAD)
            def body(g, s):
                act.wait_ge(turned, g + 1)
                act.wait_ge(projected, g + LEAD)
                nc.scalar.copy(xt[:, s], ps_xt[:, s]).then_inc(copied, 1)
                act.wait_ge(projected, g + 1 + LEAD)
                act.wait_ge(stored[s], before(g, s, 32, 2) + DMA_LEAD)
                nc.scalar.mul(q[:, s], ps_qkv[:, :, 0:D], DH ** -0.5).then_inc(q_out, 1)
            over_groups(act, body)

        @block.vector
        def _(dve):
            lead(dve, [kept, kv_out], LEAD)
            def body(g, s):
                dve.wait_ge(copied, g + 1)
                nc.vector.tensor_copy(m["acc"][:, 2, at(g, G)], ps_xt[:, s]).then_inc(kept, 1)
                dve.wait_ge(q_out, g + 1 + LEAD)
                dve.wait_ge(stored[s], before(g, s, 32, 2) + DMA_LEAD)
                nc.vector.tensor_copy(kv[:, s], ps_qkv[:, :, D:3 * D]).then_inc(kv_out, 1)
            over_groups(dve, body)


def edges0(nc, m, src, edges):
    with ExitStack() as ctx:
        sem = lambda name: ctx.enter_context(nc.semaphore(name))
        sb = lambda name, shape, dt=F32: ctx.enter_context(nc.sbuf_tensor(name, shape, dt))
        ps = lambda name, shape: ctx.enter_context(nc.psum_tensor(name, shape, F32))
        passed = sem("passed0")
        src_in = [sem(f"src_in{u}") for u in range(U)]
        edge_in = [sem(f"edge_in{u}") for u in range(U)]
        kv_in = [sem(f"kv_in{u}") for u in range(U)]
        hot_ready, turned, copied = sem("hot_ready"), sem("edges_turned"), sem("edges_copied")
        spread, gated, scored = sem("spread"), sem("gated"), sem("scored")
        weighed, valued, summed, added = sem("weighed"), sem("valued"), sem("summed"), sem("added")
        mult, clear = sem("mult"), sem("cleared")
        idx = sb("idx", [P, U, K], I32)
        ea = sb("ea", [P, U, K, D])
        qw = sb("qw", [W, U, D])
        kv = sb("kv_g", [P, U, K, 2 * D])
        hot = sb("hot", [P, U, K, W])
        eat = sb("eat", [P, 2, CE])
        hott = sb("hott", [W, 2, CE])
        prod = sb("prod", [P, CE])
        score = sb("score", [P, 2, K * H])
        pex = sb("pex", [P, 2, K, D])
        ps_eat = ps("ps_eat", [P, CE])
        ps_hott = ps("ps_hott", [P, CE])
        ps_eh = ps("ps_eh", [P, 2, K, D])
        ps_q = ps("ps_q", [P, 2, K, D])
        ps_sum = ps("ps_sum", [P, 2, CE])
        src_c = src.rearrange("(c p k) -> c p k", p=P, k=K)
        ea_c = edges[0:(NC - 1) * CE].rearrange("(c p k) d -> c p (k d)", p=P, k=K)
        ea_last = edges[(NC - 1) * CE:E].rearrange("(p k) d -> p (k d)", k=K)
        block = ctx.enter_context(nc.Block())
        acc = m["acc"]

        @block.sync
        def _(sp):
            def load_src(c, u):
                sp.dma_start(idx[:, u], row(src_c, c)).then_inc(src_in[u], 16)

            def load_edges(c, u, last=False):
                if last:
                    sp.dma_start(ea[0:LAST // K, u].rearrange("p k d -> p (k d)"), ea_last).then_inc(edge_in[u], 16)
                else:
                    sp.dma_start(ea[:, u].rearrange("p k d -> p (k d)"),
                                 row(ea_c, c)).then_inc(edge_in[u], 16)

            def load_window(c, u):
                base = sp.value_load(m["base_row"][0:1, bass.ds(c, 1)], min_val=0, max_val=N - 1)
                sp.dma_start(qw[:, u], m["q_table"][bass.ds(base, W), :]).then_inc(edge_in[u], 16)

            for u in range(U):
                load_src(u, u)
            for u in range(U):
                load_edges(u, u)
                load_window(u, u)

            def body(c, u, peeled):
                sp.wait_ge(turned, c + 1)
                load_edges(c + U, u, peeled and c + U == NC - 1)
                sp.wait_ge(spread, c + 1 + LEAD)
                load_window(c + U, u)
                sp.wait_ge(kv_in[u], landed(c, u, 16 * K, U))
                load_src(c + U, u)
            over_chunks(sp, body, NC - U)

        @block.gpsimd
        def _(pool):
            def gather(c, u):
                pool.wait_ge(src_in[u], landed(c, u, 16, U))
                alone(pool, passed)
                for k in range(K):
                    nc.gpsimd.indirect_dma_start(
                        out=kv[:, u, k], out_offset=None, in_=m["kv_table"],
                        in_offset=bass.IndirectOffsetOnAxis(ap=idx[:, u, k:k + 1], axis=0)).then_inc(kv_in[u], 16)
            for u in range(U):
                gather(u, u)

            def body(c, u, peeled):
                pool.wait_ge(summed, c + 1 + LEAD)
                gather(c + U, u)
            over_chunks(pool, body, NC - U)

        @block.tensor
        def _(pe):
            lead(pe, [spread, summed], LEAD)
            def turn(c, u):
                pe.wait_ge(edge_in[u], landed(c, u, 32, U))
                pe.wait_ge(hot_ready, c + 1)
                pe.wait_ge(copied, c + LEAD)
                for k in range(K):
                    nc.tensor.transpose(ps_eat[:, at(k, P)], ea[:, u, k], m["ident"][:])
                for k in range(K):
                    mm = nc.tensor.transpose(ps_hott[0:W, at(k, P)], hot[:, u, k], m["ident"][:])
                mm.then_inc(turned, 1)

            def spread_out(c, u, first=False):
                b = u % 2
                pe.wait_ge(copied, c + 1 + LEAD)
                if not first:
                    pe.wait_ge(gated, c - 1 + LEAD)
                for k in range(K):
                    nc.tensor.matmul(ps_q[:, b, k], hott[:, b, at(k, P)], qw[:, u], start=True, stop=True)
                for k in range(K):
                    mm = nc.tensor.matmul(ps_eh[:, b, k], eat[:, b, at(k, P)], m["w"][:, WE], start=True, stop=True)
                mm.then_inc(spread, 1)

            def sum_up(c, u):
                b = u % 2
                pe.wait_ge(valued, c + 1)
                for k in range(K):
                    nc.tensor.matmul(ps_sum[:, b, 0:W], kv[:, u, k, D:2 * D], hot[:, u, k], start=(k == 0), stop=(k == K - 1))
                for k in range(K):
                    mm = nc.tensor.matmul(ps_sum[:, b, W:2 * W], pex[:, b, k], hot[:, u, k],
                                          start=(k == 0), stop=(k == K - 1))
                mm.then_inc(summed, 1)

            turn(0, 0)
            turn(1, 1)
            spread_out(0, 0, True)

            def body(c, u, peeled):
                if not (peeled and c + 2 >= NC):
                    turn(c + 2, (u + 2) % U)
                if not (peeled and c + 1 >= NC):
                    spread_out(c + 1, (u + 1) % U)
                sum_up(c, u)
            over_chunks(pe, body, NC)

        @block.scalar
        def _(act):
            lead(act, [copied], LEAD)
            def copy_out(c, u, first=False):
                b = u % 2
                act.wait_ge(turned, c + 1)
                if not first:
                    act.wait_ge(spread, c - 1 + LEAD)
                nc.scalar.copy(eat[:, b], ps_eat[:])
                nc.scalar.copy(hott[:, b], ps_hott[0:W, :]).then_inc(copied, 1)

            def weigh(c, u, first=False):
                b = u % 2
                act.wait_ge(scored, c + 1)
                if not first:
                    act.wait_ge(summed, c - 1 + LEAD)
                nc.scalar.activation(pex[:, b].rearrange("p k (h d) -> p (k h) d", d=DH),
                                     score[:, b].unsqueeze(2).to_broadcast([P, K * H, DH]), ACT.Exp).then_inc(weighed, 1)
            copy_out(0, 0, True)
            copy_out(1, 1, True)
            weigh(0, 0, True)

            def body(c, u, peeled):
                if not (peeled and c + 2 >= NC):
                    copy_out(c + 2, (u + 2) % U)
                if not (peeled and c + 1 >= NC):
                    weigh(c + 1, (u + 1) % U)
            over_chunks(act, body, NC)

        @block.vector
        def _(dve):
            lead(dve, [gated, added], LEAD)
            def one_hot(c, u):
                nc.vector.tensor_tensor(hot[:, u],
                                        m["dst_local"][:, bass.ds(c, 1), :].rearrange("p a k -> p (a k)")
                                        .unsqueeze(2).to_broadcast([P, K, W]),
                                        m["iota"][:].unsqueeze(1).to_broadcast([P, K, W]),
                                        ALU.is_equal).then_inc(hot_ready, 1)

            def attend(c, u):
                b = u % 2
                flat = lambda v: v.rearrange("p k d -> p (k d)")
                dve.wait_ge(spread, c + 1 + LEAD)
                dve.wait_ge(kv_in[u], landed(c, u, 16 * K, U))
                nc.vector.tensor_tensor(prod[:].rearrange("p (k d) -> p k d", d=D), ps_q[:, b],
                                        kv[:, u, :, 0:D], ALU.mult).then_inc(mult, 1)
                dve.wait_ge(mult, c * 2 + 1)
                nc.vector.tensor_tensor(prod[:], prod[:], flat(ps_eh[:, b]), ALU.mult).then_inc(gated, 1)
                dve.wait_ge(gated, c + 1 + LEAD)
                nc.vector.tensor_reduce(score[:, b], prod[:].rearrange("p (h d) -> p h d", d=DH), AX,
                                        ALU.add).then_inc(mult, 1)
                dve.wait_ge(mult, c * 2 + 2)
                nc.vector.tensor_scalar(score[:, b], score[:, b], CLIP, -CLIP, ALU.min, ALU.max).then_inc(scored, 1)

            def value(c, u):
                b = u % 2
                dve.wait_ge(weighed, c + 1)
                values = kv[:, u, :, D:2 * D]
                nc.vector.tensor_tensor(values, values, pex[:, b], ALU.mult).then_inc(valued, 1)

            def add_up(c, u):
                b = u % 2
                base = dve.value_load(m["base_row"][0:1, bass.ds(c, 1)], min_val=0, max_val=N - 1)
                window = acc[:, 0:2, bass.ds(base, W)]
                dve.wait_ge(summed, c + 1 + LEAD)
                dve.wait_ge(added, c + LEAD)
                nc.vector.tensor_tensor(window, window, ps_sum[:, b, 0:2 * W].rearrange("p (a w) -> p a w", w=W),
                                        ALU.add).then_inc(added, 1)

            nc.vector.memset(acc[:, 0], 0.0).then_inc(clear, 1)
            nc.vector.memset(acc[:, 1], 0.0).then_inc(clear, 1)
            dve.wait_ge(clear, 2)
            one_hot(0, 0)
            one_hot(1, 1)
            attend(0, 0)
            value(0, 0)

            def body(c, u, peeled):
                if not (peeled and c + 2 >= NC):
                    one_hot(c + 2, (u + 2) % U)
                if not (peeled and c + 1 >= NC):
                    attend(c + 1, (u + 1) % U)
                add_up(c, u)
                if not (peeled and c + 1 >= NC):
                    value(c + 1, (u + 1) % U)
            over_chunks(dve, body, NC)


def batch_norm_scale(nc, do, mv, dev, scale, shift, gamma, beta):
    do(nc.vector.reciprocal(scale, dev))
    do(nc.vector.tensor_tensor(scale, scale, gamma, ALU.mult))
    do(nc.vector.tensor_tensor(shift, mv[:, 0:1], scale, ALU.mult))
    return nc.vector.tensor_tensor(shift, beta, shift, ALU.subtract)


def layer_norm_moments(nc, do, hold, y, stats, mv):
    for k in range(T):
        last = nc.vector.bn_stats(stats[:, k], y[:, k])
    do(last)
    hold()
    for k in range(T):
        last = nc.vector.bn_aggr(mv[:, k], stats[:, k])
    return last


def layer_norm_scale(nc, do, mv, dev, scale, shift):
    do(nc.vector.reciprocal(scale, dev))
    return nc.vector.scalar_tensor_tensor(shift, mv[:, :, 0], -1.0, scale, ALU.mult, ALU.mult)


def nodes0(nc, m):
    with ExitStack() as ctx:
        sem = lambda name: ctx.enter_context(nc.semaphore(name))
        sb = lambda name, shape, dt=F32: ctx.enter_context(nc.sbuf_tensor(name, shape, dt))
        ps = lambda name, shape: ctx.enter_context(nc.psum_tensor(name, shape, F32))
        passed = sem("passed_n0")
        wt_turned, wt_copied, wa_made, wa_ready = sem("wt_turned"), sem("wt_copied"), sem("wa_made"), sem("wa_ready")
        h_step, scale_ready, ones_set = sem("h_step"), sem("scale_ready"), sem("ones_set")
        bn_var, bn_dev, ln_var, ln_dev = sem("bn_var"), sem("bn_dev"), sem("ln_var"), sem("ln_dev")
        hn_ready, y_ready, y_turned = sem("hn_ready"), sem("y_ready"), sem("y_turned")
        ln_step, ln_ready, x1_ready = sem("ln_step"), sem("ln_ready"), sem("x1_ready")
        x1_turned, x1t_ready, multiplied = sem("x1_turned"), sem("x1t_ready"), sem("multiplied")
        row_ready, logit_read = sem("row_ready"), sem("logit_read")
        taken, kept = sem("taken"), sem("max_kept")
        x1t_out = [sem(f"x1t_out{s}") for s in range(2)]
        row_out = [sem(f"row_out{s}") for s in range(2)]
        acc, vec, w = m["acc"], m["vec"], m["w"]
        stats = sb("bn_slices", [P, NG, 6])
        mv, scale, shift = sb("bn_mv", [P, 2]), sb("bn_scale", [P, 1]), sb("bn_shift", [P, 1])
        dev = sb("bn_dev", [P, 1])
        w1gt = sb("w1gt", [P, D])
        wa = sb("wa", [P, 2])
        waug = sb("waug", [P, ROW1])
        wa_both = sb("wa_both", [P, P])
        hn = sb("hn", [P, 2, G])
        y = sb("y", [P, 2, G])
        lst, lmv = sb("lst", [P, T, 6]), sb("lmv", [P, T, 2])
        lsc, lsh, ldev = sb("lsc", [P, 2, T]), sb("lsh", [P, 2, T]), sb("ldev", [P, T])
        x1 = sb("x1", [P, T, D])
        x1t = sb("x1t", [P, 2, G])
        xl = sb("xl", [P, 2, T, ROW1])
        ad = sb("ad", [1, 2, G])
        logit = sb("logit", [P, G])
        ps_y = ps("ps_y", [P, T, D])
        ps_x1t = ps("ps_x1t", [P, G])
        ps_xl = ps("ps_xl", [P, T, 2 * D])
        ps_xlt = ps("ps_xlt", [P, G])
        ps_logit = ps("ps_logit", [P, G])
        ps_ad = ps("ps_ad", [P, G])
        table = m["xl_table"].rearrange("(g k p) d -> g p k d", k=T, p=P)
        block = ctx.enter_context(nc.Block())

        @block.sync
        def _(sp):
            lead(sp, [*x1t_out, *row_out], DMA_LEAD)
            def body(g, s):
                sp.wait_ge(x1t_ready, g + 1)
                sp.dma_start(m["x1t_table"][:, at(g, G)], x1t[:, s]).then_inc(x1t_out[s], 16)
                sp.wait_ge(row_ready, g + 1 + LEAD)
                sp.dma_start(row(table, g), xl[:, s]).then_inc(row_out[s], 16)
                sp.dma_start(m["ad_row"][at(g, G)].unsqueeze(0), ad[:, s]).then_inc(row_out[s], 16)
            over_groups(sp, body)
            for s in range(2):
                sp.wait_ge(x1t_out[s], 16 * ((NG + 1 - s) // 2) + DMA_LEAD)
                sp.wait_ge(row_out[s], 32 * ((NG + 1 - s) // 2) + DMA_LEAD)

        @block.gpsimd
        def _(pool):
            pool.wait_ge(scale_ready, 1)
            nc.gpsimd.memset(acc[:, 1], 1.0).then_inc(ones_set, 1)
            pool.wait_ge(ones_set, 1)

        @block.tensor
        def _(pe):
            lead(pe, [x1_turned], LEAD)
            nc.tensor.transpose(ps_x1t[:, 0:D], w[:, W1G], m["ident"][:]).then_inc(wt_turned, 1)
            pe.wait_ge(wt_copied, 1)
            nc.tensor.matmul(ps_ad[:, 0:2], w1gt[:], vec[:, ASRC:ADST + 1], start=True, stop=True).then_inc(wa_made, 1)
            pe.wait_ge(wa_ready, 1)

            def turn_y(g, s):
                pe.wait_ge(y_ready, g + 1 + LEAD)
                for k in range(T):
                    mm = nc.tensor.transpose(ps_y[:, k], y[:, s, at(k, P)], m["ident"][:])
                mm.then_inc(y_turned, 1)

            def turn_x1(g):
                pe.wait_ge(x1_ready, g + 1)
                for k in range(T):
                    mm = nc.tensor.transpose(ps_x1t[:, at(k, P)], x1[:, k], m["ident"][:])
                mm.then_inc(x1_turned, 1)

            def multiply(g, s):
                pe.wait_ge(x1t_ready, g + 1)
                pe.wait_ge(row_ready, g + LEAD)
                pe.wait_ge(taken, 2 * g + LEAD)
                nc.tensor.matmul(ps_xlt[:], w[:, W1G], x1t[:, s], start=True, stop=True)
                nc.tensor.matmul(ps_logit[:], wa_both[:], x1t[:, s], start=True, stop=True)
                nc.tensor.matmul(ps_ad[0:1, :], wa[:, 1:2], x1t[:, s], start=True, stop=True)
                for k in range(T):
                    mm = nc.tensor.matmul(ps_xl[:, k, 0:ROW1], x1t[:, s, at(k, P)], waug[:], start=True, stop=True)
                mm.then_inc(multiplied, 1)

            turn_y(0, 0)

            def body(g, s, last=False):
                turn_x1(g)
                if not last:
                    turn_y(g + 1, 1 - s)
                multiply(g, s)
            with pe.Fori(0, NG // 2) as turn:
                body(turn * 2, 0)
                body(turn * 2 + 1, 1)
            body(NG - 1, 0, True)

        @block.scalar
        def _(act):
            lead(act, [row_ready], LEAD)
            act.wait_ge(wt_turned, 1)
            nc.scalar.copy(w1gt[:], ps_x1t[:, 0:D]).then_inc(wt_copied, 1)
            act.wait_ge(bn_var, 1)
            nc.scalar.activation(dev[:], mv[:, 1:2], ACT.Sqrt, bias=m["eps"][:]).then_inc(bn_dev, 1)
            act.wait_ge(scale_ready, 1)

            def deviation(g):
                act.wait_ge(ln_var, g + 1)
                nc.scalar.activation(ldev[:], lmv[:, :, 1], ACT.Sqrt, bias=m["eps"][:]).then_inc(ln_dev, 1)

            def batch_norm(g, s):
                act.wait_ge(y_ready, g - 1 + LEAD)
                nc.scalar.activation(hn[:, s], acc[:, 0, at(g, G)], ACT.Identity, bias=shift[:], scale=scale[:]).then_inc(hn_ready, 1)

            def layer_norm(g, s):
                act.wait_ge(ln_ready, g + 1)
                act.wait_ge(x1_turned, g + LEAD)
                for k in range(T):
                    last = nc.scalar.activation(x1[:, k], ps_y[:, k], ACT.Identity, bias=lsh[:, s, k:k + 1],
                                                scale=lsc[:, s, k:k + 1])
                last.then_inc(x1_ready, 1)

            def keep_x1t(g, s):
                act.wait_ge(x1_turned, g + 1 + LEAD)
                act.wait_ge(x1t_out[s], before(g, s, 16, 2) + DMA_LEAD)
                nc.scalar.copy(x1t[:, s], ps_x1t[:]).then_inc(x1t_ready, 1)

            def rows_out(g, s):
                act.wait_ge(multiplied, g + 1)
                act.wait_ge(row_out[s], before(g, s, 32, 2) + DMA_LEAD)
                nc.scalar.copy(xl[:, s], ps_xl[:, :, 0:ROW1])
                nc.scalar.copy(ad[:, s], ps_ad[0:1, :]).then_inc(row_ready, 1)

            nc.scalar.activation(hn[:, 0], acc[:, 0, 0:G], ACT.Identity, bias=shift[:], scale=scale[:]).then_inc(hn_ready, 1)
            batch_norm(1, 1)
            deviation(0)
            layer_norm(0, 0)

            def body(g, s, last=False, last_but_one=False):
                keep_x1t(g, s)
                if not (last or last_but_one):
                    batch_norm(g + 2, s)
                if not last:
                    deviation(g + 1)
                rows_out(g, s)
                if not last:
                    layer_norm(g + 1, 1 - s)
            with act.Fori(0, (NG - 3) // 2) as turn:
                body(turn * 2, 0)
                body(turn * 2 + 1, 1)
            body(NG - 3, 0)
            body(NG - 2, 1, last_but_one=True)
            body(NG - 1, 0, last=True)

        @block.vector
        def _(dve):
            lead(dve, [taken, y_ready, kept], LEAD)
            with dve.Fori(0, NG, 1) as g:
                do = Steps(dve, h_step, g * 5).ordered
                part = acc[:, 0, at(g, G)]
                weight = y[:, 0]
                do(nc.vector.tensor_scalar(weight, acc[:, 1, at(g, G)], ATTN_EPS, None, ALU.add))
                do(nc.vector.reciprocal(weight, weight))
                do(nc.vector.tensor_tensor(part, part, weight, ALU.mult))
                do(nc.vector.tensor_tensor(part, part, acc[:, 2, at(g, G)], ALU.add))
                do(nc.vector.bn_stats(stats[:, bass.ds(g, 1)].rearrange("p a s -> p (a s)"), acc[:, 0, at(g, SG)]))
            do = Steps(dve, h_step, NG * 5).ordered
            nc.vector.bn_aggr(mv[:], stats[:].rearrange("p g s -> p (g s)")).then_inc(bn_var, 1)
            dve.wait_ge(bn_dev, 1)
            batch_norm_scale(nc, do, mv[:], dev[:], scale[:], shift[:],
                             vec[:, GAMMA0:GAMMA0 + 1], vec[:, BETA0:BETA0 + 1]).then_inc(scale_ready, 1)
            dve.wait_ge(wa_made, 1)
            do(nc.vector.tensor_copy(wa[:], ps_ad[:, 0:2]))
            do(nc.vector.memset(waug[:], 0.0))
            do(nc.vector.tensor_copy(waug[:, 0:D], w[:, W1G]))
            do(nc.vector.tensor_copy(waug[:, D:D + 1], wa[:, 0:1]))
            do(nc.vector.tensor_tensor(wa_both[:], wa[:, 0:1].to_broadcast([P, P]), wa[:, 1:2].to_broadcast([P, P]), ALU.add))
            nc.vector.tensor_copy(logit[:, 0:1], wa[:, 0:1]).then_inc(wa_ready, 1)

            def add_x(g, s):
                dve.wait_ge(hn_ready, g + 1)
                nc.vector.tensor_tensor(y[:, s], hn[:, s], acc[:, 2, at(g, G)], ALU.add).then_inc(y_ready, 1)

            def moments(g):
                dve.wait_ge(y_turned, g + 1)
                layer_norm_moments(nc, Steps(dve, ln_step, g * 2).ordered, lambda: alone(dve, passed), ps_y, lst, lmv).then_inc(ln_var, 1)

            def statistics(g, s):
                dve.wait_ge(ln_dev, g + 1)
                layer_norm_scale(nc, Steps(dve, ln_step, g * 2 + 1).ordered, lmv, ldev[:], lsc[:, s],
                                 lsh[:, s]).then_inc(ln_ready, 1)

            def take(g):
                dve.wait_ge(multiplied, g + 1)
                dve.wait_ge(hn_ready, g + 1)
                dve.wait_ge(kept, g + LEAD)
                nc.vector.tensor_copy(acc[:, 0, at(g, G)], ps_xlt[:]).then_inc(taken, 1)
                nc.vector.tensor_copy(logit[:], ps_logit[:]).then_inc(taken, 1)
                dve.wait_ge(taken, 2 * g + 2 + LEAD)
                nc.vector.scalar_tensor_tensor(acc[:, 2, at(g, G)], logit[:], SLOPE, logit[:], ALU.mult, ALU.max).then_inc(kept, 1)

            add_x(0, 0)
            add_x(1, 1)
            moments(0)
            statistics(0, 0)

            def body(g, s, last=False, last_but_one=False):
                if not (last or last_but_one):
                    add_x(g + 2, s)
                if not last:
                    moments(g + 1)
                take(g)
                if not last:
                    statistics(g + 1, 1 - s)
            with dve.Fori(0, (NG - 3) // 2) as turn:
                body(turn * 2, 0)
                body(turn * 2 + 1, 1)
            body(NG - 3, 0)
            body(NG - 2, 1, last_but_one=True)
            body(NG - 1, 0, last=True)
            dve.wait_ge(kept, NG + LEAD)


def edges1(nc, m, src):
    with ExitStack() as ctx:
        sem = lambda name: ctx.enter_context(nc.semaphore(name))
        sb = lambda name, shape, dt=F32: ctx.enter_context(nc.sbuf_tensor(name, shape, dt))
        ps = lambda name, shape: ctx.enter_context(nc.psum_tensor(name, shape, F32))
        passed, passed_pe = sem("passed1"), sem("passed1_pe")
        src_in = [sem(f"src1_in{u}") for u in range(U)]
        ad_in = [sem(f"ad_in{u}") for u in range(U)]
        xl_in = [sem(f"xl_in{u}") for u in range(U)]
        logit_step, largest, turned, column = sem("logit_step"), sem("largest"), sem("max_turned"), sem("max_column")
        spread, max_step, shifted = sem("max_spread"), sem("max_step"), sem("shifted")
        weighed, summed, rescaled, added, set_up = sem("weighed1"), sem("summed1"), sem("rescaled"), sem("added1"), sem("set_up")
        idx = sb("idx1", [P, U, K], I32)
        adw = sb("adw", [P, U, W])
        xg = sb("xg", [P, U, K, ROW1])
        ones = sb("ones", [P, P])
        lg = sb("lg", [P, 2, K, W])
        off = sb("off", [P, K, W])
        top = sb("top", [P, 2, W])
        col = sb("col", [W, 2])
        newm = sb("newm", [P, 2, W])
        drop = sb("drop", [P, 2, W])
        fade = sb("fade", [P, 2, W])
        pw = sb("pw", [P, 2, K, W])
        ps_top = ps("ps_top", [P, 2, G])
        ps_max = ps("ps_max", [P, 2, G])
        ps_sum = ps("ps_sum1", [P, 2, CE])
        src_c = src.rearrange("(c p k) -> c p k", p=P, k=K)
        block = ctx.enter_context(nc.Block())
        acc = m["acc"]

        @block.sync
        def _(sp):
            def load_src(c, u):
                sp.dma_start(idx[:, u], row(src_c, c)).then_inc(src_in[u], 16)

            def load_window(c, u):
                base = sp.value_load(m["base_row"][0:1, bass.ds(c, 1)], min_val=0, max_val=N - 1)
                sp.dma_start(adw[:, u], m["ad_row"][bass.ds(base, W)].partition_broadcast(P)).then_inc(ad_in[u], 16)

            for u in range(U):
                load_src(u, u)
            for u in range(U):
                load_window(u, u)

            def body(c, u, peeled):
                sp.wait_ge(largest, c + 1)
                load_window(c + U, u)
                sp.wait_ge(xl_in[u], landed(c, u, 16 * K, U))
                load_src(c + U, u)
            over_chunks(sp, body, NC - U)

        @block.gpsimd
        def _(pool):
            def gather(c, u):
                pool.wait_ge(src_in[u], landed(c, u, 16, U))
                alone(pool, passed)
                for k in range(K):
                    nc.gpsimd.indirect_dma_start(
                        out=xg[:, u, k], out_offset=None, in_=m["xl_table"],
                        in_offset=bass.IndirectOffsetOnAxis(ap=idx[:, u, k:k + 1], axis=0)).then_inc(xl_in[u], 16)
            for u in range(U):
                gather(u, u)

            def body(c, u, peeled):
                pool.wait_ge(summed, c + 1 + LEAD)
                gather(c + U, u)
            over_chunks(pool, body, NC - U)

        @block.tensor
        def _(pe):
            lead(pe, [summed], LEAD)
            def turn_top(c, u):
                pe.wait_ge(largest, c + 1)
                alone(pe, passed_pe)
                nc.tensor.transpose(ps_top[0:W, u % 2, 0:P], top[:, u % 2], m["ident"][:]).then_inc(turned, 1)

            def spread_max(c, u):
                pe.wait_ge(column, c + 1)
                nc.tensor.matmul(ps_max[:, u % 2, 0:W], col[:, u % 2:u % 2 + 1].to_broadcast([W, P]),
                                 m["ident"][0:W, 0:W], start=True, stop=True).then_inc(spread, 1)

            def sum_up(c, u):
                b = u % 2
                pe.wait_ge(weighed, c + 1 + LEAD)
                for k in range(K):
                    nc.tensor.matmul(ps_sum[:, b, 0:W], xg[:, u, k, 0:D], pw[:, b, k], start=(k == 0), stop=(k == K - 1))
                for k in range(K):
                    mm = nc.tensor.matmul(ps_sum[:, b, W:2 * W], ones[:], pw[:, b, k], start=(k == 0), stop=(k == K - 1))
                mm.then_inc(summed, 1)

            turn_top(0, 0)
            spread_max(0, 0)
            turn_top(1, 1)

            def body(c, u, peeled):
                if not (peeled and c + 1 >= NC):
                    spread_max(c + 1, (u + 1) % U)
                sum_up(c, u)
                if not (peeled and c + 2 >= NC):
                    turn_top(c + 2, (u + 2) % U)
            over_chunks(pe, body, NC)

        @block.scalar
        def _(act):
            lead(act, [weighed], LEAD)
            def weigh(c, u, first=False):
                b = u % 2
                act.wait_ge(shifted, c + 1)
                if not first:
                    act.wait_ge(summed, c - 1 + LEAD)
                nc.scalar.activation(fade[:, b], drop[:, b], ACT.Exp)
                nc.scalar.activation(pw[:, b], lg[:, b], ACT.Exp).then_inc(weighed, 1)
            weigh(0, 0, True)

            def body(c, u, peeled):
                if not (peeled and c + 1 >= NC):
                    weigh(c + 1, (u + 1) % U)
            over_chunks(act, body, NC)

        @block.vector
        def _(dve):
            nc.vector.memset(ones[:], 1.0).then_inc(set_up, 1)
            dve.wait_ge(set_up, 1)

            def logits(c, u, first=False):
                b = u % 2
                do = Steps(dve, logit_step, c * 4).ordered
                t = lg[:, b]
                dve.wait_ge(ad_in[u], landed(c, u, 16, U))
                dve.wait_ge(xl_in[u], landed(c, u, 16 * K, U))
                if not first:
                    dve.wait_ge(weighed, c - 1 + LEAD)
                do(nc.vector.tensor_tensor(t, xg[:, u, :, D:D + 1].to_broadcast([P, K, W]),
                                           adw[:, u].unsqueeze(1).to_broadcast([P, K, W]), ALU.add))
                do(nc.vector.scalar_tensor_tensor(t, t, SLOPE, t, ALU.mult, ALU.max))
                do(nc.vector.tensor_tensor(off[:], m["dst_local"][:, bass.ds(c, 1), :].rearrange("p a k -> p (a k)")
                                           .unsqueeze(2).to_broadcast([P, K, W]),
                                           m["iota"][:].unsqueeze(1).to_broadcast([P, K, W]), ALU.not_equal))
                do(nc.vector.scalar_tensor_tensor(t, off[:], MASKED, t, ALU.mult, ALU.add))
                nc.vector.tensor_reduce(top[:, b], t.rearrange("p k w -> p w k"), AX, ALU.max).then_inc(largest, 1)

            def max_column(c, u):
                b = u % 2
                dve.wait_ge(turned, c + 1)
                nc.vector.tensor_reduce(col[:, b:b + 1], ps_top[0:W, b, 0:P], AX, ALU.max).then_inc(column, 1)

            def shift(c, u):
                b = u % 2
                base = dve.value_load(m["base_row"][0:1, bass.ds(c, 1)], min_val=0, max_val=N - 1)
                running = acc[:, 2, bass.ds(base, W)]
                do = Steps(dve, max_step, c * 3).ordered
                dve.wait_ge(spread, c + 1)
                do(nc.vector.tensor_tensor(newm[:, b], running, ps_max[:, b, 0:W], ALU.max))
                do(nc.vector.tensor_tensor(drop[:, b], running, newm[:, b], ALU.subtract))
                do(nc.vector.tensor_tensor(running, running, newm[:, b], ALU.max))
                nc.vector.tensor_tensor(lg[:, b], lg[:, b], newm[:, b].unsqueeze(1).to_broadcast([P, K, W]),
                                        ALU.subtract).then_inc(shifted, 1)

            def add_up(c, u):
                b = u % 2
                base = dve.value_load(m["base_row"][0:1, bass.ds(c, 1)], min_val=0, max_val=N - 1)
                window = acc[:, 0:2, bass.ds(base, W)]
                dve.wait_ge(weighed, c + 1 + LEAD)
                nc.vector.tensor_tensor(window, window, fade[:, b].unsqueeze(1).to_broadcast([P, 2, W]),
                                        ALU.mult).then_inc(rescaled, 1)
                dve.wait_ge(rescaled, c + 1)
                dve.wait_ge(summed, c + 1 + LEAD)
                nc.vector.tensor_tensor(window, window, ps_sum[:, b, 0:2 * W].rearrange("p (a w) -> p a w", w=W),
                                        ALU.add).then_inc(added, 1)
                dve.wait_ge(added, c + 1)

            logits(0, 0, True)
            max_column(0, 0)
            shift(0, 0)
            logits(1, 1, True)

            def body(c, u, peeled):
                if not (peeled and c + 1 >= NC):
                    max_column(c + 1, (u + 1) % U)
                if not (peeled and c + 2 >= NC):
                    logits(c + 2, (u + 2) % U)
                if not (peeled and c + 1 >= NC):
                    shift(c + 1, (u + 1) % U)
                add_up(c, u)
            over_chunks(dve, body, NC)


def nodes1(nc, m, out):
    with ExitStack() as ctx:
        sem = lambda name: ctx.enter_context(nc.semaphore(name))
        sb = lambda name, shape, dt=F32: ctx.enter_context(nc.sbuf_tensor(name, shape, dt))
        ps = lambda name, shape: ctx.enter_context(nc.psum_tensor(name, shape, F32))
        acc, vec, w = m["acc"], m["vec"], m["w"]
        passed = sem("passed_n1")
        div_step, o_ready = sem("div_step"), sem("o_ready")
        lin = [sem("lin0"), sem("lin1")]
        lin_out = [sem("lin_out0"), sem("lin_out1")]
        relu_ready = sem("relu_ready")
        stat = [sem("stat0"), sem("stat1")]
        scaled = [sem("scaled0"), sem("scaled1")]
        bn_step = sem("bn_step")
        bn_var, bn_dev, ln_var, ln_dev = sem("bn_var1"), sem("bn_dev1"), sem("ln_var1"), sem("ln_dev1")
        x1_in = [sem(f"x1_in{s}") for s in range(2)]
        out_stored = [sem(f"out_stored{s}") for s in range(2)]
        h_ready, y_ready, y_turned = sem("h_ready1"), sem("y_ready1"), sem("y_turned1")
        ln_step, ln_ready, normed = sem("ln_step1"), sem("ln_ready1"), sem("normed1")
        o = sb("o", [P, 2, SG])
        r = sb("r", [P, 2, G])
        x1t = sb("x1t_b", [P, 2, G])
        y = sb("y_b", [P, 2, G])
        xo = sb("xo", [P, 2, T, D])
        stats = sb("bn_slices1", [P, NG, 6])
        mv = sb("mv1", [P, 2, 2])
        scale, shift, dev = sb("scale1", [P, 2]), sb("shift1", [P, 2]), sb("dev1", [P, 2])
        lst, lmv = sb("lst1", [P, T, 6]), sb("lmv1", [P, T, 2])
        lsc, lsh, ldev = sb("lsc1", [P, 2, T]), sb("lsh1", [P, 2, T]), sb("ldev1", [P, T])
        ps_lin = ps("ps_lin", [P, 2, 512])
        ps_y = ps("ps_y1", [P, 2, T, D])
        out_g = out.rearrange("(g k p) d -> g p k d", k=T, p=P)
        block = ctx.enter_context(nc.Block())

        @block.sync
        def _(sp):
            lead(sp, [*out_stored], DMA_LEAD)
            def load(g, s):
                sp.dma_start(x1t[:, s], m["x1t_table"][:, at(g, G)]).then_inc(x1_in[s], 16)
            load(0, 0)
            load(1, 1)

            def body(g, s, ahead=True):
                if ahead:
                    sp.wait_ge(y_ready, g + 1 + LEAD)
                    load(g + 2, s)
                sp.wait_ge(normed, g + 1 + LEAD)
                sp.dma_start(row(out_g, g), xo[:, s]).then_inc(out_stored[s], 16)
            with sp.Fori(0, (NG - 3) // 2) as turn:
                body(turn * 2, 0)
                body(turn * 2 + 1, 1)
            for g in range(NG - 3, NG):
                body(g, g % 2, g + 2 < NG)
            for s in range(2):
                sp.wait_ge(out_stored[s], 16 * ((NG + 1 - s) // 2) + DMA_LEAD)

        @block.tensor
        def _(pe):
            lead(pe, [*lin, y_turned], LEAD)
            def linear(layer):
                def body(g, s):
                    pe.wait_ge(o_ready if layer == 0 else relu_ready, g + 1)
                    pe.wait_ge(lin_out[layer], g + LEAD)
                    nc.tensor.matmul(ps_lin[:, s, 0:SG], w[:, WM1 + layer], (o if layer == 0 else r)[:, s, 0:SG],
                                     start=True, stop=True).then_inc(lin[layer], 1)
                over_groups(pe, body)
            linear(0)
            linear(1)

            def body(g, s):
                pe.wait_ge(y_ready, g + 1 + LEAD)
                pe.wait_ge(normed, g + LEAD)
                for k in range(T):
                    mm = nc.tensor.transpose(ps_y[:, s, k], y[:, s, at(k, P)], m["ident"][:])
                mm.then_inc(y_turned, 1)
            over_groups(pe, body)

        @block.scalar
        def _(act):
            lead(act, [*lin_out, normed], LEAD)
            def bias_out(layer, g, s):
                act.wait_ge(lin[layer], g + 1 + LEAD)
                nc.scalar.activation(acc[:, layer, at(g, SG)], ps_lin[:, s, 0:SG], ACT.Identity,
                                     bias=vec[:, B1 + 3 * layer:B1 + 3 * layer + 1]).then_inc(lin_out[layer], 1)

            def bn_deviation(layer):
                act.wait_ge(bn_var, layer + 1)
                nc.scalar.activation(dev[:, layer:layer + 1], mv[:, layer, 1:2], ACT.Sqrt,
                                     bias=m["eps"][:]).then_inc(bn_dev, 1)

            over_groups(act, lambda g, s: bias_out(0, g, s))
            bn_deviation(0)
            act.wait_ge(scaled[0], 1)

            def hidden(g, s):
                act.wait_ge(lin[1], g + LEAD)
                nc.scalar.activation(r[:, s, 0:SG], acc[:, 0, at(g, SG)], ACT.Relu, bias=shift[:, 0:1],
                                     scale=scale[:, 0:1]).then_inc(relu_ready, 1)
                bias_out(1, g, s)
            over_groups(act, hidden)
            bn_deviation(1)
            act.wait_ge(scaled[1], 1)

            def last_relu(g, s):
                act.wait_ge(y_ready, g + LEAD)
                nc.scalar.activation(r[:, s], acc[:, 1, at(g, G)], ACT.Relu, bias=shift[:, 1:2],
                                     scale=scale[:, 1:2]).then_inc(h_ready, 1)

            def normalise(g, s):
                act.wait_ge(ln_var, g + 1)
                nc.scalar.activation(ldev[:], lmv[:, :, 1], ACT.Sqrt, bias=m["eps"][:]).then_inc(ln_dev, 1)
                act.wait_ge(ln_ready, g + 1)
                act.wait_ge(out_stored[s], before(g, s, 16, 2) + DMA_LEAD)
                for k in range(T):
                    last = nc.scalar.activation(xo[:, s, k], ps_y[:, s, k], ACT.Identity, bias=lsh[:, s, k:k + 1],
                                                scale=lsc[:, s, k:k + 1])
                last.then_inc(normed, 1)

            last_relu(0, 0)

            def body(g, s):
                last_relu(g + 1, 1 - s)
                normalise(g, s)
            with act.Fori(0, NG // 2) as turn:
                body(turn * 2, 0)
                body(turn * 2 + 1, 1)
            normalise(NG - 1, 0)

        @block.vector
        def _(dve):
            lead(dve, [y_ready], LEAD)
            def divide(g, s):
                do = Steps(dve, div_step, g * 3).ordered
                part = o[:, s]
                do(nc.vector.tensor_scalar(part, acc[:, 1, at(g, SG)], SM_EPS, None, ALU.add))
                do(nc.vector.reciprocal(part, part))
                do(nc.vector.tensor_tensor(part, acc[:, 0, at(g, SG)], part, ALU.mult))
                nc.vector.tensor_scalar(part, part, vec[:, BGAT:BGAT + 1], None, ALU.add).then_inc(o_ready, 1)

            def slice_stats(layer, g):
                dve.wait_ge(lin_out[layer], g + 1 + LEAD)
                nc.vector.bn_stats(stats[:, bass.ds(g, 1)].rearrange("p a s -> p (a s)"),
                                   acc[:, layer, at(g, SG)]).then_inc(stat[layer], 1)

            def scales(layer):
                dve.wait_ge(stat[layer], NG)
                nc.vector.bn_aggr(mv[:, layer], stats[:].rearrange("p g s -> p (g s)")).then_inc(bn_var, 1)
                dve.wait_ge(bn_dev, layer + 1)
                batch_norm_scale(nc, Steps(dve, bn_step, 3 * layer).ordered,
                                 mv[:, layer], dev[:, layer:layer + 1], scale[:, layer:layer + 1], shift[:, layer:layer + 1],
                                 vec[:, G1 + 3 * layer:G1 + 3 * layer + 1],
                                 vec[:, BE1 + 3 * layer:BE1 + 3 * layer + 1]).then_inc(scaled[layer], 1)

            divide(0, 0)

            def first(g, s):
                dve.wait_ge(lin[0], g + LEAD)
                divide(g + 1, 1 - s)
                slice_stats(0, g)
            with dve.Fori(0, NG // 2) as turn:
                first(turn * 2, 0)
                first(turn * 2 + 1, 1)
            slice_stats(0, NG - 1)
            scales(0)
            over_groups(dve, lambda g, s: slice_stats(1, g))
            scales(1)

            def body(g, s):
                dve.wait_ge(h_ready, g + 1)
                dve.wait_ge(x1_in[s], landed(g, s, 16, 2))
                dve.wait_ge(y_turned, g + LEAD)
                nc.vector.scalar_tensor_tensor(y[:, s], x1t[:, s], 2.0, r[:, s], ALU.mult, ALU.add).then_inc(y_ready, 1)
                dve.wait_ge(y_turned, g + 1 + LEAD)
                do = Steps(dve, ln_step, g * 2).ordered
                layer_norm_moments(nc, do, lambda: alone(dve, passed), ps_y[:, s], lst, lmv).then_inc(ln_var, 1)
                dve.wait_ge(ln_dev, g + 1)
                layer_norm_scale(nc, do, lmv, ldev[:], lsc[:, s], lsh[:, s]).then_inc(ln_ready, 1)
            over_groups(dve, body)


_WEIGHTS = ["L0_gnn_WQ", "L0_gnn_WK", "L0_gnn_WV", "L0_gnn_WE", "L1_gnn_W", "L1_gnn_W1", "L1_gnn_W2"]
_VECTORS = ["L0_gnn_bn_gamma", "L0_gnn_bn_beta", "L1_gnn_att_src", "L1_gnn_att_dst", "L1_gnn_bias_gat", "L1_gnn_b1",
            "L1_gnn_g1", "L1_gnn_be1", "L1_gnn_b2", "L1_gnn_g2", "L1_gnn_be2"]


def kernel(**inputs):
    import numpy as np
    import concourse.bacc as bacc
    from concourse.bass_utils import run_bass_kernel_spmd

    src = np.asarray(inputs["src"])
    dst = np.pad(np.asarray(inputs["dst"]), (0, NC * CE - E), constant_values=-1)
    arrays = {
        "x": np.pad(np.asarray(inputs["x"]), ((0, NP - N), (0, 0))),
        "src": np.pad(src, (0, NC * CE - E)),
        "dst_rows": dst.reshape(NC, CE),
        "dst_cols": np.ascontiguousarray(dst.reshape(NC, P, K).transpose(1, 0, 2)),
        "edges": np.ascontiguousarray(inputs["edge_attr_128"]),
        "weights": np.ascontiguousarray(np.stack([np.asarray(inputs[n]) for n in _WEIGHTS], axis=1)),
        "vectors": np.ascontiguousarray(np.stack([np.asarray(inputs[n]) for n in _VECTORS], axis=1)),
    }
    nc = bacc.Bacc("TRN2", target_bir_lowering=False, num_devices=1)
    args = [nc.dram_tensor(f"in_{n}", a.shape, mybir.dt.from_np(a.dtype), kind="ExternalInput").ap()
            for n, a in arrays.items()]
    out = nc.dram_tensor("out", (NP, D), F32, kind="ExternalOutput").ap()
    build(nc, *args, out)
    result = run_bass_kernel_spmd(nc, [{f"in_{n}": a for n, a in arrays.items()}], core_ids=[0])
    return result.results[0]["out"][:N]
```

```python
from contextlib import ExitStack

import concourse.bass as bass
from concourse import mybir

F32 = mybir.dt.float32
I32 = mybir.dt.int32
ALU = mybir.AluOpType
ACT = mybir.ActivationFunctionType
AX = mybir.AxisListType.X

P = 128
D = 128
H = 8
DH = D // H
N = 12500
E = 212500
G = 512
NG = -(-N // G)
NP = NG * G
T = G // P
CE = 512
K = CE // P
U, V = 4, 8
NC = -(-(-(-E // CE)) // V) * V
CR = 104
CJ = NC // CR
W = 64
SG = N // NG
ROW1 = 132
LAST = E - (NC - 1) * CE
FAR_ROW = 32
SHIFTS = N // W + 1
FAR = 1.0e6
MASKED = -1.0e30
NORM_EPS = 1e-5
PIECES = ((0, 3), (3, 12), (12, NG))
LEAD = 2
DMA_LEAD = 16
ATTN_EPS = 1e-6
SM_EPS = 1e-16
SLOPE = 0.2
CLIP = 5.0
assert V % U == 0 and NG * SG == N and CR * CJ == NC and LAST % K == 0 and NG % 2 == 1

WQ, WK, WV, WE, W1G, WM1, WM2 = range(7)
(GAMMA0, BETA0, ASRC, ADST, BGAT, B1, G1, BE1, B2, G2, BE2) = range(11)


class Steps:

    def __init__(self, eng, sem, start=0):
        self.eng, self.sem, self.start, self.n = eng, sem, start, 0

    def ordered(self, ins):
        self.n += 1
        ins.then_inc(self.sem, 1)
        self.eng.wait_ge(self.sem, self.start + self.n)


def alone(eng, passed):
    eng.sem_inc(passed, 1)


def lead(eng, sems, by):
    for sem in sems:
        eng.sem_inc(sem, by)


def counted(nc, ctx, m, name):
    m["used"].append(ctx.enter_context(nc.semaphore(name)))
    return m["used"][-1]


def over_groups(eng, body):
    with eng.Fori(0, NG // 2) as turn:
        body(turn * 2, 0)
        body(turn * 2 + 1, 1)
    body(NG - 1, 0)


def over_chunks(eng, body, last, slots):
    with eng.Fori(0, last // slots - 1) as turn:
        for u in range(slots):
            body(turn * slots + u, u, False)
    for u in range(slots):
        body(last - slots + u, u, True)


def over_far_windows(eng, m, body):
    most = eng.value_load(m["base_row"][FAR_ROW:FAR_ROW + 1, NC:NC + 1], min_val=0, max_val=N - 1)
    with eng.If(most >= W):
        with eng.register() as visit:
            eng.reg_mov(visit, 0)
            def windows(c):
                reach = eng.value_load(m["base_row"][FAR_ROW:FAR_ROW + 1, bass.ds(c, 1)], min_val=0, max_val=N - 1)
                with eng.If(reach >= W):
                    with eng.Fori(1, reach // W + 1) as j:
                        eng.reg_add(visit, visit, 1)
                        body(c, j, eng.snap(visit, min_val=1, max_val=NC * SHIFTS))

            with eng.Fori(0, NC - 1) as c:
                windows(c)
            windows(NC - 1)


def window_base(nc, eng, m, c, j):
    base = eng.value_load(m["base_row"][0:1, bass.ds(c, 1)], min_val=0, max_val=N - 1)
    return nc.s_assert_within(base + j * W, 0, N - 1, skip_runtime_bounds_check_because="j*64 is at most the chunk's "
                              "largest destination less base[c]")


def at(i, n):
    return bass.ds(i * n, n)


def row(ap, i):
    entry = ap[bass.ds(i, 1)]
    return entry.rearrange("a p k d -> p (a k) d") if len(ap.shape) == 4 else entry.rearrange("a p k -> p (a k)")


def before(i, slot, each, slots):
    return (i - slot) * (each // slots)


def landed(i, slot, each, slots):
    return before(i, slot, each, slots) + each


def build(nc, x, src, dst_rows, dst_cols, edges, weights, vectors, out):
    with ExitStack() as ctx:
        def sb(name, shape, dt=F32):
            return ctx.enter_context(nc.sbuf_tensor(name, shape, dt))

        def dram(name, shape, dt=F32):
            return nc.dram_tensor(name, shape, dt, kind="Internal").ap()

        m = {}
        m["q_table"] = dram("q_table", [NP, D])
        m["kv_table"] = dram("kv_table", [NP, 2 * D])
        m["xl_table"] = dram("xl_table", [NP, ROW1])
        m["ad_row"] = dram("ad_row", [NP])
        m["x1t_table"] = dram("x1t_table", [P, NP])
        m["den_rows"] = dram("den_rows", [H, NP])
        m["inv_rows"] = dram("inv_rows", [H, NP])
        m["den_row1"] = dram("den_row1", [NP])
        m["inv_row1"] = dram("inv_row1", [NP])
        m["base_table"] = dram("base_table", [NC], I32)
        m["far_table"] = dram("far_table", [NC], I32)
        m["acc"] = sb("acc", [P, 3, NP])
        m["dst_local"] = sb("dst_local", [P, NC, K])
        m["base_row"] = sb("base_row", [P, NC + 1], I32)
        m["w"] = sb("w", [P, 7, D])
        m["vec"] = sb("vec", [P, 11])
        m["ident"] = sb("ident", [P, P])
        m["iota"] = sb("iota", [P, W])
        m["shifts"] = sb("shifts", [P, SHIFTS])
        m["used"] = []
        m["passed"] = ctx.enter_context(nc.semaphore("passed"))
        m["power"] = sb("power", [P, T])
        prologue(nc, m, dst_rows, dst_cols, weights, vectors)
        project(nc, m, x)
        edges0(nc, m, src, edges)
        far_windows0(nc, m, src, edges)
        nodes0(nc, m)
        edges1(nc, m, src)
        far_windows1(nc, m, src)
        nodes1(nc, m, out)


def prologue(nc, m, dst_rows, dst_cols, weights, vectors):
    with ExitStack() as ctx:
        sem = lambda name: counted(nc, ctx, m, name)
        sb = lambda name, shape, dt=F32: ctx.enter_context(nc.sbuf_tensor(name, shape, dt))
        weights_in, rows_in, cols_in = sem("weights_in"), sem("rows_in"), sem("cols_in")
        base_ready, base_stored, base_back = sem("base_ready"), sem("base_stored"), sem("base_back")
        ident_zero, made, step = sem("ident_zero"), sem("made"), sem("pro_step")
        rows = m["acc"][0:CR, 0, 0:CJ * CE].rearrange("p (j e) -> p j e", e=CE)
        low = m["acc"][0:CR, 1, 0:CJ * CE].rearrange("p (j e) -> p j e", e=CE)
        rows_i = m["acc"][0:CR, 2, 0:CJ * CE].bitcast(I32).rearrange("p (j e) -> p j e", e=CE)
        cols_i = m["acc"][:, 0, CJ * CE:CJ * CE + NC * K].bitcast(I32).rearrange("p (c k) -> p c k", k=K)
        base_f = sb("base_f", [P, CJ])
        base_i = sb("base_i", [P, CJ], I32)
        far_f = sb("far_f", [P, CJ])
        far_i = sb("far_i", [P, CJ], I32)
        base_all_i = sb("base_all_i", [P, NC], I32)
        base_all = sb("base_all", [P, NC])
        far_row = sb("far_row", [P, NC + 1])
        block = ctx.enter_context(nc.Block())

        @block.sync
        def _(sp):
            sp.dma_start(rows_i, dst_rows.rearrange("(p j) e -> p j e", j=CJ)).then_inc(rows_in, 16)
            sp.dma_start(cols_i, dst_cols).then_inc(cols_in, 16)
            sp.wait_ge(base_ready, 1)
            sp.dma_start(m["base_table"].rearrange("(p j) -> p j", j=CJ), base_i[0:CR, :]).then_inc(base_stored, 16)
            sp.dma_start(m["far_table"].rearrange("(p j) -> p j", j=CJ), far_i[0:CR, :]).then_inc(base_stored, 16)
            sp.wait_ge(base_stored, 32)
            sp.dma_start(m["base_row"][0:1, 0:NC], m["base_table"].unsqueeze(0)).then_inc(base_back, 16)
            sp.dma_start(m["base_row"][FAR_ROW:FAR_ROW + 1, 0:NC], m["far_table"].unsqueeze(0)).then_inc(base_back, 16)
            sp.dma_start(base_all_i[:], m["base_table"].partition_broadcast(P)).then_inc(base_back, 16)
            sp.wait_ge(base_back, 48)

        @block.scalar
        def _(act):
            act.dma_start(m["w"][:], weights).then_inc(weights_in, 16)
            act.dma_start(m["vec"][:], vectors).then_inc(weights_in, 16)
            act.wait_ge(weights_in, 32)

        @block.gpsimd
        def _(pool):
            nc.gpsimd.memset(m["ident"][:], 0.0).then_inc(ident_zero, 1)
            pool.wait_ge(ident_zero, 1)
            nc.gpsimd.affine_select(out=m["ident"][:], in_=m["ident"][:], compare_op=ALU.not_equal, fill=1.0,
                                    base=0, pattern=[[-1, P]], channel_multiplier=1).then_inc(made, 1)
            nc.gpsimd.iota(m["iota"][:], pattern=[[1, W]], base=0, channel_multiplier=0,
                           allow_small_or_imprecise_dtypes=True).then_inc(made, 1)
            nc.gpsimd.iota(m["shifts"][:], pattern=[[W, SHIFTS]], base=0, channel_multiplier=0,
                           allow_small_or_imprecise_dtypes=True).then_inc(made, 1)
            nc.gpsimd.memset(m["power"][:], -0.5).then_inc(made, 1)
            pool.wait_ge(made, 4)

        @block.vector
        def _(dve):
            do = Steps(dve, step).ordered
            dve.wait_ge(rows_in, 16)
            do(nc.vector.tensor_copy(rows, rows_i))
            do(nc.vector.tensor_scalar(low, rows, 0.0, FAR, ALU.is_lt, ALU.mult))
            do(nc.vector.tensor_tensor(low, low, rows, ALU.add))
            do(nc.vector.tensor_reduce(base_f[0:CR, :], low, AX, ALU.min))
            do(nc.vector.tensor_reduce(far_f[0:CR, :], rows, AX, ALU.max))
            do(nc.vector.tensor_copy(base_i[0:CR, :], base_f[0:CR, :]))
            do(nc.vector.tensor_tensor(far_f[0:CR, :], far_f[0:CR, :], base_f[0:CR, :], ALU.subtract))
            nc.vector.tensor_copy(far_i[0:CR, :], far_f[0:CR, :]).then_inc(base_ready, 1)
            dve.wait_ge(cols_in, 16)
            do(nc.vector.tensor_copy(m["dst_local"][:], cols_i))
            dve.wait_ge(base_back, 48)
            do(nc.vector.tensor_copy(base_all[:], base_all_i[:]))
            do(nc.vector.tensor_tensor(m["dst_local"][:], m["dst_local"][:],
                                       base_all[:].unsqueeze(2).to_broadcast([P, NC, K]), ALU.subtract))
            reach = far_row[FAR_ROW:FAR_ROW + 1]
            do(nc.vector.tensor_copy(reach[:, 0:NC], m["base_row"][FAR_ROW:FAR_ROW + 1, 0:NC]))
            do(nc.vector.tensor_reduce(reach[:, NC:NC + 1], reach[:, 0:NC], AX, ALU.max))
            do(nc.vector.tensor_copy(m["base_row"][FAR_ROW:FAR_ROW + 1, NC:NC + 1], reach[:, NC:NC + 1]))


def project(nc, m, x):
    with ExitStack() as ctx:
        sem = lambda name: counted(nc, ctx, m, name)
        sb = lambda name, shape, dt=F32: ctx.enter_context(nc.sbuf_tensor(name, shape, dt))
        ps = lambda name, shape: ctx.enter_context(nc.psum_tensor(name, shape, F32))
        x_in = [sem(f"x_in{s}") for s in range(2)]
        stored = [sem(f"qkv_stored{s}") for s in range(2)]
        turned, copied, kept = sem("x_turned"), sem("xt_copied"), sem("xt_kept")
        projected, q_out, kv_out = sem("projected"), sem("q_out"), sem("kv_out")
        xn = sb("xn", [P, 2, T, D])
        xt = sb("xt", [P, 2, G])
        q = sb("q", [P, 2, T, D])
        kv = sb("kv", [P, 2, T, 2 * D])
        ps_xt = ps("ps_xt", [P, 2, G])
        ps_qkv = ps("ps_qkv", [P, T, G])
        xg = x.rearrange("(g k p) d -> g p k d", k=T, p=P)
        qg = m["q_table"].rearrange("(g k p) d -> g p k d", k=T, p=P)
        kvg = m["kv_table"].rearrange("(g k p) d -> g p k d", k=T, p=P)
        wqkv = m["w"][:, WQ:WV + 1, :].rearrange("p a d -> p (a d)")
        block = ctx.enter_context(nc.Block())

        @block.sync
        def _(sp):
            lead(sp, [*stored], DMA_LEAD)
            for s in range(2):
                sp.dma_start(xn[:, s], xg[s]).then_inc(x_in[s], 16)

            def body(g, s, ahead):
                if ahead:
                    sp.wait_ge(turned, g + 1)
                    sp.dma_start(xn[:, s], row(xg, g + 2)).then_inc(x_in[s], 16)
                sp.wait_ge(q_out, g + 1 + LEAD)
                sp.dma_start(row(qg, g), q[:, s]).then_inc(stored[s], 16)
                sp.wait_ge(kv_out, g + 1 + LEAD)
                sp.dma_start(row(kvg, g), kv[:, s]).then_inc(stored[s], 16)

            with sp.Fori(0, (NG - 3) // 2) as turn:
                body(turn * 2, 0, True)
                body(turn * 2 + 1, 1, True)
            for g in range(NG - 3, NG):
                body(g, g % 2, g + 2 < NG)
            sp.wait_ge(stored[0], 32 * (NG // 2 + 1) + DMA_LEAD)
            sp.wait_ge(stored[1], 32 * (NG // 2) + DMA_LEAD)

        @block.tensor
        def _(pe):
            lead(pe, [projected], LEAD)
            def body(g, s):
                pe.wait_ge(x_in[s], landed(g, s, 16, 2))
                pe.wait_ge(kept, g + LEAD)
                for k in range(T):
                    mm = nc.tensor.transpose(ps_xt[:, s, at(k, P)], xn[:, s, k], m["ident"][:])
                mm.then_inc(turned, 1)
                pe.wait_ge(copied, g + 1)
                pe.wait_ge(kv_out, g + LEAD)
                pe.wait_ge(q_out, g + LEAD)
                for k in range(T):
                    mm = nc.tensor.matmul(ps_qkv[:, k, 0:3 * D], xt[:, s, at(k, P)], wqkv, start=True, stop=True)
                mm.then_inc(projected, 1)
            over_groups(pe, body)

        @block.scalar
        def _(act):
            lead(act, [q_out], LEAD)
            def body(g, s):
                act.wait_ge(turned, g + 1)
                act.wait_ge(projected, g + LEAD)
                nc.scalar.copy(xt[:, s], ps_xt[:, s]).then_inc(copied, 1)
                act.wait_ge(projected, g + 1 + LEAD)
                act.wait_ge(stored[s], before(g, s, 32, 2) + DMA_LEAD)
                nc.scalar.mul(q[:, s], ps_qkv[:, :, 0:D], DH ** -0.5).then_inc(q_out, 1)
            over_groups(act, body)

        @block.vector
        def _(dve):
            lead(dve, [kept, kv_out], LEAD)
            def body(g, s):
                dve.wait_ge(copied, g + 1)
                nc.vector.tensor_copy(m["acc"][:, 2, at(g, G)], ps_xt[:, s]).then_inc(kept, 1)
                dve.wait_ge(q_out, g + 1 + LEAD)
                dve.wait_ge(stored[s], before(g, s, 32, 2) + DMA_LEAD)
                nc.vector.tensor_copy(kv[:, s], ps_qkv[:, :, D:3 * D]).then_inc(kv_out, 1)
            over_groups(dve, body)


def edges0(nc, m, src, edges):
    with ExitStack() as ctx:
        sem = lambda name: counted(nc, ctx, m, name)
        sb = lambda name, shape, dt=F32: ctx.enter_context(nc.sbuf_tensor(name, shape, dt))
        ps = lambda name, shape: ctx.enter_context(nc.psum_tensor(name, shape, F32))
        src_in = [sem(f"src_in{u}") for u in range(U)]
        edge_in = [sem(f"edge_in{u}") for u in range(U)]
        kv_in = [sem(f"kv_in{u}") for u in range(U)]
        hot_ready, turned, copied = sem("hot_ready"), sem("edges_turned"), sem("edges_copied")
        spread, gated, scored = sem("spread"), sem("gated"), sem("scored")
        weighed, valued, summed, added = sem("weighed"), sem("valued"), sem("summed"), sem("added")
        mult, clear = sem("mult"), sem("cleared")
        idx = sb("idx", [P, U, K], I32)
        ea = sb("ea", [P, U, K, D])
        qw = sb("qw", [W, U, D])
        kv = sb("kv_g", [P, U, K, 2 * D])
        hot = sb("hot", [P, U, K, W])
        eat = sb("eat", [P, 2, CE])
        hott = sb("hott", [W, 2, CE])
        prod = sb("prod", [P, CE])
        score = sb("score", [P, 2, K * H])
        pex = sb("pex", [P, 2, K, D])
        ps_eat = ps("ps_eat", [P, CE])
        ps_hott = ps("ps_hott", [P, CE])
        ps_eh = ps("ps_eh", [P, 2, K, D])
        ps_q = ps("ps_q", [P, 2, K, D])
        ps_sum = ps("ps_sum", [P, 2, CE])
        src_c = src.rearrange("(c p k) -> c p k", p=P, k=K)
        ea_c = edges[0:(NC - 1) * CE].rearrange("(c p k) d -> c p (k d)", p=P, k=K)
        ea_last = edges[(NC - 1) * CE:E].rearrange("(p k) d -> p (k d)", k=K)
        block = ctx.enter_context(nc.Block())
        acc = m["acc"]

        @block.sync
        def _(sp):
            def load_src(c, u):
                sp.dma_start(idx[:, u], row(src_c, c)).then_inc(src_in[u], 16)

            def load_edges(c, u, last=False):
                if last:
                    sp.dma_start(ea[0:LAST // K, u].rearrange("p k d -> p (k d)"), ea_last).then_inc(edge_in[u], 16)
                else:
                    sp.dma_start(ea[:, u].rearrange("p k d -> p (k d)"),
                                 row(ea_c, c)).then_inc(edge_in[u], 16)

            def load_window(c, u):
                base = sp.value_load(m["base_row"][0:1, bass.ds(c, 1)], min_val=0, max_val=N - 1)
                sp.dma_start(qw[:, u], m["q_table"][bass.ds(base, W), :]).then_inc(edge_in[u], 16)

            for u in range(U):
                load_src(u, u)
            for u in range(U):
                load_edges(u, u)
                load_window(u, u)

            def body(c, u, peeled):
                sp.wait_ge(turned, c + 1)
                load_edges(c + U, u, peeled and c + U == NC - 1)
                sp.wait_ge(spread, c + 1 + LEAD)
                load_window(c + U, u)
                sp.wait_ge(kv_in[u], landed(c, u, 16 * K, U))
                load_src(c + U, u)
            over_chunks(sp, body, NC - U, U)

        @block.gpsimd
        def _(pool):
            def gather(c, u):
                pool.wait_ge(src_in[u], landed(c, u, 16, U))
                alone(pool, m["passed"])
                for k in range(K):
                    nc.gpsimd.indirect_dma_start(
                        out=kv[:, u, k], out_offset=None, in_=m["kv_table"],
                        in_offset=bass.IndirectOffsetOnAxis(ap=idx[:, u, k:k + 1], axis=0)).then_inc(kv_in[u], 16)
            for u in range(U):
                gather(u, u)

            def body(c, u, peeled):
                pool.wait_ge(summed, c + 1 + LEAD)
                gather(c + U, u)
            over_chunks(pool, body, NC - U, U)

        @block.tensor
        def _(pe):
            lead(pe, [spread, summed], LEAD)
            def turn(c, u):
                pe.wait_ge(edge_in[u], landed(c, u, 32, U))
                pe.wait_ge(hot_ready, c + 1)
                pe.wait_ge(copied, c + LEAD)
                for k in range(K):
                    nc.tensor.transpose(ps_eat[:, at(k, P)], ea[:, u, k], m["ident"][:])
                for k in range(K):
                    mm = nc.tensor.transpose(ps_hott[0:W, at(k, P)], hot[:, u, k], m["ident"][:])
                mm.then_inc(turned, 1)

            def spread_out(c, u, first=False):
                b = u % 2
                pe.wait_ge(copied, c + 1 + LEAD)
                if not first:
                    pe.wait_ge(gated, c - 1 + LEAD)
                for k in range(K):
                    nc.tensor.matmul(ps_q[:, b, k], hott[:, b, at(k, P)], qw[:, u], start=True, stop=True)
                for k in range(K):
                    mm = nc.tensor.matmul(ps_eh[:, b, k], eat[:, b, at(k, P)], m["w"][:, WE], start=True, stop=True)
                mm.then_inc(spread, 1)

            def sum_up(c, u):
                b = u % 2
                pe.wait_ge(valued, c + 1)
                for k in range(K):
                    nc.tensor.matmul(ps_sum[:, b, 0:W], kv[:, u, k, D:2 * D], hot[:, u, k], start=(k == 0), stop=(k == K - 1))
                for k in range(K):
                    mm = nc.tensor.matmul(ps_sum[:, b, W:2 * W], pex[:, b, k], hot[:, u, k],
                                          start=(k == 0), stop=(k == K - 1))
                mm.then_inc(summed, 1)

            turn(0, 0)
            turn(1, 1)
            spread_out(0, 0, True)

            def body(c, u, peeled):
                if not (peeled and c + 2 >= NC):
                    turn(c + 2, (u + 2) % U)
                if not (peeled and c + 1 >= NC):
                    spread_out(c + 1, (u + 1) % U)
                sum_up(c, u)
            over_chunks(pe, body, NC, U)

        @block.scalar
        def _(act):
            lead(act, [copied], LEAD)
            def copy_out(c, u, first=False):
                b = u % 2
                act.wait_ge(turned, c + 1)
                if not first:
                    act.wait_ge(spread, c - 1 + LEAD)
                nc.scalar.copy(eat[:, b], ps_eat[:])
                nc.scalar.copy(hott[:, b], ps_hott[0:W, :]).then_inc(copied, 1)

            def weigh(c, u, first=False):
                b = u % 2
                act.wait_ge(scored, c + 1)
                if not first:
                    act.wait_ge(summed, c - 1 + LEAD)
                nc.scalar.activation(pex[:, b].rearrange("p k (h d) -> p (k h) d", d=DH),
                                     score[:, b].unsqueeze(2).to_broadcast([P, K * H, DH]), ACT.Exp).then_inc(weighed, 1)
            copy_out(0, 0, True)
            copy_out(1, 1, True)
            weigh(0, 0, True)

            def body(c, u, peeled):
                if not (peeled and c + 2 >= NC):
                    copy_out(c + 2, (u + 2) % U)
                if not (peeled and c + 1 >= NC):
                    weigh(c + 1, (u + 1) % U)
            over_chunks(act, body, NC, U)

        @block.vector
        def _(dve):
            lead(dve, [gated, added], LEAD)
            def one_hot(c, u):
                nc.vector.tensor_tensor(hot[:, u],
                                        m["dst_local"][:, bass.ds(c, 1), :].rearrange("p a k -> p (a k)")
                                        .unsqueeze(2).to_broadcast([P, K, W]),
                                        m["iota"][:].unsqueeze(1).to_broadcast([P, K, W]),
                                        ALU.is_equal).then_inc(hot_ready, 1)

            def attend(c, u):
                b = u % 2
                flat = lambda v: v.rearrange("p k d -> p (k d)")
                dve.wait_ge(spread, c + 1 + LEAD)
                dve.wait_ge(kv_in[u], landed(c, u, 16 * K, U))
                nc.vector.tensor_tensor(prod[:].rearrange("p (k d) -> p k d", d=D), ps_q[:, b],
                                        kv[:, u, :, 0:D], ALU.mult).then_inc(mult, 1)
                dve.wait_ge(mult, c * 2 + 1)
                nc.vector.tensor_tensor(prod[:], prod[:], flat(ps_eh[:, b]), ALU.mult).then_inc(gated, 1)
                dve.wait_ge(gated, c + 1 + LEAD)
                nc.vector.tensor_reduce(score[:, b], prod[:].rearrange("p (h d) -> p h d", d=DH), AX,
                                        ALU.add).then_inc(mult, 1)
                dve.wait_ge(mult, c * 2 + 2)
                nc.vector.tensor_scalar(score[:, b], score[:, b], CLIP, -CLIP, ALU.min, ALU.max).then_inc(scored, 1)

            def value(c, u):
                b = u % 2
                dve.wait_ge(weighed, c + 1)
                values = kv[:, u, :, D:2 * D]
                nc.vector.tensor_tensor(values, values, pex[:, b], ALU.mult).then_inc(valued, 1)

            def add_up(c, u):
                b = u % 2
                base = dve.value_load(m["base_row"][0:1, bass.ds(c, 1)], min_val=0, max_val=N - 1)
                window = acc[:, 0:2, bass.ds(base, W)]
                dve.wait_ge(summed, c + 1 + LEAD)
                dve.wait_ge(added, c + LEAD)
                nc.vector.tensor_tensor(window, window, ps_sum[:, b, 0:2 * W].rearrange("p (a w) -> p a w", w=W),
                                        ALU.add).then_inc(added, 1)

            nc.vector.memset(acc[:, 0], 0.0).then_inc(clear, 1)
            nc.vector.memset(acc[:, 1], ATTN_EPS).then_inc(clear, 1)
            dve.wait_ge(clear, 2)
            one_hot(0, 0)
            one_hot(1, 1)
            one_hot(2, 2)
            attend(0, 0)
            value(0, 0)

            def body(c, u, peeled):
                if not (peeled and c + 3 >= NC):
                    one_hot(c + 3, (u + 3) % U)
                if not (peeled and c + 1 >= NC):
                    attend(c + 1, (u + 1) % U)
                add_up(c, u)
                if not (peeled and c + 1 >= NC):
                    value(c + 1, (u + 1) % U)
            over_chunks(dve, body, NC, U)


def far_windows0(nc, m, src, edges):
    with ExitStack() as ctx:
        sem = lambda name: counted(nc, ctx, m, name)
        sb = lambda name, shape, dt=F32: ctx.enter_context(nc.sbuf_tensor(name, shape, dt))
        ps = lambda name, shape: ctx.enter_context(nc.psum_tensor(name, shape, F32))
        cleared = sem("far0_cleared")
        src_in, edge_in, kv_in = sem("far0_src_in"), sem("far0_edge_in"), sem("far0_kv_in")
        hot_ready, turned, copied = sem("far0_hot_ready"), sem("far0_turned"), sem("far0_copied")
        spread, scored, weighed = sem("far0_spread"), sem("far0_scored"), sem("far0_weighed")
        valued, summed, added, step = sem("far0_valued"), sem("far0_summed"), sem("far0_added"), sem("far0_step")
        idx = sb("far0_idx", [P, K], I32)
        ea = sb("far0_ea", [P, K, D])
        qw = sb("far0_qw", [W, D])
        kv = sb("far0_kv", [P, K, 2 * D])
        nodes = sb("far0_nodes", [P, W])
        hot = sb("far0_hot", [P, K, W])
        eat, hott = sb("far0_eat", [P, CE]), sb("far0_hott", [W, CE])
        prod, score, pex = sb("far0_prod", [P, K, D]), sb("far0_score", [P, K * H]), sb("far0_pex", [P, K, D])
        ps_eat, ps_hott = ps("far0_ps_eat", [P, CE]), ps("far0_ps_hott", [P, CE])
        ps_eh, ps_q, ps_sum = ps("far0_ps_eh", [P, K, D]), ps("far0_ps_q", [P, K, D]), ps("far0_ps_sum", [P, CE])
        src_c = src.rearrange("(c p k) -> c p k", p=P, k=K)
        ea_c = edges[0:(NC - 1) * CE].rearrange("(c p k) d -> c p (k d)", p=P, k=K)
        ea_last = edges[(NC - 1) * CE:E].rearrange("(p k) d -> p (k d)", k=K)
        block = ctx.enter_context(nc.Block())

        @block.sync
        def _(sp):
            sp.wait_ge(cleared, 1)
            def body(c, j, visit):
                sp.dma_start(idx[:], row(src_c, c)).then_inc(src_in, 16)
                base = window_base(nc, sp, m, c, j)
                sp.dma_start(qw[:], m["q_table"][bass.ds(base, W), :]).then_inc(edge_in, 16)
                if isinstance(c, int):
                    sp.dma_start(ea[0:LAST // K].rearrange("p k d -> p (k d)"), ea_last).then_inc(edge_in, 16)
                else:
                    sp.dma_start(ea[:].rearrange("p k d -> p (k d)"), row(ea_c, c)).then_inc(edge_in, 16)
                sp.wait_ge(added, visit)
            over_far_windows(sp, m, body)

        @block.gpsimd
        def _(pool):
            def body(c, j, visit):
                pool.wait_ge(src_in, visit * 16)
                alone(pool, m["passed"])
                for k in range(K):
                    nc.gpsimd.indirect_dma_start(
                        out=kv[:, k], out_offset=None, in_=m["kv_table"],
                        in_offset=bass.IndirectOffsetOnAxis(ap=idx[:, k:k + 1], axis=0)).then_inc(kv_in, 16)
            over_far_windows(pool, m, body)

        @block.tensor
        def _(pe):
            def body(c, j, visit):
                pe.wait_ge(edge_in, visit * 32)
                pe.wait_ge(hot_ready, visit)
                for k in range(K):
                    nc.tensor.transpose(ps_eat[:, at(k, P)], ea[:, k], m["ident"][:])
                for k in range(K):
                    mm = nc.tensor.transpose(ps_hott[0:W, at(k, P)], hot[:, k], m["ident"][:])
                mm.then_inc(turned, 1)
                pe.wait_ge(copied, visit)
                alone(pe, m["passed"])
                for k in range(K):
                    nc.tensor.matmul(ps_q[:, k], hott[:, at(k, P)], qw[:], start=True, stop=True)
                for k in range(K):
                    mm = nc.tensor.matmul(ps_eh[:, k], eat[:, at(k, P)], m["w"][:, WE], start=True, stop=True)
                mm.then_inc(spread, 1)
                pe.wait_ge(valued, visit)
                alone(pe, m["passed"])
                for k in range(K):
                    nc.tensor.matmul(ps_sum[:, 0:W], kv[:, k, D:2 * D], hot[:, k], start=(k == 0), stop=(k == K - 1))
                for k in range(K):
                    mm = nc.tensor.matmul(ps_sum[:, W:2 * W], pex[:, k], hot[:, k], start=(k == 0), stop=(k == K - 1))
                mm.then_inc(summed, 1)
            over_far_windows(pe, m, body)

        @block.scalar
        def _(act):
            def body(c, j, visit):
                act.wait_ge(turned, visit)
                nc.scalar.copy(eat[:], ps_eat[:])
                nc.scalar.copy(hott[:], ps_hott[0:W, :]).then_inc(copied, 1)
                act.wait_ge(scored, visit)
                nc.scalar.activation(pex[:].rearrange("p k (h d) -> p (k h) d", d=DH),
                                     score[:].unsqueeze(2).to_broadcast([P, K * H, DH]), ACT.Exp).then_inc(weighed, 1)
            over_far_windows(act, m, body)

        @block.vector
        def _(dve):
            nc.vector.memset(ea[:], 0.0).then_inc(cleared, 1)
            dve.sem_inc(step, 4)
            def body(c, j, visit):
                do = Steps(dve, step, visit * 4).ordered
                do(nc.vector.tensor_tensor(nodes[:], m["iota"][:], m["shifts"][:, bass.ds(j, 1)].to_broadcast([P, W]),
                                           ALU.add))
                nc.vector.tensor_tensor(hot[:], m["dst_local"][:, bass.ds(c, 1), :].rearrange("p a k -> p (a k)")
                                        .unsqueeze(2).to_broadcast([P, K, W]),
                                        nodes[:].unsqueeze(1).to_broadcast([P, K, W]),
                                        ALU.is_equal).then_inc(hot_ready, 1)
                dve.wait_ge(spread, visit)
                dve.wait_ge(kv_in, visit * (16 * K))
                do(nc.vector.tensor_tensor(prod[:], ps_q[:], kv[:, :, 0:D], ALU.mult))
                do(nc.vector.tensor_tensor(prod[:], prod[:], ps_eh[:], ALU.mult))
                do(nc.vector.tensor_reduce(score[:], prod[:].rearrange("p k (h d) -> p (k h) d", d=DH), AX, ALU.add))
                nc.vector.tensor_scalar(score[:], score[:], CLIP, -CLIP, ALU.min, ALU.max).then_inc(scored, 1)
                dve.wait_ge(weighed, visit)
                values = kv[:, :, D:2 * D]
                nc.vector.tensor_tensor(values, values, pex[:], ALU.mult).then_inc(valued, 1)
                base = window_base(nc, dve, m, c, j)
                window = m["acc"][:, 0:2, bass.ds(base, W)]
                dve.wait_ge(summed, visit)
                nc.vector.tensor_tensor(window, window, ps_sum[:, 0:2 * W].rearrange("p (a w) -> p a w", w=W),
                                        ALU.add).then_inc(added, 1)
                dve.wait_ge(added, visit)
            over_far_windows(dve, m, body)


def batch_norm_scale(nc, do, mv, rstd, scale, shift, gamma, beta):
    do(nc.vector.tensor_tensor(scale, rstd, gamma, ALU.mult))
    do(nc.vector.tensor_tensor(shift, mv[:, 0:1], scale, ALU.mult))
    return nc.vector.tensor_tensor(shift, beta, shift, ALU.subtract)


def moments(nc, do, hold, y, stats, mv):
    for k in range(T):
        last = nc.vector.bn_stats(stats[:, k], y[:, k])
    do(last)
    hold()
    for k in range(T):
        last = nc.vector.bn_aggr(mv[:, k], stats[:, k])
    do(last)
    return nc.vector.tensor_scalar(mv[:, :, 1], mv[:, :, 1], NORM_EPS, None, ALU.add)


def one_over_deviation(nc, out, var, power):
    return nc.gpsimd.tensor_tensor(out, var, power, ALU.pow)


def nodes0(nc, m):
    with ExitStack() as ctx:
        sem = lambda name: counted(nc, ctx, m, name)
        sb = lambda name, shape, dt=F32: ctx.enter_context(nc.sbuf_tensor(name, shape, dt))
        ps = lambda name, shape: ctx.enter_context(nc.psum_tensor(name, shape, F32))
        wt_turned, wt_copied, wa_made, wa_ready = sem("wt_turned"), sem("wt_copied"), sem("wa_made"), sem("wa_ready")
        h_step, scale_ready, ones_set = sem("h_step"), sem("scale_ready"), sem("ones_set")
        bn_var, bn_dev, ln_var, ln_dev = sem("bn_var"), sem("bn_dev"), sem("ln_var"), sem("ln_dev")
        den_out, den_in, inverted, inv_out = sem("den_out"), sem("den_in"), sem("inverted"), sem("inv_out")
        inv_in = [sem(f"inv_in{piece}") for piece in range(len(PIECES))]
        hn_ready, y_ready, y_turned = sem("hn_ready"), sem("y_ready"), sem("y_turned")
        ln_step, ln_ready, x1_ready = sem("ln_step"), sem("ln_ready"), sem("x1_ready")
        x1_turned, x1t_ready, multiplied = sem("x1_turned"), sem("x1t_ready"), sem("multiplied")
        row_ready, logit_read = sem("row_ready"), sem("logit_read")
        taken, kept = sem("taken"), sem("max_kept")
        x1t_out = [sem(f"x1t_out{s}") for s in range(2)]
        row_out = [sem(f"row_out{s}") for s in range(2)]
        acc, vec, w = m["acc"], m["vec"], m["w"]
        stats = sb("bn_slices", [P, NG, 6])
        mv, scale, shift = sb("bn_mv", [P, 2]), sb("bn_scale", [P, 1]), sb("bn_shift", [P, 1])
        dev = sb("bn_dev", [P, 1])
        w1gt = sb("w1gt", [P, D])
        wa = sb("wa", [P, 2])
        waug = sb("waug", [P, ROW1])
        wa_both = sb("wa_both", [P, P])
        hn = sb("hn", [P, 2, G])
        y = sb("y", [P, 2, G])
        lst, lmv = sb("lst", [P, T, 6]), sb("lmv", [P, T, 2])
        lsc, lsh, lrs = sb("lsc", [P, 2, T]), sb("lsh", [P, 2, T]), sb("lrs", [P, T])
        x1 = sb("x1", [P, T, D])
        x1t = sb("x1t", [P, 2, G])
        xl = sb("xl", [P, 2, T, ROW1])
        ad = sb("ad", [1, 2, G])
        logit = sb("logit", [P, G])
        ps_y = ps("ps_y", [P, T, D])
        ps_x1t = ps("ps_x1t", [P, G])
        ps_xl = ps("ps_xl", [P, T, 2 * D])
        ps_xlt = ps("ps_xlt", [P, G])
        ps_logit = ps("ps_logit", [P, G])
        ps_ad = ps("ps_ad", [P, G])
        table = m["xl_table"].rearrange("(g k p) d -> g p k d", k=T, p=P)
        block = ctx.enter_context(nc.Block())

        den = sb("den0", [P, H * NP // P])

        def inverse_back(eng, heads):
            for piece, (first, end) in enumerate(PIECES):
                for h in heads:
                    eng.dma_start(acc[h * DH:(h + 1) * DH, 1, first * G:end * G],
                                  m["inv_rows"][h, first * G:end * G].partition_broadcast(DH)).then_inc(inv_in[piece], 16)

        @block.sync
        def _(sp):
            sp.dma_start(m["den_rows"], acc[0:P:DH, 1, :]).then_inc(den_out, 16)
            sp.wait_ge(den_out, 16)
            sp.dma_start(den[:], m["den_rows"].rearrange("h (a n) -> (h a) n", a=P // H)).then_inc(den_in, 16)
            sp.wait_ge(inverted, 1)
            sp.dma_start(m["inv_rows"].rearrange("h (a n) -> (h a) n", a=P // H), den[:]).then_inc(inv_out, 16)
            sp.wait_ge(inv_out, 16)
            inverse_back(sp, range(0, H, 2))
            lead(sp, [*x1t_out, *row_out], DMA_LEAD)
            def body(g, s):
                sp.wait_ge(x1t_ready, g + 1)
                sp.dma_start(m["x1t_table"][:, at(g, G)], x1t[:, s]).then_inc(x1t_out[s], 16)
                sp.wait_ge(row_ready, g + 1 + LEAD)
                sp.dma_start(row(table, g), xl[:, s]).then_inc(row_out[s], 16)
                sp.dma_start(m["ad_row"][at(g, G)].unsqueeze(0), ad[:, s]).then_inc(row_out[s], 16)
            over_groups(sp, body)
            for s in range(2):
                sp.wait_ge(x1t_out[s], 16 * ((NG + 1 - s) // 2) + DMA_LEAD)
                sp.wait_ge(row_out[s], 32 * ((NG + 1 - s) // 2) + DMA_LEAD)

        @block.gpsimd
        def _(pool):
            pool.wait_ge(bn_var, 1)
            one_over_deviation(nc, dev[:], mv[:, 1:2], m["power"][:, 0:1]).then_inc(bn_dev, 1)
            pool.wait_ge(scale_ready, 1)
            nc.gpsimd.memset(acc[:, 1], 1.0).then_inc(ones_set, 1)
            with pool.Fori(0, NG) as g:
                pool.wait_ge(ln_var, g + 1)
                one_over_deviation(nc, lrs[:], lmv[:, :, 1], m["power"][:]).then_inc(ln_dev, 1)
            pool.wait_ge(ones_set, 1)

        @block.tensor
        def _(pe):
            lead(pe, [x1_turned], LEAD)
            nc.tensor.transpose(ps_x1t[:, 0:D], w[:, W1G], m["ident"][:]).then_inc(wt_turned, 1)
            pe.wait_ge(wt_copied, 1)
            nc.tensor.matmul(ps_ad[:, 0:2], w1gt[:], vec[:, ASRC:ADST + 1], start=True, stop=True).then_inc(wa_made, 1)
            pe.wait_ge(wa_ready, 1)

            def turn_y(g, s):
                pe.wait_ge(y_ready, g + 1 + LEAD)
                for k in range(T):
                    mm = nc.tensor.transpose(ps_y[:, k], y[:, s, at(k, P)], m["ident"][:])
                mm.then_inc(y_turned, 1)

            def turn_x1(g):
                pe.wait_ge(x1_ready, g + 1)
                for k in range(T):
                    mm = nc.tensor.transpose(ps_x1t[:, at(k, P)], x1[:, k], m["ident"][:])
                mm.then_inc(x1_turned, 1)

            def multiply(g, s):
                pe.wait_ge(x1t_ready, g + 1)
                pe.wait_ge(row_ready, g + LEAD)
                pe.wait_ge(taken, 2 * g + LEAD)
                nc.tensor.matmul(ps_xlt[:], w[:, W1G], x1t[:, s], start=True, stop=True)
                nc.tensor.matmul(ps_logit[:], wa_both[:], x1t[:, s], start=True, stop=True)
                nc.tensor.matmul(ps_ad[0:1, :], wa[:, 1:2], x1t[:, s], start=True, stop=True)
                for k in range(T):
                    mm = nc.tensor.matmul(ps_xl[:, k, 0:ROW1], x1t[:, s, at(k, P)], waug[:], start=True, stop=True)
                mm.then_inc(multiplied, 1)

            turn_y(0, 0)

            def body(g, s, last=False):
                turn_x1(g)
                if not last:
                    turn_y(g + 1, 1 - s)
                multiply(g, s)
            with pe.Fori(0, NG // 2) as turn:
                body(turn * 2, 0)
                body(turn * 2 + 1, 1)
            body(NG - 1, 0, True)

        @block.scalar
        def _(act):
            lead(act, [row_ready], LEAD)
            act.wait_ge(inv_out, 16)
            inverse_back(act, range(1, H, 2))
            act.wait_ge(wt_turned, 1)
            nc.scalar.copy(w1gt[:], ps_x1t[:, 0:D]).then_inc(wt_copied, 1)
            act.wait_ge(scale_ready, 1)

            def batch_norm(g, s):
                act.wait_ge(y_ready, g - 1 + LEAD)
                nc.scalar.activation(hn[:, s], acc[:, 0, at(g, G)], ACT.Identity, bias=shift[:], scale=scale[:]).then_inc(hn_ready, 1)

            def layer_norm(g, s):
                act.wait_ge(ln_ready, g + 1)
                act.wait_ge(x1_turned, g + LEAD)
                for k in range(T):
                    last = nc.scalar.activation(x1[:, k], ps_y[:, k], ACT.Identity, bias=lsh[:, s, k:k + 1],
                                                scale=lsc[:, s, k:k + 1])
                last.then_inc(x1_ready, 1)

            def keep_x1t(g, s):
                act.wait_ge(x1_turned, g + 1 + LEAD)
                act.wait_ge(x1t_out[s], before(g, s, 16, 2) + DMA_LEAD)
                nc.scalar.copy(x1t[:, s], ps_x1t[:]).then_inc(x1t_ready, 1)

            def rows_out(g, s):
                act.wait_ge(multiplied, g + 1)
                act.wait_ge(row_out[s], before(g, s, 32, 2) + DMA_LEAD)
                nc.scalar.copy(xl[:, s], ps_xl[:, :, 0:ROW1])
                nc.scalar.copy(ad[:, s], ps_ad[0:1, :]).then_inc(row_ready, 1)

            nc.scalar.activation(hn[:, 0], acc[:, 0, 0:G], ACT.Identity, bias=shift[:], scale=scale[:]).then_inc(hn_ready, 1)
            batch_norm(1, 1)
            layer_norm(0, 0)

            def body(g, s, last=False, last_but_one=False):
                keep_x1t(g, s)
                if not (last or last_but_one):
                    batch_norm(g + 2, s)
                rows_out(g, s)
                if not last:
                    layer_norm(g + 1, 1 - s)
            with act.Fori(0, (NG - 3) // 2) as turn:
                body(turn * 2, 0)
                body(turn * 2 + 1, 1)
            body(NG - 3, 0)
            body(NG - 2, 1, last_but_one=True)
            body(NG - 1, 0, last=True)

        @block.vector
        def _(dve):
            lead(dve, [taken, y_ready, kept], LEAD)
            dve.wait_ge(den_in, 16)
            nc.vector.reciprocal(den[:], den[:]).then_inc(inverted, 1)
            for piece, (first, end) in enumerate(PIECES):
                dve.wait_ge(inv_in[piece], 16 * H)
                with dve.Fori(first, end) as g:
                    do = Steps(dve, h_step, g * 3).ordered
                    part = acc[:, 0, at(g, G)]
                    do(nc.vector.tensor_tensor(part, part, acc[:, 1, at(g, G)], ALU.mult))
                    do(nc.vector.tensor_tensor(part, part, acc[:, 2, at(g, G)], ALU.add))
                    do(nc.vector.bn_stats(stats[:, bass.ds(g, 1)].rearrange("p a s -> p (a s)"), acc[:, 0, at(g, SG)]))
            do = Steps(dve, h_step, NG * 3).ordered
            do(nc.vector.bn_aggr(mv[:], stats[:].rearrange("p g s -> p (g s)")))
            nc.vector.tensor_scalar(mv[:, 1:2], mv[:, 1:2], NORM_EPS, None, ALU.add).then_inc(bn_var, 1)
            dve.wait_ge(bn_dev, 1)
            batch_norm_scale(nc, do, mv[:], dev[:], scale[:], shift[:],
                             vec[:, GAMMA0:GAMMA0 + 1], vec[:, BETA0:BETA0 + 1]).then_inc(scale_ready, 1)
            dve.wait_ge(wa_made, 1)
            do(nc.vector.tensor_copy(wa[:], ps_ad[:, 0:2]))
            do(nc.vector.memset(waug[:], 0.0))
            do(nc.vector.tensor_copy(waug[:, 0:D], w[:, W1G]))
            do(nc.vector.tensor_copy(waug[:, D:D + 1], wa[:, 0:1]))
            do(nc.vector.tensor_tensor(wa_both[:], wa[:, 0:1].to_broadcast([P, P]), wa[:, 1:2].to_broadcast([P, P]), ALU.add))
            nc.vector.tensor_copy(logit[:, 0:1], wa[:, 0:1]).then_inc(wa_ready, 1)

            def add_x(g, s):
                dve.wait_ge(hn_ready, g + 1)
                nc.vector.tensor_tensor(y[:, s], hn[:, s], acc[:, 2, at(g, G)], ALU.add).then_inc(y_ready, 1)

            def node_moments(g):
                dve.wait_ge(y_turned, g + 1)
                moments(nc, Steps(dve, ln_step, g * 2).ordered, lambda: alone(dve, m["passed"]), ps_y, lst, lmv).then_inc(ln_var, 1)

            def statistics(g, s):
                dve.wait_ge(ln_dev, g + 1)
                nc.vector.tensor_copy(lsc[:, s], lrs[:])
                nc.vector.scalar_tensor_tensor(lsh[:, s], lmv[:, :, 0], -1.0, lrs[:], ALU.mult,
                                               ALU.mult).then_inc(ln_ready, 1)

            def take(g):
                dve.wait_ge(multiplied, g + 1)
                dve.wait_ge(hn_ready, g + 1)
                dve.wait_ge(kept, g + LEAD)
                nc.vector.tensor_copy(acc[:, 0, at(g, G)], ps_xlt[:]).then_inc(taken, 1)
                nc.vector.tensor_copy(logit[:], ps_logit[:]).then_inc(taken, 1)
                dve.wait_ge(taken, 2 * g + 2 + LEAD)
                nc.vector.scalar_tensor_tensor(acc[:, 2, at(g, G)], logit[:], SLOPE, logit[:], ALU.mult, ALU.max).then_inc(kept, 1)

            add_x(0, 0)
            add_x(1, 1)
            node_moments(0)
            statistics(0, 0)

            def body(g, s, last=False, last_but_one=False):
                if not (last or last_but_one):
                    add_x(g + 2, s)
                if not last:
                    node_moments(g + 1)
                take(g)
                if not last:
                    statistics(g + 1, 1 - s)
            with dve.Fori(0, (NG - 3) // 2) as turn:
                body(turn * 2, 0)
                body(turn * 2 + 1, 1)
            body(NG - 3, 0)
            body(NG - 2, 1, last_but_one=True)
            body(NG - 1, 0, last=True)
            dve.wait_ge(kept, NG + LEAD)


def edges1(nc, m, src):
    with ExitStack() as ctx:
        sem = lambda name: ctx.enter_context(nc.semaphore(name))
        sb = lambda name, shape, dt=F32: ctx.enter_context(nc.sbuf_tensor(name, shape, dt))
        ps = lambda name, shape: ctx.enter_context(nc.psum_tensor(name, shape, F32))
        src_in = [sem(f"src1_in{u}") for u in range(V)]
        ad_in = [sem(f"ad_in{u}") for u in range(V)]
        xl_in = [sem(f"xl_in{u}") for u in range(V)]
        summed_logit, leaky, off_ready, masked = sem("summed_logit"), sem("leaky"), sem("off_ready"), sem("masked")
        largest, turned, column = sem("largest"), sem("max_turned"), sem("max_column")
        spread, max_step, shifted = sem("max_spread"), sem("max_step"), sem("shifted")
        weighed, summed, rescaled, added, set_up = sem("weighed1"), sem("summed1"), sem("rescaled"), sem("added1"), sem("set_up")
        max_written, slots_summed = sem("max_written"), sem("slots_summed")
        idx = sb("idx1", [P, V, K], I32)
        adw = sb("adw", [P, V, W])
        xg = sb("xg", [P, V, K, ROW1])
        ones = sb("ones", [P, P])
        lg = sb("lg", [P, 4, K, W])
        off = sb("off", [P, K, W])
        top = sb("top", [P, 2, W])
        col = sb("col", [W, 2])
        newm = sb("newm", [P, 2, W])
        drop = sb("drop", [P, 2, W])
        fade = sb("fade", [P, 4, W])
        pw = sb("pw", [P, 2, K, W])
        pws = sb("pws", [P, 2, W])
        ps_top = ps("ps_top", [P, 2, G])
        ps_max = ps("ps_max", [P, 2, G])
        ps_sum = ps("ps_sum1", [P, 2, CE])
        src_c = src.rearrange("(c p k) -> c p k", p=P, k=K)
        block = ctx.enter_context(nc.Block())
        acc = m["acc"]

        @block.sync
        def _(sp):
            def load_src(c, u):
                sp.dma_start(idx[:, u], row(src_c, c)).then_inc(src_in[u], 16)

            def load_window(c, u):
                base = sp.value_load(m["base_row"][0:1, bass.ds(c, 1)], min_val=0, max_val=N - 1)
                sp.dma_start(adw[:, u], m["ad_row"][bass.ds(base, W)].partition_broadcast(P)).then_inc(ad_in[u], 16)

            for u in range(V):
                load_src(u, u)
            for u in range(V):
                load_window(u, u)

            def body(c, u, peeled):
                sp.wait_ge(largest, c + 1)
                load_window(c + V, u)
                sp.wait_ge(xl_in[u], landed(c, u, 16 * K, V))
                load_src(c + V, u)
            over_chunks(sp, body, NC - V, V)
            for finished in m["used"]:
                sp.sem_clear(finished)

        @block.gpsimd
        def _(pool):
            def gather(c, u):
                pool.wait_ge(src_in[u], landed(c, u, 16, V))
                alone(pool, m["passed"])
                for k in range(K):
                    nc.gpsimd.indirect_dma_start(
                        out=xg[:, u, k], out_offset=None, in_=m["xl_table"],
                        in_offset=bass.IndirectOffsetOnAxis(ap=idx[:, u, k:k + 1], axis=0)).then_inc(xl_in[u], 16)
            for u in range(V):
                gather(u, u)

            def body(c, u, peeled):
                pool.wait_ge(summed, c + 1 + LEAD)
                gather(c + V, u)
            over_chunks(pool, body, NC - V, V)

        @block.tensor
        def _(pe):
            lead(pe, [summed], LEAD)
            def turn_top(c, u):
                pe.wait_ge(largest, c + 1)
                alone(pe, m["passed"])
                nc.tensor.transpose(ps_top[0:W, u % 2, 0:P], top[:, u % 2], m["ident"][:]).then_inc(turned, 1)

            def spread_max(c, u):
                pe.wait_ge(column, c + 1)
                nc.tensor.matmul(ps_max[:, u % 2, 0:W], col[:, u % 2:u % 2 + 1].to_broadcast([W, P]),
                                 m["ident"][0:W, 0:W], start=True, stop=True).then_inc(spread, 1)

            def sum_up(c, u):
                b = u % 2
                pe.wait_ge(slots_summed, c + 1)
                for k in range(K):
                    nc.tensor.matmul(ps_sum[:, b, 0:W], xg[:, u, k, 0:D], pw[:, b, k], start=(k == 0), stop=(k == K - 1))
                nc.tensor.matmul(ps_sum[:, b, W:2 * W], ones[:], pws[:, b], start=True, stop=True).then_inc(summed, 1)

            for c in range(3):
                turn_top(c, c)
                spread_max(c, c)
            turn_top(3, 3)
            sum_up(0, 0)

            def body(c, u, peeled):
                if not (peeled and c + 3 >= NC):
                    spread_max(c + 3, (u + 3) % V)
                if not (peeled and c + 4 >= NC):
                    turn_top(c + 4, (u + 4) % V)
                if not (peeled and c + 1 >= NC):
                    sum_up(c + 1, (u + 1) % V)
            over_chunks(pe, body, NC, V)

        @block.scalar
        def _(act):
            lead(act, [weighed], LEAD)
            def weigh(c, u, first=False):
                b = u % 2
                base = act.value_load(m["base_row"][0:1, bass.ds(c, 1)], min_val=0, max_val=N - 1)
                act.wait_ge(shifted, c + 1)
                if not first:
                    act.wait_ge(summed, c - 1 + LEAD)
                nc.scalar.copy(acc[:, 2, bass.ds(base, W)], newm[:, b]).then_inc(max_written, 1)
                nc.scalar.activation(fade[:, u % 4], drop[:, b], ACT.Exp)
                nc.scalar.activation(pw[:, b], lg[:, u % 4], ACT.Exp).then_inc(weighed, 1)

            def logits(c, u, first=False):
                if not first:
                    act.wait_ge(weighed, c - 3 + LEAD)
                act.wait_ge(ad_in[u], landed(c, u, 16, V))
                act.wait_ge(xl_in[u], landed(c, u, 16 * K, V))
                for k in range(K):
                    last = nc.scalar.activation(lg[:, u % 4, k], adw[:, u], ACT.Identity, bias=xg[:, u, k, D:D + 1])
                last.then_inc(summed_logit, 1)

            for c in range(4):
                logits(c, c, True)
            weigh(0, 0, True)
            weigh(1, 1, True)
            logits(4, 4)

            def body(c, u, peeled):
                if not (peeled and c + 2 >= NC):
                    weigh(c + 2, (u + 2) % V)
                if not (peeled and c + 5 >= NC):
                    logits(c + 5, (u + 5) % V)
            over_chunks(act, body, NC, V)

        @block.vector
        def _(dve):
            nc.vector.memset(ones[:], 1.0).then_inc(set_up, 1)
            dve.wait_ge(set_up, 1)

            def find_off(c, u):
                t = lg[:, u % 4]
                dve.wait_ge(summed_logit, c + 1)
                nc.vector.scalar_tensor_tensor(t, t, SLOPE, t, ALU.mult, ALU.max).then_inc(leaky, 1)
                nc.vector.tensor_tensor(off[:], m["dst_local"][:, bass.ds(c, 1), :].rearrange("p a k -> p (a k)")
                                        .unsqueeze(2).to_broadcast([P, K, W]),
                                        m["iota"][:].unsqueeze(1).to_broadcast([P, K, W]),
                                        ALU.not_equal).then_inc(off_ready, 1)

            def mask(c, u):
                t = lg[:, u % 4]
                dve.wait_ge(off_ready, c + 1)
                dve.wait_ge(leaky, c + 1)
                nc.vector.scalar_tensor_tensor(t, off[:], MASKED, t, ALU.mult, ALU.add).then_inc(masked, 1)

            def find_top(c, u):
                dve.wait_ge(masked, c + 1)
                nc.vector.tensor_reduce(top[:, u % 2], lg[:, u % 4].rearrange("p k w -> p w k"), AX,
                                        ALU.max).then_inc(largest, 1)

            def max_column(c, u):
                b = u % 2
                dve.wait_ge(turned, c + 1)
                nc.vector.tensor_reduce(col[:, b:b + 1], ps_top[0:W, b, 0:P], AX, ALU.max).then_inc(column, 1)

            def new_max(c, u, first=False):
                b = u % 2
                base = dve.value_load(m["base_row"][0:1, bass.ds(c, 1)], min_val=0, max_val=N - 1)
                running = acc[:, 2, bass.ds(base, W)]
                if not first:
                    dve.wait_ge(max_written, c)
                dve.wait_ge(spread, c + 1)
                nc.vector.tensor_tensor(newm[:, b], running, ps_max[:, b, 0:W], ALU.max).then_inc(max_step, 1)
                return running

            def shift(c, u, running):
                b = u % 2
                dve.wait_ge(max_step, c + 1)
                nc.vector.tensor_tensor(drop[:, b], running, newm[:, b], ALU.subtract)
                nc.vector.tensor_tensor(lg[:, u % 4], lg[:, u % 4], newm[:, b].unsqueeze(1).to_broadcast([P, K, W]),
                                        ALU.subtract).then_inc(shifted, 1)

            def sum_slots(c, u):
                dve.wait_ge(weighed, c + 1 + LEAD)
                nc.vector.tensor_reduce(pws[:, u % 2], pw[:, u % 2].rearrange("p k w -> p w k"), AX,
                                        ALU.add).then_inc(slots_summed, 1)

            def rescale(c, u):
                base = dve.value_load(m["base_row"][0:1, bass.ds(c, 1)], min_val=0, max_val=N - 1)
                window = acc[:, 0:2, bass.ds(base, W)]
                dve.wait_ge(weighed, c + 1 + LEAD)
                nc.vector.tensor_tensor(window, window, fade[:, u % 4].unsqueeze(1).to_broadcast([P, 2, W]),
                                        ALU.mult).then_inc(rescaled, 1)
                return window

            def add_up(c, u, window):
                dve.wait_ge(rescaled, c + 1)
                dve.wait_ge(summed, c + 1 + LEAD)
                nc.vector.tensor_tensor(window, window, ps_sum[:, u % 2, 0:2 * W].rearrange("p (a w) -> p a w", w=W),
                                        ALU.add).then_inc(added, 1)

            for c in range(2):
                find_off(c, c)
                mask(c, c)
                find_top(c, c)
                max_column(c, c)
                shift(c, c, new_max(c, c, c == 0))
            for c in range(2, 4):
                find_off(c, c)
                mask(c, c)
                find_top(c, c)
                if c == 2:
                    max_column(c, c)
            sum_slots(0, 0)

            def body(c, u, peeled):
                done = lambda ahead: peeled and c + ahead >= NC
                if not done(3):
                    max_column(c + 3, (u + 3) % V)
                if not done(4):
                    find_off(c + 4, (u + 4) % V)
                if not done(2):
                    running = new_max(c + 2, (u + 2) % V)
                if not done(4):
                    mask(c + 4, (u + 4) % V)
                if not done(2):
                    shift(c + 2, (u + 2) % V, running)
                window = rescale(c, u)
                if not done(4):
                    find_top(c + 4, (u + 4) % V)
                add_up(c, u, window)
                if not done(1):
                    sum_slots(c + 1, (u + 1) % V)
                dve.wait_ge(added, c + 1)
            over_chunks(dve, body, NC, V)


def far_windows1(nc, m, src):
    with ExitStack() as ctx:
        sem = lambda name: ctx.enter_context(nc.semaphore(name))
        sb = lambda name, shape, dt=F32: ctx.enter_context(nc.sbuf_tensor(name, shape, dt))
        ps = lambda name, shape: ctx.enter_context(nc.psum_tensor(name, shape, F32))
        ones_set = sem("far1_ones_set")
        src_in, ad_in, xl_in = sem("far1_src_in"), sem("far1_ad_in"), sem("far1_xl_in")
        summed_logit, largest, turned = sem("far1_summed_logit"), sem("far1_largest"), sem("far1_turned")
        column, spread, shifted = sem("far1_column"), sem("far1_spread"), sem("far1_shifted")
        weighed, summed, added, step = sem("far1_weighed"), sem("far1_summed"), sem("far1_added"), sem("far1_step")
        idx = sb("far1_idx", [P, K], I32)
        adw = sb("far1_adw", [P, W])
        xg = sb("far1_xg", [P, K, ROW1])
        nodes = sb("far1_nodes", [P, W])
        ones = sb("far1_ones", [P, P])
        lg, off, pw = sb("far1_lg", [P, K, W]), sb("far1_off", [P, K, W]), sb("far1_pw", [P, K, W])
        top, newm, drop, fade = (sb(f"far1_{n}", [P, W]) for n in ("top", "newm", "drop", "fade"))
        col = sb("far1_col", [W, 1])
        ps_top, ps_max, ps_sum = ps("far1_ps_top", [P, G]), ps("far1_ps_max", [P, G]), ps("far1_ps_sum", [P, CE])
        src_c = src.rearrange("(c p k) -> c p k", p=P, k=K)
        acc = m["acc"]
        block = ctx.enter_context(nc.Block())

        @block.sync
        def _(sp):
            def body(c, j, visit):
                sp.dma_start(idx[:], row(src_c, c)).then_inc(src_in, 16)
                base = window_base(nc, sp, m, c, j)
                sp.dma_start(adw[:], m["ad_row"][bass.ds(base, W)].partition_broadcast(P)).then_inc(ad_in, 16)
                sp.wait_ge(added, visit)
            over_far_windows(sp, m, body)

        @block.gpsimd
        def _(pool):
            def body(c, j, visit):
                pool.wait_ge(src_in, visit * 16)
                alone(pool, m["passed"])
                for k in range(K):
                    nc.gpsimd.indirect_dma_start(
                        out=xg[:, k], out_offset=None, in_=m["xl_table"],
                        in_offset=bass.IndirectOffsetOnAxis(ap=idx[:, k:k + 1], axis=0)).then_inc(xl_in, 16)
            over_far_windows(pool, m, body)

        @block.tensor
        def _(pe):
            pe.wait_ge(ones_set, 1)
            def body(c, j, visit):
                pe.wait_ge(largest, visit)
                alone(pe, m["passed"])
                nc.tensor.transpose(ps_top[0:W, 0:P], top[:], m["ident"][:]).then_inc(turned, 1)
                pe.wait_ge(column, visit)
                nc.tensor.matmul(ps_max[:, 0:W], col[:].to_broadcast([W, P]), m["ident"][0:W, 0:W],
                                 start=True, stop=True).then_inc(spread, 1)
                pe.wait_ge(weighed, visit)
                for k in range(K):
                    nc.tensor.matmul(ps_sum[:, 0:W], xg[:, k, 0:D], pw[:, k], start=(k == 0), stop=(k == K - 1))
                for k in range(K):
                    mm = nc.tensor.matmul(ps_sum[:, W:2 * W], ones[:], pw[:, k], start=(k == 0), stop=(k == K - 1))
                mm.then_inc(summed, 1)
            over_far_windows(pe, m, body)

        @block.scalar
        def _(act):
            def body(c, j, visit):
                act.wait_ge(ad_in, visit * 16)
                act.wait_ge(xl_in, visit * (16 * K))
                for k in range(K):
                    last = nc.scalar.activation(lg[:, k], adw[:], ACT.Identity, bias=xg[:, k, D:D + 1])
                last.then_inc(summed_logit, 1)
                base = window_base(nc, act, m, c, j)
                act.wait_ge(shifted, visit)
                nc.scalar.activation(fade[:], drop[:], ACT.Exp)
                nc.scalar.copy(acc[:, 2, bass.ds(base, W)], newm[:])
                nc.scalar.activation(pw[:], lg[:], ACT.Exp).then_inc(weighed, 1)
            over_far_windows(act, m, body)

        @block.vector
        def _(dve):
            nc.vector.memset(ones[:], 1.0).then_inc(ones_set, 1)
            dve.sem_inc(step, 6)
            def body(c, j, visit):
                do = Steps(dve, step, visit * 6).ordered
                do(nc.vector.tensor_tensor(nodes[:], m["iota"][:], m["shifts"][:, bass.ds(j, 1)].to_broadcast([P, W]),
                                           ALU.add))
                do(nc.vector.tensor_tensor(off[:], m["dst_local"][:, bass.ds(c, 1), :].rearrange("p a k -> p (a k)")
                                           .unsqueeze(2).to_broadcast([P, K, W]),
                                           nodes[:].unsqueeze(1).to_broadcast([P, K, W]), ALU.not_equal))
                dve.wait_ge(summed_logit, visit)
                do(nc.vector.scalar_tensor_tensor(lg[:], lg[:], SLOPE, lg[:], ALU.mult, ALU.max))
                do(nc.vector.scalar_tensor_tensor(lg[:], off[:], MASKED, lg[:], ALU.mult, ALU.add))
                nc.vector.tensor_reduce(top[:], lg[:].rearrange("p k w -> p w k"), AX, ALU.max).then_inc(largest, 1)
                dve.wait_ge(turned, visit)
                nc.vector.tensor_reduce(col[:], ps_top[0:W, 0:P], AX, ALU.max).then_inc(column, 1)
                base = window_base(nc, dve, m, c, j)
                running = acc[:, 2, bass.ds(base, W)]
                dve.wait_ge(spread, visit)
                do(nc.vector.tensor_tensor(newm[:], running, ps_max[:, 0:W], ALU.max))
                nc.vector.tensor_tensor(drop[:], running, newm[:], ALU.subtract)
                nc.vector.tensor_tensor(lg[:], lg[:], newm[:].unsqueeze(1).to_broadcast([P, K, W]),
                                        ALU.subtract).then_inc(shifted, 1)
                window = acc[:, 0:2, bass.ds(base, W)]
                dve.wait_ge(weighed, visit)
                do(nc.vector.tensor_tensor(window, window, fade[:].unsqueeze(1).to_broadcast([P, 2, W]), ALU.mult))
                dve.wait_ge(summed, visit)
                nc.vector.tensor_tensor(window, window, ps_sum[:, 0:2 * W].rearrange("p (a w) -> p a w", w=W),
                                        ALU.add).then_inc(added, 1)
                dve.wait_ge(added, visit)
            over_far_windows(dve, m, body)


def nodes1(nc, m, out):
    with ExitStack() as ctx:
        sem = lambda name: ctx.enter_context(nc.semaphore(name))
        sb = lambda name, shape, dt=F32: ctx.enter_context(nc.sbuf_tensor(name, shape, dt))
        ps = lambda name, shape: ctx.enter_context(nc.psum_tensor(name, shape, F32))
        acc, vec, w = m["acc"], m["vec"], m["w"]
        den_out, den_in, inv_out, inv_in = sem("den1_out"), sem("den1_in"), sem("inv1_out"), sem("inv1_in")
        den_step, inverted, divided, o_ready = sem("den_step"), sem("inverted1"), sem("divided1"), sem("o_ready")
        lin = [sem("lin0"), sem("lin1")]
        lin_out = [sem("lin_out0"), sem("lin_out1")]
        relu_ready = sem("relu_ready")
        stat = [sem("stat0"), sem("stat1")]
        scaled = [sem("scaled0"), sem("scaled1")]
        bn_step = sem("bn_step")
        bn_var, bn_dev, ln_var, ln_dev = sem("bn_var1"), sem("bn_dev1"), sem("ln_var1"), sem("ln_dev1")
        x1_in = [sem(f"x1_in{s}") for s in range(2)]
        out_stored = [sem(f"out_stored{s}") for s in range(2)]
        h_ready, y_ready, y_turned = sem("h_ready1"), sem("y_ready1"), sem("y_turned1")
        ln_step, ln_ready, normed = sem("ln_step1"), sem("ln_ready1"), sem("normed1")
        o = sb("o", [P, 2, SG])
        r = sb("r", [P, 2, G])
        x1t = sb("x1t_b", [P, 2, G])
        y = sb("y_b", [P, 2, G])
        xo = sb("xo", [P, 2, T, D])
        stats = sb("bn_slices1", [P, NG, 6])
        mv = sb("mv1", [P, 2, 2])
        scale, shift, dev = sb("scale1", [P, 2]), sb("shift1", [P, 2]), sb("dev1", [P, 2])
        den = sb("den1", [P, NP // P])
        quot = sb("quot", [P, 2, SG])
        lst, lmv = sb("lst1", [P, T, 6]), sb("lmv1", [P, T, 2])
        lsc, lsh, lrs = sb("lsc1", [P, 2, T]), sb("lsh1", [P, 2, T]), sb("lrs1", [P, T])
        ps_lin = ps("ps_lin", [P, 2, 512])
        ps_y = ps("ps_y1", [P, 2, T, D])
        out_g = out.rearrange("(g k p) d -> g p k d", k=T, p=P)
        block = ctx.enter_context(nc.Block())

        @block.sync
        def _(sp):
            lead(sp, [*out_stored], DMA_LEAD)
            sp.dma_start(m["den_row1"].unsqueeze(0), acc[0:1, 1, :]).then_inc(den_out, 16)
            sp.wait_ge(den_out, 16)
            sp.dma_start(den[:], m["den_row1"].rearrange("(p n) -> p n", p=P)).then_inc(den_in, 16)
            sp.wait_ge(inverted, 1)
            sp.dma_start(m["inv_row1"].rearrange("(p n) -> p n", p=P), den[:]).then_inc(inv_out, 16)
            sp.wait_ge(inv_out, 16)
            sp.dma_start(acc[:, 1, :], m["inv_row1"].partition_broadcast(P)).then_inc(inv_in, 16)

            def load(g, s):
                sp.dma_start(x1t[:, s], m["x1t_table"][:, at(g, G)]).then_inc(x1_in[s], 16)
            load(0, 0)
            load(1, 1)

            def body(g, s, ahead=True):
                if ahead:
                    sp.wait_ge(y_ready, g + 1 + LEAD)
                    load(g + 2, s)
                sp.wait_ge(normed, g + 1 + LEAD)
                sp.dma_start(row(out_g, g), xo[:, s]).then_inc(out_stored[s], 16)
            with sp.Fori(0, (NG - 3) // 2) as turn:
                body(turn * 2, 0)
                body(turn * 2 + 1, 1)
            for g in range(NG - 3, NG):
                body(g, g % 2, g + 2 < NG)
            for s in range(2):
                sp.wait_ge(out_stored[s], 16 * ((NG + 1 - s) // 2) + DMA_LEAD)

        @block.gpsimd
        def _(pool):
            for layer in range(2):
                pool.wait_ge(bn_var, layer + 1)
                one_over_deviation(nc, dev[:, layer:layer + 1], mv[:, layer, 1:2], m["power"][:, 0:1]).then_inc(bn_dev, 1)
            with pool.Fori(0, NG) as g:
                pool.wait_ge(ln_var, g + 1)
                one_over_deviation(nc, lrs[:], lmv[:, :, 1], m["power"][:]).then_inc(ln_dev, 1)

        @block.tensor
        def _(pe):
            lead(pe, [*lin, y_turned], LEAD)
            def linear(layer):
                def body(g, s):
                    pe.wait_ge(*((o_ready, g + 1 + LEAD) if layer == 0 else (relu_ready, g + 1)))
                    pe.wait_ge(lin_out[layer], g + LEAD)
                    nc.tensor.matmul(ps_lin[:, s, 0:SG], w[:, WM1 + layer], (o if layer == 0 else r)[:, s, 0:SG],
                                     start=True, stop=True).then_inc(lin[layer], 1)
                over_groups(pe, body)
            linear(0)
            linear(1)

            def body(g, s):
                pe.wait_ge(y_ready, g + 1 + LEAD)
                pe.wait_ge(normed, g + LEAD)
                for k in range(T):
                    mm = nc.tensor.transpose(ps_y[:, s, k], y[:, s, at(k, P)], m["ident"][:])
                mm.then_inc(y_turned, 1)
            over_groups(pe, body)

        @block.scalar
        def _(act):
            lead(act, [*lin_out, normed, o_ready], LEAD)
            def bias_out(layer, g, s):
                act.wait_ge(lin[layer], g + 1 + LEAD)
                nc.scalar.activation(acc[:, layer, at(g, SG)], ps_lin[:, s, 0:SG], ACT.Identity,
                                     bias=vec[:, B1 + 3 * layer:B1 + 3 * layer + 1]).then_inc(lin_out[layer], 1)

            def with_bias(g, s):
                act.wait_ge(divided, g + 1)
                act.wait_ge(lin[0], g - 1 + LEAD)
                nc.scalar.activation(o[:, s], quot[:, s], ACT.Identity, bias=vec[:, BGAT:BGAT + 1]).then_inc(o_ready, 1)

            act.wait_ge(divided, 1)
            nc.scalar.activation(o[:, 0], quot[:, 0], ACT.Identity, bias=vec[:, BGAT:BGAT + 1]).then_inc(o_ready, 1)

            def first(g, s):
                with_bias(g + 1, 1 - s)
                bias_out(0, g, s)
            with act.Fori(0, NG // 2) as turn:
                first(turn * 2, 0)
                first(turn * 2 + 1, 1)
            bias_out(0, NG - 1, 0)
            act.wait_ge(scaled[0], 1)

            def hidden(g, s):
                act.wait_ge(lin[1], g + LEAD)
                nc.scalar.activation(r[:, s, 0:SG], acc[:, 0, at(g, SG)], ACT.Relu, bias=shift[:, 0:1],
                                     scale=scale[:, 0:1]).then_inc(relu_ready, 1)
                bias_out(1, g, s)
            over_groups(act, hidden)
            act.wait_ge(scaled[1], 1)

            def last_relu(g, s):
                act.wait_ge(y_ready, g + LEAD)
                nc.scalar.activation(r[:, s], acc[:, 1, at(g, G)], ACT.Relu, bias=shift[:, 1:2],
                                     scale=scale[:, 1:2]).then_inc(h_ready, 1)

            def normalise(g, s):
                act.wait_ge(ln_ready, g + 1)
                act.wait_ge(out_stored[s], before(g, s, 16, 2) + DMA_LEAD)
                for k in range(T):
                    last = nc.scalar.activation(xo[:, s, k], ps_y[:, s, k], ACT.Identity, bias=lsh[:, s, k:k + 1],
                                                scale=lsc[:, s, k:k + 1])
                last.then_inc(normed, 1)

            last_relu(0, 0)

            def body(g, s):
                last_relu(g + 1, 1 - s)
                normalise(g, s)
            with act.Fori(0, NG // 2) as turn:
                body(turn * 2, 0)
                body(turn * 2 + 1, 1)
            normalise(NG - 1, 0)

        @block.vector
        def _(dve):
            lead(dve, [y_ready], LEAD)
            dve.wait_ge(den_in, 16)
            nc.vector.tensor_scalar(den[:], den[:], SM_EPS, None, ALU.add).then_inc(den_step, 1)
            dve.wait_ge(den_step, 1)
            nc.vector.reciprocal(den[:], den[:]).then_inc(inverted, 1)
            dve.wait_ge(inv_in, 16)

            def divide(g, s):
                nc.vector.tensor_tensor(quot[:, s], acc[:, 0, at(g, SG)], acc[:, 1, at(g, SG)],
                                        ALU.mult).then_inc(divided, 1)

            def slice_stats(layer, g):
                dve.wait_ge(lin_out[layer], g + 1 + LEAD)
                nc.vector.bn_stats(stats[:, bass.ds(g, 1)].rearrange("p a s -> p (a s)"),
                                   acc[:, layer, at(g, SG)]).then_inc(stat[layer], 1)

            def scales(layer):
                dve.wait_ge(stat[layer], NG)
                do = Steps(dve, bn_step, 3 * layer).ordered
                do(nc.vector.bn_aggr(mv[:, layer], stats[:].rearrange("p g s -> p (g s)")))
                nc.vector.tensor_scalar(mv[:, layer, 1:2], mv[:, layer, 1:2], NORM_EPS, None, ALU.add).then_inc(bn_var, 1)
                dve.wait_ge(bn_dev, layer + 1)
                batch_norm_scale(nc, do,
                                 mv[:, layer], dev[:, layer:layer + 1], scale[:, layer:layer + 1], shift[:, layer:layer + 1],
                                 vec[:, G1 + 3 * layer:G1 + 3 * layer + 1],
                                 vec[:, BE1 + 3 * layer:BE1 + 3 * layer + 1]).then_inc(scaled[layer], 1)

            divide(0, 0)
            divide(1, 1)

            def first(g, s, last=False):
                if not last:
                    dve.wait_ge(o_ready, g + 1 + LEAD)
                    divide(g + 2, s)
                slice_stats(0, g)
            with dve.Fori(0, (NG - 3) // 2) as turn:
                first(turn * 2, 0)
                first(turn * 2 + 1, 1)
            first(NG - 3, 0)
            first(NG - 2, 1, True)
            first(NG - 1, 0, True)
            scales(0)
            over_groups(dve, lambda g, s: slice_stats(1, g))
            scales(1)

            def body(g, s):
                dve.wait_ge(h_ready, g + 1)
                dve.wait_ge(x1_in[s], landed(g, s, 16, 2))
                dve.wait_ge(y_turned, g + LEAD)
                nc.vector.scalar_tensor_tensor(y[:, s], x1t[:, s], 2.0, r[:, s], ALU.mult, ALU.add).then_inc(y_ready, 1)
                dve.wait_ge(y_turned, g + 1 + LEAD)
                do = Steps(dve, ln_step, g * 2).ordered
                moments(nc, do, lambda: alone(dve, m["passed"]), ps_y[:, s], lst, lmv).then_inc(ln_var, 1)
                dve.wait_ge(ln_dev, g + 1)
                nc.vector.tensor_copy(lsc[:, s], lrs[:])
                nc.vector.scalar_tensor_tensor(lsh[:, s], lmv[:, :, 0], -1.0, lrs[:], ALU.mult,
                                               ALU.mult).then_inc(ln_ready, 1)
            over_groups(dve, body)


_WEIGHTS = ["L0_gnn_WQ", "L0_gnn_WK", "L0_gnn_WV", "L0_gnn_WE", "L1_gnn_W", "L1_gnn_W1", "L1_gnn_W2"]
_VECTORS = ["L0_gnn_bn_gamma", "L0_gnn_bn_beta", "L1_gnn_att_src", "L1_gnn_att_dst", "L1_gnn_bias_gat", "L1_gnn_b1",
            "L1_gnn_g1", "L1_gnn_be1", "L1_gnn_b2", "L1_gnn_g2", "L1_gnn_be2"]


def kernel(**inputs):
    import numpy as np
    import concourse.bacc as bacc
    from concourse.bass_utils import run_bass_kernel_spmd

    src = np.asarray(inputs["src"])
    dst = np.pad(np.asarray(inputs["dst"]), (0, NC * CE - E), constant_values=-1)
    arrays = {
        "x": np.pad(np.asarray(inputs["x"]), ((0, NP - N), (0, 0))),
        "src": np.pad(src, (0, NC * CE - E)),
        "dst_rows": dst.reshape(NC, CE),
        "dst_cols": np.ascontiguousarray(dst.reshape(NC, P, K).transpose(1, 0, 2)),
        "edges": np.ascontiguousarray(inputs["edge_attr_128"]),
        "weights": np.ascontiguousarray(np.stack([np.asarray(inputs[n]) for n in _WEIGHTS], axis=1)),
        "vectors": np.ascontiguousarray(np.stack([np.asarray(inputs[n]) for n in _VECTORS], axis=1)),
    }
    nc = bacc.Bacc("TRN2", target_bir_lowering=False, num_devices=1)
    args = [nc.dram_tensor(f"in_{n}", a.shape, mybir.dt.from_np(a.dtype), kind="ExternalInput").ap()
            for n, a in arrays.items()]
    out = nc.dram_tensor("out", (NP, D), F32, kind="ExternalOutput").ap()
    build(nc, *args, out)
    result = run_bass_kernel_spmd(nc, [{f"in_{n}": a for n, a in arrays.items()}], core_ids=[0])
    return result.results[0]["out"][:N]
```

```python
from contextlib import ExitStack

import concourse.bass as bass
from concourse import mybir

F32 = mybir.dt.float32
I32 = mybir.dt.int32
ALU = mybir.AluOpType
ACT = mybir.ActivationFunctionType
AX = mybir.AxisListType.X

P = 128
D = 128
H = 8
DH = D // H
N = 12500
E = 212500
G = 512
NG = -(-N // G)
NP = NG * G
T = G // P
CE = 512
K = CE // P
U, V = 4, 8
NC = -(-(-(-E // CE)) // V) * V
CR = 104
CJ = NC // CR
W = 64
SG = N // NG
ROW1 = 132
LAST = E - (NC - 1) * CE
FAR_ROW = 32
SHIFTS = N // W + 1
FAR = 1.0e6
MASKED = -1.0e30
NORM_EPS = 1e-5
PIECES = ((0, 3), (3, 12), (12, NG))
LEAD = 2
DMA_LEAD = 16
ATTN_EPS = 1e-6
SM_EPS = 1e-16
SLOPE = 0.2
CLIP = 5.0
assert V % U == 0 and NG * SG == N and (NG - 5) % 4 == 0 and CR * CJ == NC and LAST % K == 0 and NG % 2 == 1

WQ, WK, WV, WE, W1G, WM1, WM2 = range(7)
(GAMMA0, BETA0, ASRC, ADST, BGAT, B1, G1, BE1, B2, G2, BE2) = range(11)


class Steps:

    def __init__(self, eng, sem, start=0):
        self.eng, self.sem, self.start, self.n = eng, sem, start, 0

    def ordered(self, ins):
        self.n += 1
        ins.then_inc(self.sem, 1)
        self.eng.wait_ge(self.sem, self.start + self.n)


def alone(eng, passed):
    eng.sem_inc(passed, 1)


def lead(eng, sems, by):
    for sem in sems:
        eng.sem_inc(sem, by)


def counted(nc, ctx, m, name):
    m["used"].append(ctx.enter_context(nc.semaphore(name)))
    return m["used"][-1]


def over_groups(eng, body):
    with eng.Fori(0, NG // 2) as turn:
        body(turn * 2, 0)
        body(turn * 2 + 1, 1)
    body(NG - 1, 0)


def over_groups_ahead(eng, body, slots=2):
    with eng.Fori(0, (NG - 5) // slots) as turn:
        for s in range(slots):
            body(turn * slots + s, s)
    for g in range(NG - 5, NG):
        body(g, g % slots)


def exists(g):
    return not isinstance(g, int) or g < NG


def over_chunks(eng, body, last, slots):
    with eng.Fori(0, last // slots - 1) as turn:
        for u in range(slots):
            body(turn * slots + u, u, False)
    for u in range(slots):
        body(last - slots + u, u, True)


def over_far_windows(eng, m, body):
    most = eng.value_load(m["base_row"][FAR_ROW:FAR_ROW + 1, NC:NC + 1], min_val=0, max_val=N - 1)
    with eng.If(most >= W):
        with eng.register() as visit:
            eng.reg_mov(visit, 0)
            def windows(c):
                reach = eng.value_load(m["base_row"][FAR_ROW:FAR_ROW + 1, bass.ds(c, 1)], min_val=0, max_val=N - 1)
                with eng.If(reach >= W):
                    with eng.Fori(1, reach // W + 1) as j:
                        eng.reg_add(visit, visit, 1)
                        body(c, j, eng.snap(visit, min_val=1, max_val=NC * SHIFTS))

            with eng.Fori(0, NC - 1) as c:
                windows(c)
            windows(NC - 1)


def window_base(nc, eng, m, c, j):
    base = eng.value_load(m["base_row"][0:1, bass.ds(c, 1)], min_val=0, max_val=N - 1)
    return nc.s_assert_within(base + j * W, 0, N - 1, skip_runtime_bounds_check_because="j*64 is at most the chunk's "
                              "largest destination less base[c]")


def at(i, n):
    return bass.ds(i * n, n)


def row(ap, i):
    entry = ap[bass.ds(i, 1)]
    return entry.rearrange("a p k d -> p (a k) d") if len(ap.shape) == 4 else entry.rearrange("a p k -> p (a k)")


def before(i, slot, each, slots):
    return (i - slot) * (each // slots)


def landed(i, slot, each, slots):
    return before(i, slot, each, slots) + each


def build(nc, x, src, dst_rows, dst_cols, edges, weights, vectors, out):
    with ExitStack() as ctx:
        def sb(name, shape, dt=F32):
            return ctx.enter_context(nc.sbuf_tensor(name, shape, dt))

        def dram(name, shape, dt=F32):
            return nc.dram_tensor(name, shape, dt, kind="Internal").ap()

        m = {}
        m["q_table"] = dram("q_table", [NP, D])
        m["kv_table"] = dram("kv_table", [NP, 2 * D])
        m["xl_table"] = dram("xl_table", [NP, ROW1])
        m["ad_row"] = dram("ad_row", [NP])
        m["x1t_table"] = dram("x1t_table", [P, NP])
        m["den_rows"] = dram("den_rows", [H, NP])
        m["inv_rows"] = dram("inv_rows", [H, NP])
        m["den_row1"] = dram("den_row1", [NP])
        m["inv_row1"] = dram("inv_row1", [NP])
        m["base_table"] = dram("base_table", [NC], I32)
        m["far_table"] = dram("far_table", [NC], I32)
        m["acc"] = sb("acc", [P, 3, NP])
        m["dst_local"] = sb("dst_local", [P, NC, K])
        m["base_row"] = sb("base_row", [P, NC + 1], I32)
        m["w"] = sb("w", [P, 7, D])
        m["vec"] = sb("vec", [P, 11])
        m["ident"] = sb("ident", [P, P])
        m["iota"] = sb("iota", [P, W])
        m["shifts"] = sb("shifts", [P, SHIFTS])
        m["used"] = []
        m["passed"] = ctx.enter_context(nc.semaphore("passed"))
        m["power"] = sb("power", [P, T])
        prologue(nc, m, dst_rows, dst_cols, weights, vectors)
        project(nc, m, x)
        edges0(nc, m, src, edges)
        far_windows0(nc, m, src, edges)
        nodes0(nc, m)
        edges1(nc, m, src)
        far_windows1(nc, m, src)
        nodes1(nc, m, out)


def prologue(nc, m, dst_rows, dst_cols, weights, vectors):
    with ExitStack() as ctx:
        sem = lambda name: counted(nc, ctx, m, name)
        sb = lambda name, shape, dt=F32: ctx.enter_context(nc.sbuf_tensor(name, shape, dt))
        weights_in, rows_in, cols_in = sem("weights_in"), sem("rows_in"), sem("cols_in")
        base_ready, base_stored, base_back = sem("base_ready"), sem("base_stored"), sem("base_back")
        ident_zero, made, step = sem("ident_zero"), sem("made"), sem("pro_step")
        rows = m["acc"][0:CR, 0, 0:CJ * CE].rearrange("p (j e) -> p j e", e=CE)
        low = m["acc"][0:CR, 1, 0:CJ * CE].rearrange("p (j e) -> p j e", e=CE)
        rows_i = m["acc"][0:CR, 2, 0:CJ * CE].bitcast(I32).rearrange("p (j e) -> p j e", e=CE)
        cols_i = m["acc"][:, 0, CJ * CE:CJ * CE + NC * K].bitcast(I32).rearrange("p (c k) -> p c k", k=K)
        base_f = sb("base_f", [P, CJ])
        base_i = sb("base_i", [P, CJ], I32)
        far_f = sb("far_f", [P, CJ])
        far_i = sb("far_i", [P, CJ], I32)
        base_all_i = sb("base_all_i", [P, NC], I32)
        base_all = sb("base_all", [P, NC])
        far_row = sb("far_row", [P, NC + 1])
        block = ctx.enter_context(nc.Block())

        @block.sync
        def _(sp):
            sp.dma_start(rows_i, dst_rows.rearrange("(p j) e -> p j e", j=CJ)).then_inc(rows_in, 16)
            sp.dma_start(cols_i, dst_cols).then_inc(cols_in, 16)
            sp.wait_ge(base_ready, 1)
            sp.dma_start(m["base_table"].rearrange("(p j) -> p j", j=CJ), base_i[0:CR, :]).then_inc(base_stored, 16)
            sp.dma_start(m["far_table"].rearrange("(p j) -> p j", j=CJ), far_i[0:CR, :]).then_inc(base_stored, 16)
            sp.wait_ge(base_stored, 32)
            sp.dma_start(m["base_row"][0:1, 0:NC], m["base_table"].unsqueeze(0)).then_inc(base_back, 16)
            sp.dma_start(m["base_row"][FAR_ROW:FAR_ROW + 1, 0:NC], m["far_table"].unsqueeze(0)).then_inc(base_back, 16)
            sp.dma_start(base_all_i[:], m["base_table"].partition_broadcast(P)).then_inc(base_back, 16)
            sp.wait_ge(base_back, 48)

        @block.scalar
        def _(act):
            act.dma_start(m["w"][:], weights).then_inc(weights_in, 16)
            act.dma_start(m["vec"][:], vectors).then_inc(weights_in, 16)
            act.wait_ge(weights_in, 32)

        @block.gpsimd
        def _(pool):
            nc.gpsimd.memset(m["ident"][:], 0.0).then_inc(ident_zero, 1)
            pool.wait_ge(ident_zero, 1)
            nc.gpsimd.affine_select(out=m["ident"][:], in_=m["ident"][:], compare_op=ALU.not_equal, fill=1.0,
                                    base=0, pattern=[[-1, P]], channel_multiplier=1).then_inc(made, 1)
            nc.gpsimd.iota(m["iota"][:], pattern=[[1, W]], base=0, channel_multiplier=0,
                           allow_small_or_imprecise_dtypes=True).then_inc(made, 1)
            nc.gpsimd.iota(m["shifts"][:], pattern=[[W, SHIFTS]], base=0, channel_multiplier=0,
                           allow_small_or_imprecise_dtypes=True).then_inc(made, 1)
            nc.gpsimd.memset(m["power"][:], -0.5).then_inc(made, 1)
            pool.wait_ge(made, 4)

        @block.vector
        def _(dve):
            do = Steps(dve, step).ordered
            dve.wait_ge(rows_in, 16)
            do(nc.vector.tensor_copy(rows, rows_i))
            do(nc.vector.tensor_scalar(low, rows, 0.0, FAR, ALU.is_lt, ALU.mult))
            do(nc.vector.tensor_tensor(low, low, rows, ALU.add))
            do(nc.vector.tensor_reduce(base_f[0:CR, :], low, AX, ALU.min))
            do(nc.vector.tensor_reduce(far_f[0:CR, :], rows, AX, ALU.max))
            do(nc.vector.tensor_copy(base_i[0:CR, :], base_f[0:CR, :]))
            do(nc.vector.tensor_tensor(far_f[0:CR, :], far_f[0:CR, :], base_f[0:CR, :], ALU.subtract))
            nc.vector.tensor_copy(far_i[0:CR, :], far_f[0:CR, :]).then_inc(base_ready, 1)
            dve.wait_ge(cols_in, 16)
            do(nc.vector.tensor_copy(m["dst_local"][:], cols_i))
            dve.wait_ge(base_back, 48)
            do(nc.vector.tensor_copy(base_all[:], base_all_i[:]))
            do(nc.vector.tensor_tensor(m["dst_local"][:], m["dst_local"][:],
                                       base_all[:].unsqueeze(2).to_broadcast([P, NC, K]), ALU.subtract))
            reach = far_row[FAR_ROW:FAR_ROW + 1]
            do(nc.vector.tensor_copy(reach[:, 0:NC], m["base_row"][FAR_ROW:FAR_ROW + 1, 0:NC]))
            do(nc.vector.tensor_reduce(reach[:, NC:NC + 1], reach[:, 0:NC], AX, ALU.max))
            do(nc.vector.tensor_copy(m["base_row"][FAR_ROW:FAR_ROW + 1, NC:NC + 1], reach[:, NC:NC + 1]))


def project(nc, m, x):
    with ExitStack() as ctx:
        sem = lambda name: counted(nc, ctx, m, name)
        sb = lambda name, shape, dt=F32: ctx.enter_context(nc.sbuf_tensor(name, shape, dt))
        ps = lambda name, shape: ctx.enter_context(nc.psum_tensor(name, shape, F32))
        x_in = [sem(f"x_in{s}") for s in range(4)]
        stored = [sem(f"qkv_stored{s}") for s in range(2)]
        turned, copied, kept = sem("x_turned"), sem("xt_copied"), sem("xt_kept")
        projected, q_out, kv_out = sem("projected"), sem("q_out"), sem("kv_out")
        xn = sb("xn", [P, 4, T, D])
        xt = sb("xt", [P, 2, G])
        q = sb("q", [P, 2, T, D])
        kv = sb("kv", [P, 2, T, 2 * D])
        ps_xt = ps("ps_xt", [P, 2, G])
        ps_qkv = ps("ps_qkv", [P, T, G])
        xg = x.rearrange("(g k p) d -> g p k d", k=T, p=P)
        qg = m["q_table"].rearrange("(g k p) d -> g p k d", k=T, p=P)
        kvg = m["kv_table"].rearrange("(g k p) d -> g p k d", k=T, p=P)
        wqkv = m["w"][:, WQ:WV + 1, :].rearrange("p a d -> p (a d)")
        block = ctx.enter_context(nc.Block())

        @block.sync
        def _(sp):
            lead(sp, [*stored], DMA_LEAD)
            for s in range(4):
                sp.dma_start(xn[:, s], xg[s]).then_inc(x_in[s], 16)

            def body(g, s):
                if exists(g + 4):
                    sp.wait_ge(turned, g + 1)
                    sp.dma_start(xn[:, s], row(xg, g + 4)).then_inc(x_in[s], 16)
                sp.wait_ge(q_out, g * 2 + 2 + LEAD)
                sp.dma_start(row(qg, g), q[:, s % 2]).then_inc(stored[s % 2], 16)
                sp.wait_ge(kv_out, g * 2 + 2 + LEAD)
                sp.dma_start(row(kvg, g), kv[:, s % 2]).then_inc(stored[s % 2], 16)
            over_groups_ahead(sp, body, 4)
            sp.wait_ge(stored[0], 32 * (NG // 2 + 1) + DMA_LEAD)
            sp.wait_ge(stored[1], 32 * (NG // 2) + DMA_LEAD)

        @block.tensor
        def _(pe):
            lead(pe, [projected], LEAD)
            def turn_x(g, s):
                pe.wait_ge(x_in[s], landed(g, s, 16, 4))
                if not (isinstance(g, int) and g < 2):
                    pe.wait_ge(kept, g - 1 + LEAD)
                for k in range(T):
                    mm = nc.tensor.transpose(ps_xt[:, s % 2, at(k, P)], xn[:, s, k], m["ident"][:])
                mm.then_inc(turned, 1)

            turn_x(0, 0)

            def body(g, s):
                if exists(g + 1):
                    turn_x(g + 1, (s + 1) % 4)
                pe.wait_ge(copied, g + 1)
                for half in range(2):
                    pe.wait_ge(kv_out, g * 2 + half + LEAD - 1)
                    pe.wait_ge(q_out, g * 2 + half + LEAD - 1)
                    for k in (2 * half, 2 * half + 1):
                        mm = nc.tensor.matmul(ps_qkv[:, k, 0:3 * D], xt[:, s % 2, at(k, P)], wqkv, start=True, stop=True)
                    mm.then_inc(projected, 1)
            over_groups_ahead(pe, body, 4)

        @block.scalar
        def _(act):
            lead(act, [q_out], LEAD)
            def copy_x(g, s):
                act.wait_ge(turned, g + 1)
                if not (isinstance(g, int) and g < 2):
                    act.wait_ge(projected, g * 2 - 2 + LEAD)
                nc.scalar.activation(xt[:, s], ps_xt[:, s], ACT.Identity).then_inc(copied, 1)

            copy_x(0, 0)

            def body(g, s):
                if exists(g + 1):
                    copy_x(g + 1, 1 - s)
                act.wait_ge(stored[s], before(g, s, 32, 2) + DMA_LEAD)
                for half in range(2):
                    tiles = slice(2 * half, 2 * half + 2)
                    act.wait_ge(projected, g * 2 + half + 1 + LEAD)
                    nc.scalar.activation(q[:, s, tiles], ps_qkv[:, tiles, 0:D], ACT.Identity,
                                         scale=DH ** -0.5).then_inc(q_out, 1)
            over_groups_ahead(act, body)

        @block.vector
        def _(dve):
            lead(dve, [kept, kv_out], LEAD)
            def body(g, s):
                dve.wait_ge(copied, g + 1)
                nc.vector.tensor_copy(m["acc"][:, 2, at(g, G)], ps_xt[:, s]).then_inc(kept, 1)
                dve.wait_ge(stored[s], before(g, s, 32, 2) + DMA_LEAD)
                for half in range(2):
                    tiles = slice(2 * half, 2 * half + 2)
                    dve.wait_ge(q_out, g * 2 + half + 1 + LEAD)
                    nc.vector.tensor_copy(kv[:, s, tiles], ps_qkv[:, tiles, D:3 * D]).then_inc(kv_out, 1)
            over_groups(dve, body)


def edges0(nc, m, src, edges):
    with ExitStack() as ctx:
        sem = lambda name: counted(nc, ctx, m, name)
        sb = lambda name, shape, dt=F32: ctx.enter_context(nc.sbuf_tensor(name, shape, dt))
        ps = lambda name, shape: ctx.enter_context(nc.psum_tensor(name, shape, F32))
        src_in = [sem(f"src_in{u}") for u in range(U)]
        edge_in = [sem(f"edge_in{u}") for u in range(U)]
        kv_in = [sem(f"kv_in{u}") for u in range(U)]
        hot_ready, turned, copied = sem("hot_ready"), sem("edges_turned"), sem("edges_copied")
        spread, gated, scored = sem("spread"), sem("gated"), sem("scored")
        weighed, valued, summed, added = sem("weighed"), sem("valued"), sem("summed"), sem("added")
        mult, clear = sem("mult"), sem("cleared")
        idx = sb("idx", [P, U, K], I32)
        ea = sb("ea", [P, U, K, D])
        qw = sb("qw", [W, U, D])
        kv = sb("kv_g", [P, U, K, 2 * D])
        hot = sb("hot", [P, U, K, W])
        eat = sb("eat", [P, 2, CE])
        hott = sb("hott", [W, 2, CE])
        prod = sb("prod", [P, CE])
        score = sb("score", [P, 2, K * H])
        pex = sb("pex", [P, 2, K, D])
        ps_eat = ps("ps_eat", [P, CE])
        ps_hott = ps("ps_hott", [P, CE])
        ps_eh = ps("ps_eh", [P, 2, K, D])
        ps_q = ps("ps_q", [P, 2, K, D])
        ps_sum = ps("ps_sum", [P, 2, CE])
        src_c = src.rearrange("(c p k) -> c p k", p=P, k=K)
        ea_c = edges[0:(NC - 1) * CE].rearrange("(c p k) d -> c p (k d)", p=P, k=K)
        ea_last = edges[(NC - 1) * CE:E].rearrange("(p k) d -> p (k d)", k=K)
        block = ctx.enter_context(nc.Block())
        acc = m["acc"]

        @block.sync
        def _(sp):
            def load_src(c, u):
                sp.dma_start(idx[:, u], row(src_c, c)).then_inc(src_in[u], 16)

            def load_edges(c, u, last=False):
                if last:
                    sp.dma_start(ea[0:LAST // K, u].rearrange("p k d -> p (k d)"), ea_last).then_inc(edge_in[u], 16)
                else:
                    sp.dma_start(ea[:, u].rearrange("p k d -> p (k d)"),
                                 row(ea_c, c)).then_inc(edge_in[u], 16)

            def load_window(c, u):
                base = sp.value_load(m["base_row"][0:1, bass.ds(c, 1)], min_val=0, max_val=N - 1)
                sp.dma_start(qw[:, u], m["q_table"][bass.ds(base, W), :]).then_inc(edge_in[u], 16)

            for u in range(U):
                load_src(u, u)
            for u in range(U):
                load_edges(u, u)
                load_window(u, u)

            def body(c, u, peeled):
                sp.wait_ge(turned, c + 1)
                load_edges(c + U, u, peeled and c + U == NC - 1)
                sp.wait_ge(spread, c + 1 + LEAD)
                load_window(c + U, u)
                sp.wait_ge(kv_in[u], landed(c, u, 16 * K, U))
                load_src(c + U, u)
            over_chunks(sp, body, NC - U, U)

        @block.gpsimd
        def _(pool):
            def gather(c, u):
                pool.wait_ge(src_in[u], landed(c, u, 16, U))
                alone(pool, m["passed"])
                for k in range(K):
                    nc.gpsimd.indirect_dma_start(
                        out=kv[:, u, k], out_offset=None, in_=m["kv_table"],
                        in_offset=bass.IndirectOffsetOnAxis(ap=idx[:, u, k:k + 1], axis=0)).then_inc(kv_in[u], 16)
            for u in range(U):
                gather(u, u)

            def body(c, u, peeled):
                pool.wait_ge(summed, c + 1 + LEAD)
                gather(c + U, u)
            over_chunks(pool, body, NC - U, U)

        @block.tensor
        def _(pe):
            lead(pe, [spread, summed], LEAD)
            def turn(c, u):
                pe.wait_ge(edge_in[u], landed(c, u, 32, U))
                pe.wait_ge(hot_ready, c + 1)
                pe.wait_ge(copied, c + LEAD)
                for k in range(K):
                    nc.tensor.transpose(ps_eat[:, at(k, P)], ea[:, u, k], m["ident"][:])
                for k in range(K):
                    mm = nc.tensor.transpose(ps_hott[0:W, at(k, P)], hot[:, u, k], m["ident"][:])
                mm.then_inc(turned, 1)

            def spread_out(c, u, first=False):
                b = u % 2
                pe.wait_ge(copied, c + 1 + LEAD)
                if not first:
                    pe.wait_ge(gated, c - 1 + LEAD)
                for k in range(K):
                    nc.tensor.matmul(ps_q[:, b, k], hott[:, b, at(k, P)], qw[:, u], start=True, stop=True)
                for k in range(K):
                    mm = nc.tensor.matmul(ps_eh[:, b, k], eat[:, b, at(k, P)], m["w"][:, WE], start=True, stop=True)
                mm.then_inc(spread, 1)

            def sum_up(c, u):
                b = u % 2
                pe.wait_ge(valued, c + 1)
                for k in range(K):
                    nc.tensor.matmul(ps_sum[:, b, 0:W], kv[:, u, k, D:2 * D], hot[:, u, k], start=(k == 0), stop=(k == K - 1))
                for k in range(K):
                    mm = nc.tensor.matmul(ps_sum[:, b, W:2 * W], pex[:, b, k], hot[:, u, k],
                                          start=(k == 0), stop=(k == K - 1))
                mm.then_inc(summed, 1)

            turn(0, 0)
            turn(1, 1)
            spread_out(0, 0, True)

            def body(c, u, peeled):
                if not (peeled and c + 2 >= NC):
                    turn(c + 2, (u + 2) % U)
                if not (peeled and c + 1 >= NC):
                    spread_out(c + 1, (u + 1) % U)
                sum_up(c, u)
            over_chunks(pe, body, NC, U)

        @block.scalar
        def _(act):
            lead(act, [copied], LEAD)
            def copy_out(c, u, first=False):
                b = u % 2
                act.wait_ge(turned, c + 1)
                if not first:
                    act.wait_ge(spread, c - 1 + LEAD)
                nc.scalar.copy(eat[:, b], ps_eat[:])
                nc.scalar.copy(hott[:, b], ps_hott[0:W, :]).then_inc(copied, 1)

            def weigh(c, u, first=False):
                b = u % 2
                act.wait_ge(scored, c + 1)
                if not first:
                    act.wait_ge(summed, c - 1 + LEAD)
                nc.scalar.activation(pex[:, b].rearrange("p k (h d) -> p (k h) d", d=DH),
                                     score[:, b].unsqueeze(2).to_broadcast([P, K * H, DH]), ACT.Exp).then_inc(weighed, 1)
            copy_out(0, 0, True)
            copy_out(1, 1, True)
            weigh(0, 0, True)

            def body(c, u, peeled):
                if not (peeled and c + 2 >= NC):
                    copy_out(c + 2, (u + 2) % U)
                if not (peeled and c + 1 >= NC):
                    weigh(c + 1, (u + 1) % U)
            over_chunks(act, body, NC, U)

        @block.vector
        def _(dve):
            lead(dve, [gated, added], LEAD)
            def one_hot(c, u):
                nc.vector.tensor_tensor(hot[:, u],
                                        m["dst_local"][:, bass.ds(c, 1), :].rearrange("p a k -> p (a k)")
                                        .unsqueeze(2).to_broadcast([P, K, W]),
                                        m["iota"][:].unsqueeze(1).to_broadcast([P, K, W]),
                                        ALU.is_equal).then_inc(hot_ready, 1)

            def attend(c, u):
                b = u % 2
                flat = lambda v: v.rearrange("p k d -> p (k d)")
                dve.wait_ge(spread, c + 1 + LEAD)
                dve.wait_ge(kv_in[u], landed(c, u, 16 * K, U))
                nc.vector.tensor_tensor(prod[:].rearrange("p (k d) -> p k d", d=D), ps_q[:, b],
                                        kv[:, u, :, 0:D], ALU.mult).then_inc(mult, 1)
                dve.wait_ge(mult, c * 2 + 1)
                nc.vector.tensor_tensor(prod[:], prod[:], flat(ps_eh[:, b]), ALU.mult).then_inc(gated, 1)
                dve.wait_ge(gated, c + 1 + LEAD)
                nc.vector.tensor_reduce(score[:, b], prod[:].rearrange("p (h d) -> p h d", d=DH), AX,
                                        ALU.add).then_inc(mult, 1)
                dve.wait_ge(mult, c * 2 + 2)
                nc.vector.tensor_scalar(score[:, b], score[:, b], CLIP, -CLIP, ALU.min, ALU.max).then_inc(scored, 1)

            def value(c, u):
                b = u % 2
                dve.wait_ge(weighed, c + 1)
                values = kv[:, u, :, D:2 * D]
                nc.vector.tensor_tensor(values, values, pex[:, b], ALU.mult).then_inc(valued, 1)

            def add_up(c, u):
                b = u % 2
                base = dve.value_load(m["base_row"][0:1, bass.ds(c, 1)], min_val=0, max_val=N - 1)
                window = acc[:, 0:2, bass.ds(base, W)]
                dve.wait_ge(summed, c + 1 + LEAD)
                dve.wait_ge(added, c + LEAD)
                nc.vector.tensor_tensor(window, window, ps_sum[:, b, 0:2 * W].rearrange("p (a w) -> p a w", w=W),
                                        ALU.add).then_inc(added, 1)

            nc.vector.memset(acc[:, 0], 0.0).then_inc(clear, 1)
            nc.vector.memset(acc[:, 1], ATTN_EPS).then_inc(clear, 1)
            dve.wait_ge(clear, 2)
            one_hot(0, 0)
            one_hot(1, 1)
            one_hot(2, 2)
            attend(0, 0)
            value(0, 0)

            def body(c, u, peeled):
                if not (peeled and c + 3 >= NC):
                    one_hot(c + 3, (u + 3) % U)
                if not (peeled and c + 1 >= NC):
                    attend(c + 1, (u + 1) % U)
                add_up(c, u)
                if not (peeled and c + 1 >= NC):
                    value(c + 1, (u + 1) % U)
            over_chunks(dve, body, NC, U)


def far_windows0(nc, m, src, edges):
    with ExitStack() as ctx:
        sem = lambda name: counted(nc, ctx, m, name)
        sb = lambda name, shape, dt=F32: ctx.enter_context(nc.sbuf_tensor(name, shape, dt))
        ps = lambda name, shape: ctx.enter_context(nc.psum_tensor(name, shape, F32))
        cleared = sem("far0_cleared")
        src_in, edge_in, kv_in = sem("far0_src_in"), sem("far0_edge_in"), sem("far0_kv_in")
        hot_ready, turned, copied = sem("far0_hot_ready"), sem("far0_turned"), sem("far0_copied")
        spread, scored, weighed = sem("far0_spread"), sem("far0_scored"), sem("far0_weighed")
        valued, summed, added, step = sem("far0_valued"), sem("far0_summed"), sem("far0_added"), sem("far0_step")
        idx = sb("far0_idx", [P, K], I32)
        ea = sb("far0_ea", [P, K, D])
        qw = sb("far0_qw", [W, D])
        kv = sb("far0_kv", [P, K, 2 * D])
        nodes = sb("far0_nodes", [P, W])
        hot = sb("far0_hot", [P, K, W])
        eat, hott = sb("far0_eat", [P, CE]), sb("far0_hott", [W, CE])
        prod, score, pex = sb("far0_prod", [P, K, D]), sb("far0_score", [P, K * H]), sb("far0_pex", [P, K, D])
        ps_eat, ps_hott = ps("far0_ps_eat", [P, CE]), ps("far0_ps_hott", [P, CE])
        ps_eh, ps_q, ps_sum = ps("far0_ps_eh", [P, K, D]), ps("far0_ps_q", [P, K, D]), ps("far0_ps_sum", [P, CE])
        src_c = src.rearrange("(c p k) -> c p k", p=P, k=K)
        ea_c = edges[0:(NC - 1) * CE].rearrange("(c p k) d -> c p (k d)", p=P, k=K)
        ea_last = edges[(NC - 1) * CE:E].rearrange("(p k) d -> p (k d)", k=K)
        block = ctx.enter_context(nc.Block())

        @block.sync
        def _(sp):
            sp.wait_ge(cleared, 1)
            def body(c, j, visit):
                sp.dma_start(idx[:], row(src_c, c)).then_inc(src_in, 16)
                base = window_base(nc, sp, m, c, j)
                sp.dma_start(qw[:], m["q_table"][bass.ds(base, W), :]).then_inc(edge_in, 16)
                if isinstance(c, int):
                    sp.dma_start(ea[0:LAST // K].rearrange("p k d -> p (k d)"), ea_last).then_inc(edge_in, 16)
                else:
                    sp.dma_start(ea[:].rearrange("p k d -> p (k d)"), row(ea_c, c)).then_inc(edge_in, 16)
                sp.wait_ge(added, visit)
            over_far_windows(sp, m, body)

        @block.gpsimd
        def _(pool):
            def body(c, j, visit):
                pool.wait_ge(src_in, visit * 16)
                alone(pool, m["passed"])
                for k in range(K):
                    nc.gpsimd.indirect_dma_start(
                        out=kv[:, k], out_offset=None, in_=m["kv_table"],
                        in_offset=bass.IndirectOffsetOnAxis(ap=idx[:, k:k + 1], axis=0)).then_inc(kv_in, 16)
            over_far_windows(pool, m, body)

        @block.tensor
        def _(pe):
            def body(c, j, visit):
                pe.wait_ge(edge_in, visit * 32)
                pe.wait_ge(hot_ready, visit)
                for k in range(K):
                    nc.tensor.transpose(ps_eat[:, at(k, P)], ea[:, k], m["ident"][:])
                for k in range(K):
                    mm = nc.tensor.transpose(ps_hott[0:W, at(k, P)], hot[:, k], m["ident"][:])
                mm.then_inc(turned, 1)
                pe.wait_ge(copied, visit)
                alone(pe, m["passed"])
                for k in range(K):
                    nc.tensor.matmul(ps_q[:, k], hott[:, at(k, P)], qw[:], start=True, stop=True)
                for k in range(K):
                    mm = nc.tensor.matmul(ps_eh[:, k], eat[:, at(k, P)], m["w"][:, WE], start=True, stop=True)
                mm.then_inc(spread, 1)
                pe.wait_ge(valued, visit)
                alone(pe, m["passed"])
                for k in range(K):
                    nc.tensor.matmul(ps_sum[:, 0:W], kv[:, k, D:2 * D], hot[:, k], start=(k == 0), stop=(k == K - 1))
                for k in range(K):
                    mm = nc.tensor.matmul(ps_sum[:, W:2 * W], pex[:, k], hot[:, k], start=(k == 0), stop=(k == K - 1))
                mm.then_inc(summed, 1)
            over_far_windows(pe, m, body)

        @block.scalar
        def _(act):
            def body(c, j, visit):
                act.wait_ge(turned, visit)
                nc.scalar.copy(eat[:], ps_eat[:])
                nc.scalar.copy(hott[:], ps_hott[0:W, :]).then_inc(copied, 1)
                act.wait_ge(scored, visit)
                nc.scalar.activation(pex[:].rearrange("p k (h d) -> p (k h) d", d=DH),
                                     score[:].unsqueeze(2).to_broadcast([P, K * H, DH]), ACT.Exp).then_inc(weighed, 1)
            over_far_windows(act, m, body)

        @block.vector
        def _(dve):
            nc.vector.memset(ea[:], 0.0).then_inc(cleared, 1)
            dve.sem_inc(step, 4)
            def body(c, j, visit):
                do = Steps(dve, step, visit * 4).ordered
                do(nc.vector.tensor_tensor(nodes[:], m["iota"][:], m["shifts"][:, bass.ds(j, 1)].to_broadcast([P, W]),
                                           ALU.add))
                nc.vector.tensor_tensor(hot[:], m["dst_local"][:, bass.ds(c, 1), :].rearrange("p a k -> p (a k)")
                                        .unsqueeze(2).to_broadcast([P, K, W]),
                                        nodes[:].unsqueeze(1).to_broadcast([P, K, W]),
                                        ALU.is_equal).then_inc(hot_ready, 1)
                dve.wait_ge(spread, visit)
                dve.wait_ge(kv_in, visit * (16 * K))
                do(nc.vector.tensor_tensor(prod[:], ps_q[:], kv[:, :, 0:D], ALU.mult))
                do(nc.vector.tensor_tensor(prod[:], prod[:], ps_eh[:], ALU.mult))
                do(nc.vector.tensor_reduce(score[:], prod[:].rearrange("p k (h d) -> p (k h) d", d=DH), AX, ALU.add))
                nc.vector.tensor_scalar(score[:], score[:], CLIP, -CLIP, ALU.min, ALU.max).then_inc(scored, 1)
                dve.wait_ge(weighed, visit)
                values = kv[:, :, D:2 * D]
                nc.vector.tensor_tensor(values, values, pex[:], ALU.mult).then_inc(valued, 1)
                base = window_base(nc, dve, m, c, j)
                window = m["acc"][:, 0:2, bass.ds(base, W)]
                dve.wait_ge(summed, visit)
                nc.vector.tensor_tensor(window, window, ps_sum[:, 0:2 * W].rearrange("p (a w) -> p a w", w=W),
                                        ALU.add).then_inc(added, 1)
                dve.wait_ge(added, visit)
            over_far_windows(dve, m, body)


def batch_norm_scale(nc, do, mv, rstd, scale, shift, gamma, beta):
    do(nc.vector.tensor_tensor(scale, rstd, gamma, ALU.mult))
    do(nc.vector.tensor_tensor(shift, mv[:, 0:1], scale, ALU.mult))
    return nc.vector.tensor_tensor(shift, beta, shift, ALU.subtract)


def moments(nc, do, hold, y, stats, mv):
    for k in range(T):
        last = nc.vector.bn_stats(stats[:, k], y[:, k])
    do(last)
    hold()
    for k in range(T):
        last = nc.vector.bn_aggr(mv[:, k], stats[:, k])
    do(last)
    return nc.vector.tensor_scalar(mv[:, :, 1], mv[:, :, 1], NORM_EPS, None, ALU.add)


def one_over_deviation(nc, out, var, power):
    return nc.gpsimd.tensor_tensor(out, var, power, ALU.pow)


def nodes0(nc, m):
    with ExitStack() as ctx:
        sem = lambda name: counted(nc, ctx, m, name)
        sb = lambda name, shape, dt=F32: ctx.enter_context(nc.sbuf_tensor(name, shape, dt))
        ps = lambda name, shape: ctx.enter_context(nc.psum_tensor(name, shape, F32))
        wt_turned, wt_copied, wa_made, wa_ready = sem("wt_turned"), sem("wt_copied"), sem("wa_made"), sem("wa_ready")
        divided, h_ready, counted_slices = sem("h_divided"), sem("h_ready"), sem("counted_slices")
        h_step, scale_ready, ones_set = sem("h_step"), sem("scale_ready"), sem("ones_set")
        bn_var, bn_dev, ln_var, ln_dev = sem("bn_var"), sem("bn_dev"), sem("ln_var"), sem("ln_dev")
        den_out, den_in, inverted, inv_out = sem("den_out"), sem("den_in"), sem("inverted"), sem("inv_out")
        inv_in = [sem(f"inv_in{piece}") for piece in range(len(PIECES))]
        hn_ready, y_ready, y_turned = sem("hn_ready"), sem("y_ready"), sem("y_turned")
        ln_step, ln_ready, x1_ready = sem("ln_step"), sem("ln_ready"), sem("x1_ready")
        x1_turned, x1t_ready = sem("x1_turned"), sem("x1t_ready")
        logit_made, rows_made = sem("logit_made"), sem("rows_made")
        row_ready, logit_read = sem("row_ready"), sem("logit_read")
        taken, kept = sem("taken"), sem("max_kept")
        x1t_out = [sem(f"x1t_out{s}") for s in range(2)]
        row_out = [sem(f"row_out{s}") for s in range(2)]
        acc, vec, w = m["acc"], m["vec"], m["w"]
        stats = sb("bn_slices", [P, NG, 6])
        mv, scale, shift = sb("bn_mv", [P, 2]), sb("bn_scale", [P, 1]), sb("bn_shift", [P, 1])
        dev = sb("bn_dev", [P, 1])
        w1gt = sb("w1gt", [P, D])
        wa = sb("wa", [P, 2])
        waug = sb("waug", [P, ROW1])
        wa_both = sb("wa_both", [P, P])
        hn = sb("hn", [P, 2, G])
        y = sb("y", [P, 2, G])
        lst, lmv = sb("lst", [P, T, 6]), sb("lmv", [P, T, 2])
        lsc, lsh, lrs = sb("lsc", [P, 2, T]), sb("lsh", [P, 2, T]), sb("lrs", [P, T])
        x1 = sb("x1", [P, T, D])
        x1t = sb("x1t", [P, 2, G])
        xl = sb("xl", [P, 2, T, ROW1])
        ad = sb("ad", [1, 2, G])
        logit = sb("logit", [P, G])
        ps_y = ps("ps_y", [P, 2, T, D])
        ps_x1t = ps("ps_x1t", [P, G])
        ps_xl = ps("ps_xl", [P, T, 2 * D])
        ps_xlt = ps("ps_xlt", [P, G])
        ps_logit = ps("ps_logit", [P, G])
        ps_ad = ps("ps_ad", [P, G])
        table = m["xl_table"].rearrange("(g k p) d -> g p k d", k=T, p=P)
        block = ctx.enter_context(nc.Block())

        den = sb("den0", [P, H * NP // P])

        def inverse_back(eng, heads):
            for piece, (first, end) in enumerate(PIECES):
                for h in heads:
                    eng.dma_start(acc[h * DH:(h + 1) * DH, 1, first * G:end * G],
                                  m["inv_rows"][h, first * G:end * G].partition_broadcast(DH)).then_inc(inv_in[piece], 16)

        @block.sync
        def _(sp):
            sp.dma_start(m["den_rows"], acc[0:P:DH, 1, :]).then_inc(den_out, 16)
            sp.wait_ge(den_out, 16)
            sp.dma_start(den[:], m["den_rows"].rearrange("h (a n) -> (h a) n", a=P // H)).then_inc(den_in, 16)
            sp.wait_ge(inverted, 1)
            sp.dma_start(m["inv_rows"].rearrange("h (a n) -> (h a) n", a=P // H), den[:]).then_inc(inv_out, 16)
            sp.wait_ge(inv_out, 16)
            inverse_back(sp, range(0, H, 2))
            lead(sp, [*x1t_out, *row_out], DMA_LEAD)
            def body(g, s):
                sp.wait_ge(x1t_ready, g + 1)
                sp.dma_start(m["x1t_table"][:, at(g, G)], x1t[:, s]).then_inc(x1t_out[s], 16)
                sp.wait_ge(row_ready, g + 1 + LEAD)
                sp.dma_start(row(table, g), xl[:, s]).then_inc(row_out[s], 16)
                sp.dma_start(m["ad_row"][at(g, G)].unsqueeze(0), ad[:, s]).then_inc(row_out[s], 16)
            over_groups(sp, body)
            for s in range(2):
                sp.wait_ge(x1t_out[s], 16 * ((NG + 1 - s) // 2) + DMA_LEAD)
                sp.wait_ge(row_out[s], 32 * ((NG + 1 - s) // 2) + DMA_LEAD)

        @block.gpsimd
        def _(pool):
            with pool.Fori(0, NG) as g:
                pool.wait_ge(divided, g + 1)
                nc.gpsimd.tensor_tensor(acc[:, 0, at(g, G)], acc[:, 0, at(g, G)], acc[:, 2, at(g, G)],
                                        ALU.add).then_inc(h_ready, 1)
            pool.wait_ge(bn_var, 1)
            one_over_deviation(nc, dev[:], mv[:, 1:2], m["power"][:, 0:1]).then_inc(bn_dev, 1)
            pool.wait_ge(scale_ready, 1)
            nc.gpsimd.memset(acc[:, 1], 1.0).then_inc(ones_set, 1)
            with pool.Fori(0, NG) as g:
                pool.wait_ge(ln_var, g + 1)
                one_over_deviation(nc, lrs[:], lmv[:, :, 1], m["power"][:]).then_inc(ln_dev, 1)
            pool.wait_ge(ones_set, 1)

        @block.tensor
        def _(pe):
            lead(pe, [x1_turned], LEAD)
            nc.tensor.transpose(ps_x1t[:, 0:D], w[:, W1G], m["ident"][:]).then_inc(wt_turned, 1)
            pe.wait_ge(wt_copied, 1)
            nc.tensor.matmul(ps_ad[:, 0:2], w1gt[:], vec[:, ASRC:ADST + 1], start=True, stop=True).then_inc(wa_made, 1)
            pe.wait_ge(wa_ready, 1)

            def turn_y(g, s):
                pe.wait_ge(y_ready, g + 1 + LEAD)
                if not (isinstance(g, int) and g < 2):
                    pe.wait_ge(x1_ready, g - 1)
                for k in range(T):
                    mm = nc.tensor.transpose(ps_y[:, s, k], y[:, s, at(k, P)], m["ident"][:])
                mm.then_inc(y_turned, 1)

            def turn_x1(g):
                pe.wait_ge(x1_ready, g + 1)
                for k in range(T):
                    mm = nc.tensor.transpose(ps_x1t[:, at(k, P)], x1[:, k], m["ident"][:])
                mm.then_inc(x1_turned, 1)

            def multiply(g, s):
                pe.wait_ge(x1t_ready, g + 1)
                pe.wait_ge(taken, 2 * g + LEAD)
                nc.tensor.matmul(ps_xlt[:], w[:, W1G], x1t[:, s], start=True, stop=True)
                nc.tensor.matmul(ps_logit[:], wa_both[:], x1t[:, s], start=True, stop=True).then_inc(logit_made, 1)
                pe.wait_ge(row_ready, g + LEAD)
                for k in range(T):
                    nc.tensor.matmul(ps_xl[:, k, 0:ROW1], x1t[:, s, at(k, P)], waug[:], start=True, stop=True)
                nc.tensor.matmul(ps_ad[0:1, :], wa[:, 1:2], x1t[:, s], start=True, stop=True).then_inc(rows_made, 1)

            for g in range(3):
                turn_y(g, g % 2)
            turn_x1(0)

            def body(g, s):
                multiply(g, s)
                if exists(g + 3):
                    turn_y(g + 3, 1 - s)
                if exists(g + 1):
                    turn_x1(g + 1)
            over_groups_ahead(pe, body)

        @block.scalar
        def _(act):
            lead(act, [row_ready], LEAD)
            act.wait_ge(inv_out, 16)
            inverse_back(act, range(1, H, 2))
            act.wait_ge(wt_turned, 1)
            nc.scalar.copy(w1gt[:], ps_x1t[:, 0:D]).then_inc(wt_copied, 1)
            act.wait_ge(scale_ready, 1)

            def batch_norm(g, s):
                if not (isinstance(g, int) and g < 2):
                    act.wait_ge(y_ready, g - 1 + LEAD)
                nc.scalar.activation(hn[:, s], acc[:, 0, at(g, G)], ACT.Identity, bias=shift[:], scale=scale[:]).then_inc(hn_ready, 1)

            def layer_norm(g, s):
                act.wait_ge(ln_ready, g + 1)
                act.wait_ge(x1_turned, g + LEAD)
                for k in range(T):
                    last = nc.scalar.activation(x1[:, k], ps_y[:, s, k], ACT.Identity, bias=lsh[:, s, k:k + 1],
                                                scale=lsc[:, s, k:k + 1])
                last.then_inc(x1_ready, 1)

            def keep_x1t(g, s):
                act.wait_ge(x1_turned, g + 1 + LEAD)
                act.wait_ge(x1t_out[s], before(g, s, 16, 2) + DMA_LEAD)
                nc.scalar.copy(x1t[:, s], ps_x1t[:]).then_inc(x1t_ready, 1)

            def rows_out(g, s):
                act.wait_ge(rows_made, g + 1)
                act.wait_ge(row_out[s], before(g, s, 32, 2) + DMA_LEAD)
                nc.scalar.copy(xl[:, s], ps_xl[:, :, 0:ROW1])
                nc.scalar.copy(ad[:, s], ps_ad[0:1, :]).then_inc(row_ready, 1)

            for g in range(4):
                batch_norm(g, g % 2)
            layer_norm(0, 0)

            def body(g, s):
                keep_x1t(g, s)
                if exists(g + 1):
                    layer_norm(g + 1, 1 - s)
                if exists(g + 4):
                    batch_norm(g + 4, s)
                rows_out(g, s)
            over_groups_ahead(act, body)

        @block.vector
        def _(dve):
            lead(dve, [taken, y_ready, kept], LEAD)
            dve.wait_ge(den_in, 16)
            nc.vector.reciprocal(den[:], den[:]).then_inc(inverted, 1)
            def divide(g):
                part = acc[:, 0, at(g, G)]
                nc.vector.tensor_tensor(part, part, acc[:, 1, at(g, G)], ALU.mult).then_inc(divided, 1)

            def slice_stats(g):
                dve.wait_ge(h_ready, g + 1)
                nc.vector.bn_stats(stats[:, bass.ds(g, 1)].rearrange("p a s -> p (a s)"),
                                   acc[:, 0, at(g, SG)]).then_inc(counted_slices, 1)

            for piece, (first, end) in enumerate(PIECES):
                dve.wait_ge(inv_in[piece], 16 * H)
                if first == 0:
                    divide(0)
                with dve.Fori(max(first, 1), end) as g:
                    divide(g)
                    slice_stats(g - 1)
            slice_stats(NG - 1)
            dve.wait_ge(counted_slices, NG)
            do = Steps(dve, h_step).ordered
            do(nc.vector.bn_aggr(mv[:], stats[:].rearrange("p g s -> p (g s)")))
            nc.vector.tensor_scalar(mv[:, 1:2], mv[:, 1:2], NORM_EPS, None, ALU.add).then_inc(bn_var, 1)
            dve.wait_ge(bn_dev, 1)
            batch_norm_scale(nc, do, mv[:], dev[:], scale[:], shift[:],
                             vec[:, GAMMA0:GAMMA0 + 1], vec[:, BETA0:BETA0 + 1]).then_inc(scale_ready, 1)
            dve.wait_ge(wa_made, 1)
            do(nc.vector.tensor_copy(wa[:], ps_ad[:, 0:2]))
            do(nc.vector.memset(waug[:], 0.0))
            do(nc.vector.tensor_copy(waug[:, 0:D], w[:, W1G]))
            do(nc.vector.tensor_copy(waug[:, D:D + 1], wa[:, 0:1]))
            do(nc.vector.tensor_tensor(wa_both[:], wa[:, 0:1].to_broadcast([P, P]), wa[:, 1:2].to_broadcast([P, P]), ALU.add))
            nc.vector.tensor_copy(logit[:, 0:1], wa[:, 0:1]).then_inc(wa_ready, 1)

            def add_x(g, s):
                dve.wait_ge(hn_ready, g + 1)
                nc.vector.tensor_tensor(y[:, s], hn[:, s], acc[:, 2, at(g, G)], ALU.add).then_inc(y_ready, 1)

            def node_moments(g, s):
                dve.wait_ge(y_turned, g + 1)
                moments(nc, Steps(dve, ln_step, g * 2).ordered, lambda: alone(dve, m["passed"]), ps_y[:, s], lst, lmv).then_inc(ln_var, 1)

            def statistics(g, s):
                dve.wait_ge(ln_dev, g + 1)
                nc.vector.tensor_copy(lsc[:, s], lrs[:])
                nc.vector.scalar_tensor_tensor(lsh[:, s], lmv[:, :, 0], -1.0, lrs[:], ALU.mult,
                                               ALU.mult).then_inc(ln_ready, 1)

            def take(g):
                dve.wait_ge(logit_made, g + 1)
                dve.wait_ge(hn_ready, g + 1)
                dve.wait_ge(kept, g + LEAD)
                nc.vector.tensor_copy(acc[:, 0, at(g, G)], ps_xlt[:]).then_inc(taken, 1)
                nc.vector.tensor_copy(logit[:], ps_logit[:]).then_inc(taken, 1)
                dve.wait_ge(taken, 2 * g + 2 + LEAD)
                nc.vector.scalar_tensor_tensor(acc[:, 2, at(g, G)], logit[:], SLOPE, logit[:], ALU.mult, ALU.max).then_inc(kept, 1)

            add_x(0, 0)
            add_x(1, 1)
            node_moments(0, 0)
            add_x(2, 0)
            statistics(0, 0)
            node_moments(1, 1)

            def body(g, s):
                if exists(g + 1):
                    statistics(g + 1, 1 - s)
                if exists(g + 3):
                    add_x(g + 3, 1 - s)
                if exists(g + 2):
                    node_moments(g + 2, s)
                take(g)
            over_groups_ahead(dve, body)
            dve.wait_ge(kept, NG + LEAD)


def edges1(nc, m, src):
    with ExitStack() as ctx:
        sem = lambda name: ctx.enter_context(nc.semaphore(name))
        sb = lambda name, shape, dt=F32: ctx.enter_context(nc.sbuf_tensor(name, shape, dt))
        ps = lambda name, shape: ctx.enter_context(nc.psum_tensor(name, shape, F32))
        src_in = [sem(f"src1_in{u}") for u in range(V)]
        ad_in = [sem(f"ad_in{u}") for u in range(V)]
        xl_in = [sem(f"xl_in{u}") for u in range(V)]
        summed_logit, leaky, off_ready, masked = sem("summed_logit"), sem("leaky"), sem("off_ready"), sem("masked")
        largest, turned, column = sem("largest"), sem("max_turned"), sem("max_column")
        spread, max_step, shifted = sem("max_spread"), sem("max_step"), sem("shifted")
        weighed, summed, rescaled, added, set_up = sem("weighed1"), sem("summed1"), sem("rescaled"), sem("added1"), sem("set_up")
        max_written, slots_summed = sem("max_written"), sem("slots_summed")
        idx = sb("idx1", [P, V, K], I32)
        adw = sb("adw", [P, V, W])
        xg = sb("xg", [P, V, K, ROW1])
        ones = sb("ones", [P, P])
        lg = sb("lg", [P, 4, K, W])
        off = sb("off", [P, K, W])
        top = sb("top", [P, 2, W])
        col = sb("col", [W, 2])
        newm = sb("newm", [P, 2, W])
        drop = sb("drop", [P, 2, W])
        fade = sb("fade", [P, 4, W])
        pw = sb("pw", [P, 2, K, W])
        pws = sb("pws", [P, 2, W])
        ps_top = ps("ps_top", [P, 2, G])
        ps_max = ps("ps_max", [P, 2, G])
        ps_sum = ps("ps_sum1", [P, 2, CE])
        src_c = src.rearrange("(c p k) -> c p k", p=P, k=K)
        block = ctx.enter_context(nc.Block())
        acc = m["acc"]

        @block.sync
        def _(sp):
            def load_src(c, u):
                sp.dma_start(idx[:, u], row(src_c, c)).then_inc(src_in[u], 16)

            def load_window(c, u):
                base = sp.value_load(m["base_row"][0:1, bass.ds(c, 1)], min_val=0, max_val=N - 1)
                sp.dma_start(adw[:, u], m["ad_row"][bass.ds(base, W)].partition_broadcast(P)).then_inc(ad_in[u], 16)

            for u in range(V):
                load_src(u, u)
            for u in range(V):
                load_window(u, u)

            def body(c, u, peeled):
                sp.wait_ge(largest, c + 1)
                load_window(c + V, u)
                sp.wait_ge(xl_in[u], landed(c, u, 16 * K, V))
                load_src(c + V, u)
            over_chunks(sp, body, NC - V, V)
            for finished in m["used"]:
                sp.sem_clear(finished)

        @block.gpsimd
        def _(pool):
            def gather(c, u):
                pool.wait_ge(src_in[u], landed(c, u, 16, V))
                alone(pool, m["passed"])
                for k in range(K):
                    nc.gpsimd.indirect_dma_start(
                        out=xg[:, u, k], out_offset=None, in_=m["xl_table"],
                        in_offset=bass.IndirectOffsetOnAxis(ap=idx[:, u, k:k + 1], axis=0)).then_inc(xl_in[u], 16)
            for u in range(V):
                gather(u, u)

            def body(c, u, peeled):
                pool.wait_ge(summed, c + 1 + LEAD)
                gather(c + V, u)
            over_chunks(pool, body, NC - V, V)

        @block.tensor
        def _(pe):
            lead(pe, [summed], LEAD)
            def turn_top(c, u):
                pe.wait_ge(largest, c + 1)
                alone(pe, m["passed"])
                nc.tensor.transpose(ps_top[0:W, u % 2, 0:P], top[:, u % 2], m["ident"][:]).then_inc(turned, 1)

            def spread_max(c, u):
                pe.wait_ge(column, c + 1)
                nc.tensor.matmul(ps_max[:, u % 2, 0:W], col[:, u % 2:u % 2 + 1].to_broadcast([W, P]),
                                 m["ident"][0:W, 0:W], start=True, stop=True).then_inc(spread, 1)

            def sum_up(c, u):
                b = u % 2
                pe.wait_ge(slots_summed, c + 1)
                for k in range(K):
                    nc.tensor.matmul(ps_sum[:, b, 0:W], xg[:, u, k, 0:D], pw[:, b, k], start=(k == 0), stop=(k == K - 1))
                nc.tensor.matmul(ps_sum[:, b, W:2 * W], ones[:], pws[:, b], start=True, stop=True).then_inc(summed, 1)

            for c in range(3):
                turn_top(c, c)
                spread_max(c, c)
            turn_top(3, 3)
            sum_up(0, 0)

            def body(c, u, peeled):
                if not (peeled and c + 3 >= NC):
                    spread_max(c + 3, (u + 3) % V)
                if not (peeled and c + 4 >= NC):
                    turn_top(c + 4, (u + 4) % V)
                if not (peeled and c + 1 >= NC):
                    sum_up(c + 1, (u + 1) % V)
            over_chunks(pe, body, NC, V)

        @block.scalar
        def _(act):
            lead(act, [weighed], LEAD)
            def weigh(c, u, first=False):
                b = u % 2
                base = act.value_load(m["base_row"][0:1, bass.ds(c, 1)], min_val=0, max_val=N - 1)
                act.wait_ge(shifted, c + 1)
                if not first:
                    act.wait_ge(summed, c - 1 + LEAD)
                nc.scalar.copy(acc[:, 2, bass.ds(base, W)], newm[:, b]).then_inc(max_written, 1)
                nc.scalar.activation(fade[:, u % 4], drop[:, b], ACT.Exp)
                nc.scalar.activation(pw[:, b], lg[:, u % 4], ACT.Exp).then_inc(weighed, 1)

            def logits(c, u, first=False):
                if not first:
                    act.wait_ge(weighed, c - 3 + LEAD)
                act.wait_ge(ad_in[u], landed(c, u, 16, V))
                act.wait_ge(xl_in[u], landed(c, u, 16 * K, V))
                for k in range(K):
                    last = nc.scalar.activation(lg[:, u % 4, k], adw[:, u], ACT.Identity, bias=xg[:, u, k, D:D + 1])
                last.then_inc(summed_logit, 1)

            for c in range(4):
                logits(c, c, True)
            weigh(0, 0, True)
            weigh(1, 1, True)
            logits(4, 4)

            def body(c, u, peeled):
                if not (peeled and c + 2 >= NC):
                    weigh(c + 2, (u + 2) % V)
                if not (peeled and c + 5 >= NC):
                    logits(c + 5, (u + 5) % V)
            over_chunks(act, body, NC, V)

        @block.vector
        def _(dve):
            nc.vector.memset(ones[:], 1.0).then_inc(set_up, 1)
            dve.wait_ge(set_up, 1)

            def find_off(c, u):
                t = lg[:, u % 4]
                dve.wait_ge(summed_logit, c + 1)
                nc.vector.scalar_tensor_tensor(t, t, SLOPE, t, ALU.mult, ALU.max).then_inc(leaky, 1)
                nc.vector.tensor_tensor(off[:], m["dst_local"][:, bass.ds(c, 1), :].rearrange("p a k -> p (a k)")
                                        .unsqueeze(2).to_broadcast([P, K, W]),
                                        m["iota"][:].unsqueeze(1).to_broadcast([P, K, W]),
                                        ALU.not_equal).then_inc(off_ready, 1)

            def mask(c, u):
                t = lg[:, u % 4]
                dve.wait_ge(off_ready, c + 1)
                dve.wait_ge(leaky, c + 1)
                nc.vector.scalar_tensor_tensor(t, off[:], MASKED, t, ALU.mult, ALU.add).then_inc(masked, 1)

            def find_top(c, u):
                dve.wait_ge(masked, c + 1)
                nc.vector.tensor_reduce(top[:, u % 2], lg[:, u % 4].rearrange("p k w -> p w k"), AX,
                                        ALU.max).then_inc(largest, 1)

            def max_column(c, u):
                b = u % 2
                dve.wait_ge(turned, c + 1)
                nc.vector.tensor_reduce(col[:, b:b + 1], ps_top[0:W, b, 0:P], AX, ALU.max).then_inc(column, 1)

            def new_max(c, u, first=False):
                b = u % 2
                base = dve.value_load(m["base_row"][0:1, bass.ds(c, 1)], min_val=0, max_val=N - 1)
                running = acc[:, 2, bass.ds(base, W)]
                if not first:
                    dve.wait_ge(max_written, c)
                dve.wait_ge(spread, c + 1)
                nc.vector.tensor_tensor(newm[:, b], running, ps_max[:, b, 0:W], ALU.max).then_inc(max_step, 1)
                return running

            def shift(c, u, running):
                b = u % 2
                dve.wait_ge(max_step, c + 1)
                nc.vector.tensor_tensor(drop[:, b], running, newm[:, b], ALU.subtract)
                nc.vector.tensor_tensor(lg[:, u % 4], lg[:, u % 4], newm[:, b].unsqueeze(1).to_broadcast([P, K, W]),
                                        ALU.subtract).then_inc(shifted, 1)

            def sum_slots(c, u):
                dve.wait_ge(weighed, c + 1 + LEAD)
                nc.vector.tensor_reduce(pws[:, u % 2], pw[:, u % 2].rearrange("p k w -> p w k"), AX,
                                        ALU.add).then_inc(slots_summed, 1)

            def rescale(c, u):
                base = dve.value_load(m["base_row"][0:1, bass.ds(c, 1)], min_val=0, max_val=N - 1)
                window = acc[:, 0:2, bass.ds(base, W)]
                dve.wait_ge(weighed, c + 1 + LEAD)
                nc.vector.tensor_tensor(window, window, fade[:, u % 4].unsqueeze(1).to_broadcast([P, 2, W]),
                                        ALU.mult).then_inc(rescaled, 1)
                return window

            def add_up(c, u, window):
                dve.wait_ge(rescaled, c + 1)
                dve.wait_ge(summed, c + 1 + LEAD)
                nc.vector.tensor_tensor(window, window, ps_sum[:, u % 2, 0:2 * W].rearrange("p (a w) -> p a w", w=W),
                                        ALU.add).then_inc(added, 1)

            for c in range(2):
                find_off(c, c)
                mask(c, c)
                find_top(c, c)
                max_column(c, c)
                shift(c, c, new_max(c, c, c == 0))
            for c in range(2, 4):
                find_off(c, c)
                mask(c, c)
                find_top(c, c)
                if c == 2:
                    max_column(c, c)
            sum_slots(0, 0)

            def body(c, u, peeled):
                done = lambda ahead: peeled and c + ahead >= NC
                if not done(3):
                    max_column(c + 3, (u + 3) % V)
                if not done(4):
                    find_off(c + 4, (u + 4) % V)
                if not done(2):
                    running = new_max(c + 2, (u + 2) % V)
                if not done(4):
                    mask(c + 4, (u + 4) % V)
                if not done(2):
                    shift(c + 2, (u + 2) % V, running)
                window = rescale(c, u)
                if not done(4):
                    find_top(c + 4, (u + 4) % V)
                add_up(c, u, window)
                if not done(1):
                    sum_slots(c + 1, (u + 1) % V)
                dve.wait_ge(added, c + 1)
            over_chunks(dve, body, NC, V)


def far_windows1(nc, m, src):
    with ExitStack() as ctx:
        sem = lambda name: ctx.enter_context(nc.semaphore(name))
        sb = lambda name, shape, dt=F32: ctx.enter_context(nc.sbuf_tensor(name, shape, dt))
        ps = lambda name, shape: ctx.enter_context(nc.psum_tensor(name, shape, F32))
        ones_set = sem("far1_ones_set")
        src_in, ad_in, xl_in = sem("far1_src_in"), sem("far1_ad_in"), sem("far1_xl_in")
        summed_logit, largest, turned = sem("far1_summed_logit"), sem("far1_largest"), sem("far1_turned")
        column, spread, shifted = sem("far1_column"), sem("far1_spread"), sem("far1_shifted")
        weighed, summed, added, step = sem("far1_weighed"), sem("far1_summed"), sem("far1_added"), sem("far1_step")
        idx = sb("far1_idx", [P, K], I32)
        adw = sb("far1_adw", [P, W])
        xg = sb("far1_xg", [P, K, ROW1])
        nodes = sb("far1_nodes", [P, W])
        ones = sb("far1_ones", [P, P])
        lg, off, pw = sb("far1_lg", [P, K, W]), sb("far1_off", [P, K, W]), sb("far1_pw", [P, K, W])
        top, newm, drop, fade = (sb(f"far1_{n}", [P, W]) for n in ("top", "newm", "drop", "fade"))
        col = sb("far1_col", [W, 1])
        ps_top, ps_max, ps_sum = ps("far1_ps_top", [P, G]), ps("far1_ps_max", [P, G]), ps("far1_ps_sum", [P, CE])
        src_c = src.rearrange("(c p k) -> c p k", p=P, k=K)
        acc = m["acc"]
        block = ctx.enter_context(nc.Block())

        @block.sync
        def _(sp):
            def body(c, j, visit):
                sp.dma_start(idx[:], row(src_c, c)).then_inc(src_in, 16)
                base = window_base(nc, sp, m, c, j)
                sp.dma_start(adw[:], m["ad_row"][bass.ds(base, W)].partition_broadcast(P)).then_inc(ad_in, 16)
                sp.wait_ge(added, visit)
            over_far_windows(sp, m, body)

        @block.gpsimd
        def _(pool):
            def body(c, j, visit):
                pool.wait_ge(src_in, visit * 16)
                alone(pool, m["passed"])
                for k in range(K):
                    nc.gpsimd.indirect_dma_start(
                        out=xg[:, k], out_offset=None, in_=m["xl_table"],
                        in_offset=bass.IndirectOffsetOnAxis(ap=idx[:, k:k + 1], axis=0)).then_inc(xl_in, 16)
            over_far_windows(pool, m, body)

        @block.tensor
        def _(pe):
            pe.wait_ge(ones_set, 1)
            def body(c, j, visit):
                pe.wait_ge(largest, visit)
                alone(pe, m["passed"])
                nc.tensor.transpose(ps_top[0:W, 0:P], top[:], m["ident"][:]).then_inc(turned, 1)
                pe.wait_ge(column, visit)
                nc.tensor.matmul(ps_max[:, 0:W], col[:].to_broadcast([W, P]), m["ident"][0:W, 0:W],
                                 start=True, stop=True).then_inc(spread, 1)
                pe.wait_ge(weighed, visit)
                for k in range(K):
                    nc.tensor.matmul(ps_sum[:, 0:W], xg[:, k, 0:D], pw[:, k], start=(k == 0), stop=(k == K - 1))
                for k in range(K):
                    mm = nc.tensor.matmul(ps_sum[:, W:2 * W], ones[:], pw[:, k], start=(k == 0), stop=(k == K - 1))
                mm.then_inc(summed, 1)
            over_far_windows(pe, m, body)

        @block.scalar
        def _(act):
            def body(c, j, visit):
                act.wait_ge(ad_in, visit * 16)
                act.wait_ge(xl_in, visit * (16 * K))
                for k in range(K):
                    last = nc.scalar.activation(lg[:, k], adw[:], ACT.Identity, bias=xg[:, k, D:D + 1])
                last.then_inc(summed_logit, 1)
                base = window_base(nc, act, m, c, j)
                act.wait_ge(shifted, visit)
                nc.scalar.activation(fade[:], drop[:], ACT.Exp)
                nc.scalar.copy(acc[:, 2, bass.ds(base, W)], newm[:])
                nc.scalar.activation(pw[:], lg[:], ACT.Exp).then_inc(weighed, 1)
            over_far_windows(act, m, body)

        @block.vector
        def _(dve):
            nc.vector.memset(ones[:], 1.0).then_inc(ones_set, 1)
            dve.sem_inc(step, 6)
            def body(c, j, visit):
                do = Steps(dve, step, visit * 6).ordered
                do(nc.vector.tensor_tensor(nodes[:], m["iota"][:], m["shifts"][:, bass.ds(j, 1)].to_broadcast([P, W]),
                                           ALU.add))
                do(nc.vector.tensor_tensor(off[:], m["dst_local"][:, bass.ds(c, 1), :].rearrange("p a k -> p (a k)")
                                           .unsqueeze(2).to_broadcast([P, K, W]),
                                           nodes[:].unsqueeze(1).to_broadcast([P, K, W]), ALU.not_equal))
                dve.wait_ge(summed_logit, visit)
                do(nc.vector.scalar_tensor_tensor(lg[:], lg[:], SLOPE, lg[:], ALU.mult, ALU.max))
                do(nc.vector.scalar_tensor_tensor(lg[:], off[:], MASKED, lg[:], ALU.mult, ALU.add))
                nc.vector.tensor_reduce(top[:], lg[:].rearrange("p k w -> p w k"), AX, ALU.max).then_inc(largest, 1)
                dve.wait_ge(turned, visit)
                nc.vector.tensor_reduce(col[:], ps_top[0:W, 0:P], AX, ALU.max).then_inc(column, 1)
                base = window_base(nc, dve, m, c, j)
                running = acc[:, 2, bass.ds(base, W)]
                dve.wait_ge(spread, visit)
                do(nc.vector.tensor_tensor(newm[:], running, ps_max[:, 0:W], ALU.max))
                nc.vector.tensor_tensor(drop[:], running, newm[:], ALU.subtract)
                nc.vector.tensor_tensor(lg[:], lg[:], newm[:].unsqueeze(1).to_broadcast([P, K, W]),
                                        ALU.subtract).then_inc(shifted, 1)
                window = acc[:, 0:2, bass.ds(base, W)]
                dve.wait_ge(weighed, visit)
                do(nc.vector.tensor_tensor(window, window, fade[:].unsqueeze(1).to_broadcast([P, 2, W]), ALU.mult))
                dve.wait_ge(summed, visit)
                nc.vector.tensor_tensor(window, window, ps_sum[:, 0:2 * W].rearrange("p (a w) -> p a w", w=W),
                                        ALU.add).then_inc(added, 1)
                dve.wait_ge(added, visit)
            over_far_windows(dve, m, body)


def nodes1(nc, m, out):
    with ExitStack() as ctx:
        sem = lambda name: ctx.enter_context(nc.semaphore(name))
        sb = lambda name, shape, dt=F32: ctx.enter_context(nc.sbuf_tensor(name, shape, dt))
        ps = lambda name, shape: ctx.enter_context(nc.psum_tensor(name, shape, F32))
        acc, vec, w = m["acc"], m["vec"], m["w"]
        den_out, den_in, inv_out = sem("den1_out"), sem("den1_in"), sem("inv1_out")
        inv_in = [sem(f"inv1_in{piece}") for piece in range(len(PIECES))]
        bias_made, bias_ready = sem("bias_made"), sem("bias_ready")
        den_step, inverted, divided = sem("den_step"), sem("inverted1"), sem("divided1")
        lin = [sem("lin0"), sem("lin1")]
        lin_out = [sem("lin_out0"), sem("lin_out1")]
        relu_ready = sem("relu_ready")
        stat = [sem("stat0"), sem("stat1")]
        scaled = [sem("scaled0"), sem("scaled1")]
        bn_step = sem("bn_step")
        bn_var, bn_dev, ln_var, ln_dev = sem("bn_var1"), sem("bn_dev1"), sem("ln_var1"), sem("ln_dev1")
        x1_in = [sem(f"x1_in{s}") for s in range(2)]
        out_stored = [sem(f"out_stored{s}") for s in range(2)]
        h_ready, y_ready, y_turned = sem("h_ready1"), sem("y_ready1"), sem("y_turned1")
        ln_step, ln_ready, normed = sem("ln_step1"), sem("ln_ready1"), sem("normed1")
        bias = sb("bias_both", [P, 1])
        r = sb("r", [P, 2, G])
        x1t = sb("x1t_b", [P, 2, G])
        y = sb("y_b", [P, 2, G])
        xo = sb("xo", [P, 2, T, D])
        stats = sb("bn_slices1", [P, NG, 6])
        mv = sb("mv1", [P, 2, 2])
        scale, shift, dev = sb("scale1", [P, 2]), sb("shift1", [P, 2]), sb("dev1", [P, 2])
        den = sb("den1", [P, NP // P])
        quot = sb("quot", [P, 4, SG])
        lst, lmv = sb("lst1", [P, T, 6]), sb("lmv1", [P, T, 2])
        lsc, lsh, lrs = sb("lsc1", [P, 2, T]), sb("lsh1", [P, 2, T]), sb("lrs1", [P, T])
        ps_lin = ps("ps_lin", [P, 2, 512])
        ps_y = ps("ps_y1", [P, 2, T, D])
        out_g = out.rearrange("(g k p) d -> g p k d", k=T, p=P)
        block = ctx.enter_context(nc.Block())

        @block.sync
        def _(sp):
            lead(sp, [*out_stored], DMA_LEAD)
            sp.dma_start(m["den_row1"].unsqueeze(0), acc[0:1, 1, :]).then_inc(den_out, 16)
            sp.wait_ge(den_out, 16)
            sp.dma_start(den[:], m["den_row1"].rearrange("(p n) -> p n", p=P)).then_inc(den_in, 16)
            sp.wait_ge(inverted, 1)
            sp.dma_start(m["inv_row1"].rearrange("(p n) -> p n", p=P), den[:]).then_inc(inv_out, 16)
            sp.wait_ge(inv_out, 16)
            for piece, (first, end) in enumerate(PIECES):
                sp.dma_start(acc[:, 1, first * G:end * G],
                             m["inv_row1"][first * G:end * G].partition_broadcast(P)).then_inc(inv_in[piece], 16)

            def load(g, s):
                sp.dma_start(x1t[:, s], m["x1t_table"][:, at(g, G)]).then_inc(x1_in[s], 16)
            load(0, 0)
            load(1, 1)

            def body(g, s, ahead=True):
                if ahead:
                    sp.wait_ge(y_ready, g + 1 + LEAD)
                    load(g + 2, s)
                sp.wait_ge(normed, g + 1 + LEAD)
                sp.dma_start(row(out_g, g), xo[:, s]).then_inc(out_stored[s], 16)
            with sp.Fori(0, (NG - 3) // 2) as turn:
                body(turn * 2, 0)
                body(turn * 2 + 1, 1)
            for g in range(NG - 3, NG):
                body(g, g % 2, g + 2 < NG)
            for s in range(2):
                sp.wait_ge(out_stored[s], 16 * ((NG + 1 - s) // 2) + DMA_LEAD)

        @block.gpsimd
        def _(pool):
            for layer in range(2):
                pool.wait_ge(bn_var, layer + 1)
                one_over_deviation(nc, dev[:, layer:layer + 1], mv[:, layer, 1:2], m["power"][:, 0:1]).then_inc(bn_dev, 1)
            with pool.Fori(0, NG) as g:
                pool.wait_ge(ln_var, g + 1)
                one_over_deviation(nc, lrs[:], lmv[:, :, 1], m["power"][:]).then_inc(ln_dev, 1)

        @block.tensor
        def _(pe):
            lead(pe, [*lin, y_turned], LEAD)
            nc.tensor.matmul(ps_y[:, 0, 0, 0:1], w[:, WM1], vec[:, BGAT:BGAT + 1], start=True, stop=True).then_inc(bias_made, 1)

            def linear(layer, source, ready, slots):
                def body(g, s):
                    pe.wait_ge(ready, g + 1)
                    if not (isinstance(g, int) and g < 2):
                        pe.wait_ge(lin_out[layer], g - 1 + LEAD)
                    nc.tensor.matmul(ps_lin[:, s % 2, 0:SG], w[:, WM1 + layer], source[:, s, 0:SG],
                                     start=True, stop=True).then_inc(lin[layer], 1)
                over_groups_ahead(pe, body, slots)
            linear(0, quot, divided, 4)
            linear(1, r, relu_ready, 2)

            def turn_y(g, s):
                pe.wait_ge(y_ready, g + 1 + LEAD)
                if not (isinstance(g, int) and g < 2):
                    pe.wait_ge(normed, g - 1 + LEAD)
                for k in range(T):
                    mm = nc.tensor.transpose(ps_y[:, s, k], y[:, s, at(k, P)], m["ident"][:])
                mm.then_inc(y_turned, 1)
            over_groups_ahead(pe, turn_y)

        @block.scalar
        def _(act):
            lead(act, [lin_out[0], normed], LEAD)
            act.wait_ge(bias_ready, 1)

            def bias_out(g, s):
                act.wait_ge(lin[0], g + 1 + LEAD)
                nc.scalar.activation(acc[:, 0, at(g, SG)], ps_lin[:, s, 0:SG], ACT.Identity,
                                     bias=bias[:]).then_inc(lin_out[0], 1)
            over_groups(act, bias_out)
            act.wait_ge(scaled[0], 1)

            def hidden(g, s):
                if not (isinstance(g, int) and g < 2):
                    act.wait_ge(lin[1], g - 1 + LEAD)
                nc.scalar.activation(r[:, s, 0:SG], acc[:, 0, at(g, SG)], ACT.Relu, bias=shift[:, 0:1],
                                     scale=scale[:, 0:1]).then_inc(relu_ready, 1)
            over_groups_ahead(act, hidden)
            act.wait_ge(scaled[1], 1)

            def last_relu(g, s):
                if not (isinstance(g, int) and g < 2):
                    act.wait_ge(y_ready, g - 1 + LEAD)
                nc.scalar.activation(r[:, s], acc[:, 1, at(g, G)], ACT.Relu, bias=shift[:, 1:2],
                                     scale=scale[:, 1:2]).then_inc(h_ready, 1)

            def normalise(g, s):
                act.wait_ge(ln_ready, g + 1)
                act.wait_ge(out_stored[s], before(g, s, 16, 2) + DMA_LEAD)
                for k in range(T):
                    last = nc.scalar.activation(xo[:, s, k], ps_y[:, s, k], ACT.Identity, bias=lsh[:, s, k:k + 1],
                                                scale=lsc[:, s, k:k + 1])
                last.then_inc(normed, 1)

            for g in range(3):
                last_relu(g, g % 2)

            def body(g, s):
                normalise(g, s)
                if exists(g + 3):
                    last_relu(g + 3, 1 - s)
            over_groups_ahead(act, body)

        @block.vector
        def _(dve):
            lead(dve, [y_ready, lin_out[1]], LEAD)
            dve.wait_ge(bias_made, 1)
            nc.vector.tensor_tensor(bias[:], ps_y[:, 0, 0, 0:1], vec[:, B1:B1 + 1], ALU.add).then_inc(bias_ready, 1)
            dve.wait_ge(den_in, 16)
            nc.vector.tensor_scalar(den[:], den[:], SM_EPS, None, ALU.add).then_inc(den_step, 1)
            dve.wait_ge(den_step, 1)
            nc.vector.reciprocal(den[:], den[:]).then_inc(inverted, 1)

            def divide(g, s):
                if not (isinstance(g, int) and g < 4):
                    dve.wait_ge(lin[0], g - 3 + LEAD)
                nc.vector.tensor_tensor(quot[:, s], acc[:, 0, at(g, SG)], acc[:, 1, at(g, SG)],
                                        ALU.mult).then_inc(divided, 1)

            def slice_stats(layer, g):
                dve.wait_ge(lin_out[layer], g + 1 + LEAD)
                nc.vector.bn_stats(stats[:, bass.ds(g, 1)].rearrange("p a s -> p (a s)"),
                                   acc[:, layer, at(g, SG)]).then_inc(stat[layer], 1)

            def scales(layer):
                dve.wait_ge(stat[layer], NG)
                do = Steps(dve, bn_step, 3 * layer).ordered
                do(nc.vector.bn_aggr(mv[:, layer], stats[:].rearrange("p g s -> p (g s)")))
                nc.vector.tensor_scalar(mv[:, layer, 1:2], mv[:, layer, 1:2], NORM_EPS, None, ALU.add).then_inc(bn_var, 1)
                dve.wait_ge(bn_dev, layer + 1)
                batch_norm_scale(nc, do,
                                 mv[:, layer], dev[:, layer:layer + 1], scale[:, layer:layer + 1], shift[:, layer:layer + 1],
                                 vec[:, G1 + 3 * layer:G1 + 3 * layer + 1],
                                 vec[:, BE1 + 3 * layer:BE1 + 3 * layer + 1]).then_inc(scaled[layer], 1)

            for g in range(3):
                dve.wait_ge(inv_in[0], 16)
                divide(g, g)
            for piece in range(1, len(PIECES)):
                dve.wait_ge(inv_in[piece], 16)

            def first(g, s):
                if exists(g + 3):
                    divide(g + 3, (s + 3) % 4)
                slice_stats(0, g)
            over_groups_ahead(dve, first, 4)
            scales(0)

            def second_bias(g, s):
                dve.wait_ge(lin[1], g + 1 + LEAD)
                nc.vector.tensor_scalar(acc[:, 1, at(g, SG)], ps_lin[:, s, 0:SG], vec[:, B2:B2 + 1], None,
                                        ALU.add).then_inc(lin_out[1], 1)
            second_bias(0, 0)

            def second(g, s):
                if exists(g + 1):
                    second_bias(g + 1, 1 - s)
                slice_stats(1, g)
            over_groups_ahead(dve, second)
            scales(1)

            def add_x1(g, s):
                dve.wait_ge(h_ready, g + 1)
                dve.wait_ge(x1_in[s], landed(g, s, 16, 2))
                nc.vector.scalar_tensor_tensor(y[:, s], x1t[:, s], 2.0, r[:, s], ALU.mult, ALU.add).then_inc(y_ready, 1)

            def node_moments(g, s):
                dve.wait_ge(y_turned, g + 1 + LEAD)
                do = Steps(dve, ln_step, g * 2).ordered
                moments(nc, do, lambda: alone(dve, m["passed"]), ps_y[:, s], lst, lmv).then_inc(ln_var, 1)

            def statistics(g, s):
                dve.wait_ge(ln_dev, g + 1)
                nc.vector.tensor_copy(lsc[:, s], lrs[:])
                nc.vector.scalar_tensor_tensor(lsh[:, s], lmv[:, :, 0], -1.0, lrs[:], ALU.mult,
                                               ALU.mult).then_inc(ln_ready, 1)

            add_x1(0, 0)
            add_x1(1, 1)
            node_moments(0, 0)

            def body(g, s):
                statistics(g, s)
                if exists(g + 2):
                    add_x1(g + 2, s)
                if exists(g + 1):
                    node_moments(g + 1, 1 - s)
            over_groups_ahead(dve, body)


_WEIGHTS = ["L0_gnn_WQ", "L0_gnn_WK", "L0_gnn_WV", "L0_gnn_WE", "L1_gnn_W", "L1_gnn_W1", "L1_gnn_W2"]
_VECTORS = ["L0_gnn_bn_gamma", "L0_gnn_bn_beta", "L1_gnn_att_src", "L1_gnn_att_dst", "L1_gnn_bias_gat", "L1_gnn_b1",
            "L1_gnn_g1", "L1_gnn_be1", "L1_gnn_b2", "L1_gnn_g2", "L1_gnn_be2"]


def kernel(**inputs):
    import numpy as np
    import concourse.bacc as bacc
    from concourse.bass_utils import run_bass_kernel_spmd

    src = np.asarray(inputs["src"])
    dst = np.pad(np.asarray(inputs["dst"]), (0, NC * CE - E), constant_values=-1)
    arrays = {
        "x": np.pad(np.asarray(inputs["x"]), ((0, NP - N), (0, 0))),
        "src": np.pad(src, (0, NC * CE - E)),
        "dst_rows": dst.reshape(NC, CE),
        "dst_cols": np.ascontiguousarray(dst.reshape(NC, P, K).transpose(1, 0, 2)),
        "edges": np.ascontiguousarray(inputs["edge_attr_128"]),
        "weights": np.ascontiguousarray(np.stack([np.asarray(inputs[n]) for n in _WEIGHTS], axis=1)),
        "vectors": np.ascontiguousarray(np.stack([np.asarray(inputs[n]) for n in _VECTORS], axis=1)),
    }
    nc = bacc.Bacc("TRN2", target_bir_lowering=False, num_devices=1)
    args = [nc.dram_tensor(f"in_{n}", a.shape, mybir.dt.from_np(a.dtype), kind="ExternalInput").ap()
            for n, a in arrays.items()]
    out = nc.dram_tensor("out", (NP, D), F32, kind="ExternalOutput").ap()
    build(nc, *args, out)
    result = run_bass_kernel_spmd(nc, [{f"in_{n}": a for n, a in arrays.items()}], core_ids=[0])
    return result.results[0]["out"][:N]
```
